# Optimizing a Trainium2 kernel written in Bass

```python
import numpy as np
import jax
import jax.numpy as jnp

def _softmax(x, axis=-1):
    return jax.nn.softmax(x, axis=axis)

def _gelu(x):
    return jax.nn.gelu(x, approximate=True)

def _silu(x):
    return jax.nn.silu(x)

def _sigmoid(x):
    return jax.nn.sigmoid(x)

def _layernorm(x, axis=-1, eps=1e-05):
    m = jnp.mean(x, axis=axis, keepdims=True)
    v = jnp.var(x, axis=axis, keepdims=True)
    return (x - m) / jnp.sqrt(v + eps)

def _scatter_add(tgt, idx, src, axis=0):
    return tgt.at[idx].add(src)

def _segment_sum(src, seg, n):
    return jax.ops.segment_sum(src, seg, n)
kernel_name = 'mk_gnn_resnorm_d4_gnn_r8_10d1a4'

def setup_inputs(seed: int=0):
    np.random.seed(seed)
    _w = jnp.asarray

    def _rec_inputs():
        import jax
        import jax.numpy as jnp
        _gk = jax.random.key(seed)
        x = -8.776e-05 + 1 * jax.random.normal(jax.random.fold_in(_gk, 1), (1250, 512), jnp.float32)
        _s = jax.random.randint(jax.random.fold_in(_gk, 2), (10000,), 0, 1250, jnp.int32)
        _d = jax.random.randint(jax.random.fold_in(_gk, 3), (10000,), 0, 1250, jnp.int32)
        _loop = jnp.arange(1250, dtype=jnp.int32)
        src = jnp.concatenate([_s, _d, _loop])
        dst = jnp.concatenate([_d, _s, _loop])
        _o = jnp.argsort(dst, stable=True)
        src = src[_o]
        dst = dst[_o]
        edge_attr_512 = 2.93046e-05 + 1.00006 * jax.random.normal(jax.random.fold_in(_gk, 12), (21250, 512), jnp.float32)
        return (x, src, dst, edge_attr_512)
    x, src, dst, edge_attr_512 = _rec_inputs()

    def _L0_gnn_setup():
        import jax, jax.numpy as jnp
        import numpy as np
        N_NODES = 1250
        N_EDGES = 20000
        D = 512
        key = jax.random.key(seed)
        k_h, k_e, k_w1, k_w2 = jax.random.split(key, 4)
        h = jax.random.normal(k_h, (N_NODES, D), dtype=jnp.float32)
        edge_index = jax.random.randint(k_e, (2, N_EDGES), 0, N_NODES, dtype=jnp.int64)
        scale = 1.0 / np.sqrt(D)
        W1 = jax.random.normal(k_w1, (D, D), dtype=jnp.float32) * scale
        b1 = jnp.zeros((D,), dtype=jnp.float32)
        W2 = jax.random.normal(k_w2, (D, D), dtype=jnp.float32) * scale
        b2 = jnp.zeros((D,), dtype=jnp.float32)
        return {'h': h, 'edge_index': edge_index, 'W1': W1, 'b1': b1, 'W2': W2, 'b2': b2}
    _L0_gnn_all = _L0_gnn_setup()
    _L0_gnn_in = {k: v for k, v in _L0_gnn_all.items() if k in ('W1', 'b1', 'W2', 'b2')}
    del _L0_gnn_all

    def _L1_gnn_setup():
        import jax, jax.numpy as jnp
        import numpy as np
        N = 6250
        E = 50000
        D_IN = 512
        D_HID = 256
        D_OUT = 512
        key = jax.random.key(seed)
        k1, k2, k3, k4 = jax.random.split(key, 4)
        x = jax.random.normal(k1, (N, D_IN), dtype=jnp.float32)
        edge_index = jax.random.randint(k2, (2, E), 0, N, dtype=jnp.int64)
        W1 = jax.random.normal(k3, (D_IN, D_HID), dtype=jnp.float32) * (1.0 / np.sqrt(D_IN))
        b1 = jnp.zeros((D_HID,), dtype=jnp.float32)
        W2 = jax.random.normal(k4, (D_HID, D_OUT), dtype=jnp.float32) * (1.0 / np.sqrt(D_HID))
        b2 = jnp.zeros((D_OUT,), dtype=jnp.float32)
        return {'x': x, 'edge_index': edge_index, 'W1': W1, 'b1': b1, 'W2': W2, 'b2': b2}
    _L1_gnn_all = _L1_gnn_setup()
    _L1_gnn_in = {k: v for k, v in _L1_gnn_all.items() if k in ('W1', 'b1', 'W2', 'b2')}
    del _L1_gnn_all

    def _L2_gnn_setup():
        import jax, jax.numpy as jnp
        import numpy as np
        N_NODES = 6250
        N_EDGES = 100000
        D = 512
        key = jax.random.key(seed)
        k1, k2, k3, k4 = jax.random.split(key, 4)
        x = jax.random.normal(k1, (N_NODES, D), dtype=jnp.float32)
        W = jax.random.normal(k2, (D, D), dtype=jnp.float32) * (1.0 / np.sqrt(D))
        b = jnp.zeros((D,), dtype=jnp.float32)
        src = jax.random.randint(k3, (N_EDGES,), 0, N_NODES, dtype=jnp.int32)
        dst = jax.random.randint(k4, (N_EDGES,), 0, N_NODES, dtype=jnp.int32)
        return {'x': x, 'W': W, 'b': b, 'src': src, 'dst': dst}
    _L2_gnn_all = _L2_gnn_setup()
    _L2_gnn_in = {k: v for k, v in _L2_gnn_all.items() if k in ('W', 'b')}
    del _L2_gnn_all

    def _L3_gnn_setup():
        import jax, jax.numpy as jnp
        import numpy as np
        N, E, D = (1250, 20000, 512)
        BN_EPS = 1e-05
        key = jax.random.key(seed)
        k = jax.random.split(key, 6)
        x = jax.random.normal(k[0], (N, D), dtype=jnp.float32)
        edge_index = jax.random.randint(k[1], (2, E), 0, N, dtype=jnp.int32)
        edge_attr = jax.random.normal(k[2], (E, D), dtype=jnp.float32)
        W1 = jax.random.normal(k[3], (D, D), dtype=jnp.float32) * 0.02
        b1 = jnp.zeros((D,), dtype=jnp.float32)
        W2 = jax.random.normal(k[4], (D, D), dtype=jnp.float32) * 0.02
        b2 = jnp.zeros((D,), dtype=jnp.float32)
        gamma = jnp.ones((D,), dtype=jnp.float32)
        beta = jnp.zeros((D,), dtype=jnp.float32)
        return {'x': x, 'edge_index': edge_index, 'edge_attr': edge_attr, 'W1': W1, 'b1': b1, 'W2': W2, 'b2': b2, 'gamma': gamma, 'beta': beta}
    _L3_gnn_all = _L3_gnn_setup()
    _L3_gnn_in = {k: v for k, v in _L3_gnn_all.items() if k in ('W1', 'b1', 'W2', 'b2', 'gamma', 'beta')}
    del _L3_gnn_all
    return {'x': x, 'src': src, 'dst': dst, 'edge_attr_512': edge_attr_512, 'L0_gnn_W1': _L0_gnn_in['W1'], 'L0_gnn_b1': _L0_gnn_in['b1'], 'L0_gnn_W2': _L0_gnn_in['W2'], 'L0_gnn_b2': _L0_gnn_in['b2'], 'L1_gnn_W1': _L1_gnn_in['W1'], 'L1_gnn_b1': _L1_gnn_in['b1'], 'L1_gnn_W2': _L1_gnn_in['W2'], 'L1_gnn_b2': _L1_gnn_in['b2'], 'L2_gnn_W': _L2_gnn_in['W'], 'L2_gnn_b': _L2_gnn_in['b'], 'L3_gnn_W1': _L3_gnn_in['W1'], 'L3_gnn_b1': _L3_gnn_in['b1'], 'L3_gnn_W2': _L3_gnn_in['W2'], 'L3_gnn_b2': _L3_gnn_in['b2'], 'L3_gnn_gamma': _L3_gnn_in['gamma'], 'L3_gnn_beta': _L3_gnn_in['beta']}

def reference(x, src, dst, edge_attr_512, L0_gnn_W1, L0_gnn_b1, L0_gnn_W2, L0_gnn_b2, L1_gnn_W1, L1_gnn_b1, L1_gnn_W2, L1_gnn_b2, L2_gnn_W, L2_gnn_b, L3_gnn_W1, L3_gnn_b1, L3_gnn_W2, L3_gnn_b2, L3_gnn_gamma, L3_gnn_beta):
    import jax
    import jax.numpy as jnp

    def _L0_gnn_ref(h, edge_index, W1, b1, W2, b2):
        import jax, jax.numpy as jnp
        import numpy as np
        N_NODES = 1250
        N_EDGES = 20000
        D = 512
        send, rec = (edge_index[0], edge_index[1])
        agg = jax.ops.segment_sum(h[send], rec, num_segments=h.shape[0])
        x = h + agg
        x = jax.nn.relu(x @ W1 + b1)
        x = x @ W2 + b2
        return x

    def _L1_gnn_ref(x, edge_index, W1, b1, W2, b2):
        import jax, jax.numpy as jnp
        import numpy as np
        N = 6250
        E = 50000
        D_IN = 512
        D_HID = 256
        D_OUT = 512
        h = jax.nn.relu(x @ W1 + b1) @ W2 + b2
        row, col = (edge_index[0], edge_index[1])
        agg = jax.ops.segment_sum(h[col], row, num_segments=h.shape[0])
        return h + agg

    def _L2_gnn_ref(x, W, b, src, dst):
        import jax, jax.numpy as jnp
        import numpy as np
        N_NODES = 6250
        N_EDGES = 100000
        D = 512
        N = x.shape[0]
        ones = jnp.ones(src.shape[0], dtype=x.dtype)
        deg_out = jnp.clip(jax.ops.segment_sum(ones, src, num_segments=N), 1.0)
        deg_in = jnp.clip(jax.ops.segment_sum(ones, dst, num_segments=N), 1.0)
        h = x * (deg_out ** (-0.5))[:, None]
        agg = jax.ops.segment_sum(h[src], dst, num_segments=N)
        agg = agg * (deg_in ** (-0.5))[:, None]
        return agg @ W + b

    def _L3_gnn_ref(x, edge_index, edge_attr, W1, b1, W2, b2, gamma, beta):
        import jax, jax.numpy as jnp
        import numpy as np
        N, E, D = (1250, 20000, 512)
        BN_EPS = 1e-05
        src, dst = (edge_index[0], edge_index[1])
        msg = jax.nn.relu(x[src] + edge_attr)
        agg = jax.ops.segment_sum(msg, dst, num_segments=x.shape[0])
        h = x + agg
        h = jax.nn.relu(h @ W1 + b1) @ W2 + b2
        h = x + h
        mean = h.mean(axis=0)
        var = h.var(axis=0)
        h = (h - mean) * jax.lax.rsqrt(var + BN_EPS) * gamma + beta
        return h
    edge_index = jnp.stack([src, dst])
    x = _layernorm(x + _L0_gnn_ref(x, edge_index, L0_gnn_W1, L0_gnn_b1, L0_gnn_W2, L0_gnn_b2), axis=-1)
    x = _layernorm(x + _L1_gnn_ref(x, edge_index, L1_gnn_W1, L1_gnn_b1, L1_gnn_W2, L1_gnn_b2), axis=-1)
    x = _layernorm(x + _L2_gnn_ref(x, L2_gnn_W, L2_gnn_b, src, dst), axis=-1)
    x = _layernorm(x + _L3_gnn_ref(x, edge_index, edge_attr_512, L3_gnn_W1, L3_gnn_b1, L3_gnn_W2, L3_gnn_b2, L3_gnn_gamma, L3_gnn_beta), axis=-1)
    return x

_drawn_inputs = setup_inputs


def setup_inputs(seed=0):
    import zlib

    import numpy as np

    out = dict(_drawn_inputs(seed))
    spreads = {'L0_gnn_b1': (0.0, 0.396),
     'L0_gnn_b2': (0.0, 0.1),
     'L1_gnn_b1': (0.0, 0.1),
     'L1_gnn_b2': (0.0, 0.1),
     'L2_gnn_b': (0.0, 0.1),
     'L3_gnn_b1': (0.0, 0.637),
     'L3_gnn_b2': (0.0, 0.8),
     'L3_gnn_gamma': (1.0, 0.2),
     'L3_gnn_beta': (0.0, 0.1)}
    factors = {}
    for name, (base, spread) in spreads.items():
        noise = np.random.default_rng([zlib.crc32(name.encode()), seed]).standard_normal(out[name].shape)
        drawn = base * np.exp(spread * noise) if base else spread * noise
        out[name] = jnp.asarray(drawn.astype(out[name].dtype))
    for name, factor in factors.items():
        out[name] = (out[name] * factor).astype(out[name].dtype)
    return out
```

```python
from contextlib import ExitStack

import concourse.bass as bass
from concourse import mybir

F32 = mybir.dt.float32
F32R = mybir.dt.float32r
BF16 = mybir.dt.bfloat16
F16 = mybir.dt.float16
I32 = mybir.dt.int32
ALU = mybir.AluOpType
ACT = mybir.ActivationFunctionType
AX = mybir.AxisListType

P = 128
N = 1250
D = 512
DH = 256
E = 21250
KC = D // P
NT = (N + P - 1) // P
TAIL = N - (NT - 1) * P
TPG = 4
GE = P * TPG
NG = (E + GE - 1) // GE
LAST = E - (NG - 1) * GE
LAST_P, LAST_R = divmod(LAST, TPG)
W = 48
NCODE = NT * W
CH = 418
CS = CH - 2
NCH = 3
CUTS = [(0, CH), (CH, 2 * CS + 2), (2 * CS + 2, N)]
BLOCK_SPAN = 7
RING = 6
XRING = 3
ITERS = NG // RING
PRE_LEAD = 4
TLAG = 3
EPS = 1e-5
assert CS * (NCH - 1) + CH == N and NCODE <= 512 and NG % RING == 0 and RING % XRING == 0
assert BLOCK_SPAN * GE + 1 <= 4096 and LAST_P < P


def pre_after(s):
    return range(PRE_LEAD + 2 * s, min(PRE_LEAD + 2 * s + 2, KC * NCH))


def rows(j):
    return P if j < NT - 1 else TAIL


def gnn_kernel(nc, x, src, dst, edge_attr, w01, b01, w02, b02, w11, b11, w12, b12, w2, b2,
               w31, b31, w32, b32, gamma, beta, out, x3_dram):
    with ExitStack() as ctx:
        cursor = [(nc.sbuf_base + 31) // 32 * 32]

        def place(nbytes):
            at = cursor[0]
            cursor[0] += (nbytes + 31) // 32 * 32
            return at

        def at(name, shape, dtype, offset):
            return nc.alloc_sbuf_tensor_at(name, shape, dtype, offset=offset)

        def sb(name, shape, dtype):
            size = 2 if dtype in (BF16, F16) else 4
            n = 1
            for s in shape[1:]:
                n *= s
            return at(name, shape, dtype, place(n * size))

        def sem(name):
            return ctx.enter_context(nc.semaphore(name))

        xn = sb("xn", [P, NT, D], F32)
        r_z, r_h = place(NT * D * 4), place(NT * D * 4)
        r_c, r_a = place(NT * N * 4 + 16), place(NT * N * 4 + 16)
        r_w = place(2 * KC * D * 4)
        w11_at = cursor[0]
        w11_s = sb("w11_s", [P, KC, DH], F32)
        w12_s = sb("w12_s", [P, DH // P, D], F32)
        w2_s = sb("w2_s", [P, KC, D], F32)
        w01_s, w02_s = (at(n, [P, KC, D], F32, r_w + i * KC * D * 4) for i, n in enumerate(("w01_s", "w02_s")))
        w31_s, w32_s = (at(n, [P, KC, D], F32, r_w + i * KC * D * 4) for i, n in enumerate(("w31_s", "w32_s")))

        counts = at("counts", [P, NT, N], F32R, r_c)
        countsT = at("countsT", [P, NT, N], F32R, r_a)
        counts_x = at("counts_x", [P, NT, N], F32, r_c)
        countsT_x = at("countsT_x", [P, NT, N], F32, r_a)

        def f32(ap):
            return ap if ap.dtype == F32 else ap.bitcast(F32)

        xT0 = at("xT0", [P, KC, N], F32, r_z)
        u_hi = at("u_hi", [P, NT, D], F32R, r_h)
        a = r_a
        hot_code = at("hot_code", [P, 2, TPG, NCODE], BF16, a); a += 2 * TPG * NCODE * 2
        hot_lo = at("hot_lo", [P, 2, TPG, P], BF16, a); a += 2 * TPG * P * 2
        codeT = at("codeT", [P, NG, TPG], F32, a); a += NG * TPG * 4
        src_loT = at("src_loT", [P, NG, TPG], F32, a); a += NG * TPG * 4
        dstT = at("dstT", [P, NG, TPG], F32, a); a += NG * TPG * 4
        u_f = at("u_f", [P, 2, D], F32, a); a += 2 * D * 4
        u_lo = at("u_lo", [P, NT, D], F32R, a)
        row_at = a
        h1T0 = at("h1T0", [P, KC, N], F32, r_z)
        row = {}
        for n in ("dst_i", "src_i", "lo_i", "hi_i"):
            row[n] = at("row_" + n, [NG, GE], I32, row_at); row_at += GE * 4
        for n in ("dst", "src", "lo", "hi", "rel", "valid", "code", "relw", "left", "t"):
            row[n] = at("row_" + n, [NG, GE], F32, row_at); row_at += GE * 4
        base_row = at("base_row", [NG, P], F32, row_at); row_at += P * 4
        left_row = at("left_row", [NG, P], F32, row_at); row_at += P * 4
        left_max = at("left_max", [NG, 1], F32, row_at); row_at += 32
        assert row_at <= r_a + NT * N * 4
        fixc_dst = at("fixc_dst", [P, N], BF16, r_a)
        fixc_src = at("fixc_src", [P, P], BF16, r_a + 2 * TPG * NCODE * 2)
        x1T = at("x1T", [P, KC, N], F32, r_h)
        g_f = at("g_f", [P, 4, DH], F32, r_w)
        g_hi = at("g_hi", [P, NT, DH], F32R, r_z)
        g_lo = at("g_lo", [P, NT, DH], F32R, r_z + NT * DH * 4)
        z1T = at("z1T", [P, DH // P, N], F32, r_h)
        xs_hi = at("xs_hi", [P, NT, D], F32R, r_z)
        xs_lo = at("xs_lo", [P, NT, D], F32R, r_a)
        xs_f = at("xs_f", [P, 2, D], F32, r_a + NT * D * 4)
        z2T = at("z2T", [P, KC, N], F32, r_h)
        x3T = at("x3T", [P, KC, N], F32, r_z)
        hT = at("hT", [P, KC, N], F32, r_h)
        ea = at("ea", [P, RING, TPG, D], F32, r_a)
        c = r_c
        xg = at("xg", [P, XRING, TPG, D], F32, c); c += XRING * TPG * D * 4
        preT = at("preT", [P, KC, N], F32, c); c += KC * N * 4
        zg = at("zg", [P, 3, KC, 2, W], F32, c); c += 3 * KC * 2 * W * 4
        assert c <= r_c + NT * N * 4
        fix_hot = at("fix_hot", [P, N], F32, r_c + 2 * TPG * D * 4)

        ident = sb("ident", [P, P], F32)
        b02_b = sb("b02_b", [P, D], F32)
        b11_b = sb("b11_b", [P, DH], F32)
        b12_b = sb("b12_b", [P, D], F32)
        b2_b = sb("b2_b", [P, D], F32)
        cols = sb("cols", [P, 5, KC], F32)
        relwT = sb("relwT", [P, NG, TPG], F32)
        leftT = sb("leftT", [P, NG, TPG], F32)
        srcT = sb("srcT", [P, NG, TPG], F32)
        srcT_i = sb("srcT_i", [P, NG, TPG], I32)
        idx4 = sb("idx4", [P, XRING, TPG], I32)
        iota_n = sb("iota_n", [P, N], F16)
        hot_w = at("hot_w", [P, RING, TPG, W], F32, w11_at)
        base_f = sb("base_f", [1, NG], F32)
        base_i = sb("base_i", [1, NG], I32)
        gap = sb("gap", [1, NG], F32)
        flag4 = sb("flag4", [1, 4], F32)
        flag_i = sb("flag_i", [1, 1], I32)
        eps_s = sb("eps_s", [P, 1], F32)
        stats = sb("stats", [P, 2, 6], F32)
        mv = sb("mv", [P, 2, 2], F32)
        std = sb("std", [P, 2], F32)
        rstd = sb("rstd", [P, 2], F32)
        deg = sb("deg", [P, 4, NT], F32)
        degt = sb("degt", [P, 4, NT], F32)
        bn_st = sb("bn_st", [P, KC, NCH, 6], F32)
        bn_mv = sb("bn_mv", [P, KC, 2], F32)
        bn_t = sb("bn_t", [P, 4, KC], F32)
        assert cursor[0] <= nc.sbuf_usable_end, cursor[0] - nc.sbuf_usable_end

        ps = ctx.enter_context(nc.psum_tensor("ps", [P, 8, 512], F32))

        rows_loaded = sem("rows_loaded")
        x_loaded = [sem(f"x_loaded{i}") for i in range(4)]
        w01_loaded, w02_loaded = sem("w01_loaded"), sem("w02_loaded")
        w1_loaded, w2_loaded, w3_loaded = sem("w1_loaded"), sem("w2_loaded"), sem("w3_loaded")
        bias_loaded = sem("bias_loaded")
        cols_loaded = sem("cols_loaded")
        consts = sem("consts")
        counts_zero = sem("counts_zero")
        row_pad = sem("row_pad")
        prep = sem("prep")
        rows_ready = sem("rows_ready")
        idx_done = sem("idx_done")
        idx_ready = sem("idx_ready")
        xT_done, xT_evac = sem("xT_done"), sem("xT_evac")
        u_done, u_evac, u_ready = sem("u_done"), sem("u_evac"), sem("u_ready")
        hot_ready, cnt_done, cnt_added = sem("hot_ready"), sem("cnt_done"), sem("cnt_added")
        fixc_hot, fixc_done, fixc_added = sem("fixc_hot"), sem("fixc_done"), sem("fixc_added")
        diag_added, diag_taken = sem("diag_added"), sem("diag_taken")
        agg_done = [sem(f"agg_done{i}") for i in range(3)]
        agg_evac = [sem(f"agg_evac{i}") for i in range(3)]
        y_done, y_read = sem("y_done"), sem("y_read")
        xb_ready = [sem(f"xb_ready{i}") for i in range(3)]
        ln_step, std_ready, rstd_ready, x_ready = sem("ln_step"), sem("std_ready"), sem("rstd_ready"), sem("x_ready")
        t_done, t_evac = sem("t_done"), sem("t_evac")
        g_done, g_read, g_relu, g_ready = sem("g_done"), sem("g_read"), sem("g_relu"), sem("g_ready")
        deg_set, deg_step, deg_sq, deg_ready = sem("deg_set"), sem("deg_step"), sem("deg_sq"), sem("deg_ready")
        xs_done, xs_ready = sem("xs_done"), sem("xs_ready")
        x3_stored = sem("x3_stored")
        x3_copied = sem("x3_copied")
        pre_done, pre_evac = sem("pre_done"), sem("pre_evac")
        ea_loaded = [sem(f"ea_loaded{i}") for i in range(RING)]
        xg_loaded = [sem(f"xg_loaded{i}") for i in range(XRING)]
        idx_staged, idx_seen = sem("idx_staged"), sem("idx_seen")
        add_done, relu_done, win_ready = sem("add_done"), sem("relu_done"), sem("win_ready")
        scat_done, zg_ready, pair_done, pre_added = sem("scat_done"), sem("zg_ready"), sem("pair_done"), sem("pre_added")
        fix_x, fix_e, fix_msg, fix_done, fix_added = (sem("fix_x"), sem("fix_e"), sem("fix_msg"), sem("fix_done"), sem("fix_added"))
        fix_idx = sem("fix_idx")
        h1_ready = sem("h1_ready")
        w32_done, h2_ready, bn_step, bn_sq, bn_ready, hn_ready = (
            sem("w32_done"), sem("h2_ready"), sem("bn_step"), sem("bn_sq"), sem("bn_ready"), sem("hn_ready"))
        bn_calc = sem("bn_calc")
        out_stored = sem("out_stored")

        def node_rows(t):
            return t[0:(NT - 1) * P, :].rearrange("(j p) d -> p j d", p=P)

        def w_view(t):
            return t.rearrange("(k p) n -> p k n", p=P)

        def feature_cols(t):
            return t.rearrange("(c p) -> p c", p=P)

        def ea_rows(g):
            return edge_attr[bass.ds(g * GE, GE), :].rearrange("(p r) d -> p (r d)", p=P)

        block = ctx.enter_context(nc.Block())

        @block.sync
        def _(sp):
            sp.wait_ge(row_pad, 2)
            for n, t in (("dst_i", dst), ("src_i", src)):
                sp.dma_start(row[n][0:NG - 1, :], t[0:(NG - 1) * GE].rearrange("(g e) -> g e", e=GE)).then_inc(rows_loaded, 16)
                sp.dma_start(row[n][NG - 1:NG, 0:LAST],
                             t[(NG - 1) * GE:E].rearrange("(a e) -> a e", a=1)).then_inc(rows_loaded, 16)
            for i in range(3):
                sp.dma_start(xn[:, 3 * i:3 * i + 3, :], node_rows(x)[:, 3 * i:3 * i + 3, :]).then_inc(x_loaded[i], 16)
            sp.dma_start(xn[0:TAIL, NT - 1, :], x[(NT - 1) * P:N, :]).then_inc(x_loaded[3], 16)
            sp.dma_start(w01_s[:, :, :], w_view(w01)).then_inc(w01_loaded, 16)
            sp.dma_start(cols[:, 0, :], feature_cols(b01), allow_slow_non_contiguous=True).then_inc(cols_loaded, 16)
            sp.dma_start(w02_s[:, :, :], w_view(w02)).then_inc(w02_loaded, 16)
            for t, b in ((b02_b, b02), (b11_b, b11), (b12_b, b12), (b2_b, b2)):
                sp.dma_start(t[:, :], b.partition_broadcast(P)).then_inc(bias_loaded, 16)
            sp.dma_start(w11_s[:, :, :], w_view(w11)).then_inc(w1_loaded, 16)
            sp.dma_start(w12_s[:, :, :], w_view(w12)).then_inc(w1_loaded, 16)
            sp.dma_start(w2_s[:, :, :], w_view(w2)).then_inc(w2_loaded, 16)
            for i, b in enumerate((b31, b32, gamma, beta)):
                sp.dma_start(cols[:, 1 + i, :], feature_cols(b), allow_slow_non_contiguous=True).then_inc(cols_loaded, 16)
            sp.wait_ge(g_ready, NT)
            sp.dma_start(w31_s[:, :, :], w_view(w31)).then_inc(w3_loaded, 16)
            sp.dma_start(w32_s[:, :, :], w_view(w32)).then_inc(w3_loaded, 16)

            sp.wait_ge(agg_done[2], NCH * KC)
            for s in range(RING):
                sp.dma_start(ea[:, s, :, :].rearrange("p r d -> p (r d)"), ea_rows(s)).then_inc(ea_loaded[s], 16)
            for j in range(NT):
                sp.wait_ge(x_ready, 2 * NT + j + 1)
                sp.dma_start(x3_dram[j * P:j * P + rows(j), :], xn[0:rows(j), j, :]).then_inc(x3_stored, 16)

            def reload(it, s):
                sp.wait_ge(scat_done, RING * (it - 1) + s + 1)
                g = RING * it + s
                if isinstance(it, int) and g == NG - 1:
                    e0 = g * GE
                    sp.dma_start(ea[0:LAST_P, s, :, :].rearrange("p r d -> p (r d)"),
                                 edge_attr[e0:e0 + LAST_P * TPG, :].rearrange("(p r) d -> p (r d)", r=TPG)).then_inc(ea_loaded[s], 16)
                    if LAST_R:
                        sp.dma_start(ea[LAST_P:LAST_P + 1, s, 0:LAST_R, :].rearrange("p r d -> p (r d)"),
                                     edge_attr[e0 + LAST_P * TPG:E, :].rearrange("(p r) d -> p (r d)", p=1)).then_inc(ea_loaded[s], 16)
                else:
                    sp.dma_start(ea[:, s, :, :].rearrange("p r d -> p (r d)"), ea_rows(g)).then_inc(ea_loaded[s], 16)

            with sp.Fori(1, ITERS - 1) as it:
                for s in range(RING):
                    reload(it, s)
            for s in range(RING):
                reload(ITERS - 1, s)

            for j in range(NT):
                sp.wait_ge(x_ready, 3 * NT + j + 1)
                sp.dma_start(out[j * P:j * P + rows(j), :], xn[0:rows(j), j, :]).then_inc(out_stored, 16)
            sp.wait_ge(x3_stored, 16 * NT)
            sp.wait_ge(out_stored, 16 * NT)

        @block.gpsimd
        def _(pool):
            pool.memset(ident[:, :], 0.0).then_inc(consts, 1)
            pool.wait_ge(consts, 1)
            pool.affine_select(out=ident[:, :], in_=ident[:, :], compare_op=ALU.not_equal, fill=1.0, base=0,
                               pattern=[[-1, P]], channel_multiplier=1).then_inc(consts, 1)
            pool.iota(iota_n[:, :], [[1, N]], base=0, channel_multiplier=0, allow_small_or_imprecise_dtypes=True).then_inc(consts, 1)
            pool.memset(eps_s[:, :], EPS).then_inc(consts, 1)
            pool.memset(f32(counts[:, :, :]), 0.0).then_inc(counts_zero, 1)
            for j in range(NT):
                pool.wait_ge(u_evac, j + 1)
                pool.tensor_tensor(u_lo[0:rows(j), j, :], u_f[0:rows(j), j % 2, :], u_hi[0:rows(j), j, :].bitcast(F32),
                                   ALU.subtract).then_inc(u_ready, 1)
            pool.wait_ge(bias_loaded, 64)
            for j in range(NT):
                pool.tensor_tensor(xn[0:rows(j), j, :], xn[0:rows(j), j, :], b02_b[0:rows(j), :], ALU.add).then_inc(xb_ready[0], 1)
            for j in range(NT):
                pool.wait_ge(g_relu, j + 1)
                pool.tensor_tensor(g_lo[0:rows(j), j, :], g_f[0:rows(j), j % 4, :], g_hi[0:rows(j), j, :].bitcast(F32),
                                   ALU.subtract).then_inc(g_ready, 1)
            for j in range(NT):
                pool.wait_ge(xs_done, j + 1)
                pool.tensor_tensor(xs_lo[0:rows(j), j, :], xs_f[0:rows(j), j % 2, :], xs_hi[0:rows(j), j, :].bitcast(F32),
                                   ALU.subtract).then_inc(xs_ready, 1)
            for j in range(NT):
                pool.tensor_tensor(xn[0:rows(j), j, :], xn[0:rows(j), j, :], b2_b[0:rows(j), :], ALU.add).then_inc(xb_ready[2], 1)

            pool.wait_ge(x3_stored, 16 * NT)
            pool.wait_ge(agg_done[2], NCH * KC)
            irregular = pool.value_load(flag_i[0:1, 0:1], min_val=0, max_val=1)
            with pool.If(irregular > 0):
                def fix_load(g, r, attrs):
                    n = g * TPG + r
                    pool.tensor_copy(idx4[:, 0, 0:1], srcT_i[:, bass.ds(g, 1), r:r + 1].rearrange("p a b -> p (a b)")).then_inc(fix_idx, 1)
                    pool.wait_ge(fix_idx, n + 1)
                    pool.sem_inc(idx_seen, 1)
                    pool.indirect_dma_start(out=xg[:, 0, 0, :], out_offset=None, in_=x3_dram[:, :],
                                            in_offset=bass.IndirectOffsetOnAxis(ap=idx4[:, 0, 0:1], axis=0)).then_inc(fix_x, 16)
                    pool.dma_start(xg[0:attrs.shape[0], 1, 0, :], attrs).then_inc(fix_e, 16)
                    pool.wait_ge(fix_added, n * KC + KC + 1)
                with pool.Fori(0, NG - 1) as g:
                    for r in range(TPG):
                        fix_load(g, r, edge_attr[bass.ds(g * GE, GE), :].rearrange("(p r) d -> r p d", r=TPG)[r, :, :])
                for r in range(TPG):
                    fix_load(NG - 1, r, edge_attr[(NG - 1) * GE + r:E:TPG, :])

            def gather(it, s):
                g, slot = RING * it + s, s % XRING
                if not (isinstance(g, int) and g < XRING):
                    pool.wait_ge(add_done, g - XRING + 1)
                pool.tensor_copy(idx4[:, slot, :], srcT_i[:, bass.ds(g, 1), :].rearrange("p a b -> p (a b)")).then_inc(idx_staged, 1)
                pool.wait_ge(idx_staged, g + 1)
                pool.sem_inc(idx_seen, 1)
                for r in range(TPG):
                    pool.indirect_dma_start(out=xg[:, slot, r, :], out_offset=None, in_=x3_dram[:, :],
                                            in_offset=bass.IndirectOffsetOnAxis(ap=idx4[:, slot, r:r + 1], axis=0)).then_inc(xg_loaded[slot], 16)

            for s in range(RING):
                gather(0, s)
            with pool.Fori(1, ITERS) as it:
                for s in range(RING):
                    gather(it, s)

        @block.scalar
        def _(act):
            def evac_T(n, j, dst_t):
                act.wait_ge(xT_done, n + 1)
                act.copy(dst_t[:, :, P * j:P * j + rows(j)],
                         ps[:, n % 2, :].rearrange("p (c n) -> p c n", c=KC)[:, :, 0:rows(j)]).then_inc(xT_evac, 1)

            for j in range(NT):
                evac_T(j, j, xT0)
            for j in range(NT):
                act.wait_ge(u_done, j + 1)
                if j >= 2:
                    act.wait_ge(u_ready, j - 1)
                act.copy(u_f[0:rows(j), j % 2, :], ps[0:rows(j), 2 + j % 2, :])
                act.copy(u_hi[0:rows(j), j, :], ps[0:rows(j), 2 + j % 2, :]).then_inc(u_evac, 1)

            def evac_agg(layer, nc_, emit):
                act.sem_inc(agg_evac[layer], nc_)
                with act.Fori(0, NCH) as i:
                    for cc in range(nc_):
                        act.wait_ge(agg_done[layer], i * nc_ + cc + 1)
                        emit(cc, bass.ds(i * CS, CH)).then_inc(agg_evac[layer], 1)

            act.wait_ge(cols_loaded, 80)
            evac_agg(0, KC, lambda cc, n: act.activation(h1T0[:, cc, n], ps[:, cc, 0:CH], ACT.Relu, bias=cols[:, 0, cc:cc + 1]))

            def sqrt_var(n):
                act.wait_ge(ln_step, 2 * n + 2)
                act.activation(std[:, n % 2:n % 2 + 1], mv[:, n % 2, 1:2], ACT.Sqrt, bias=eps_s[:, 0:1]).then_inc(std_ready, 1)

            def norm_and_turn(cT):
                for j in range(NT):
                    for q in range(3):
                        t = 3 * j + q
                        act.wait_ge(t_done, t + 1)
                        n0, n1 = 4 * P * q, min(4 * P * (q + 1), N)
                        act.copy(cT[0:rows(j), j, n0:n1], ps[0:rows(j), t % 4, 0:n1 - n0]).then_inc(t_evac, 1)
                    sqrt_var(j)

            irregular = act.value_load(flag_i[0:1, 0:1], min_val=0, max_val=1)
            with act.If(irregular > 0):
                norm_and_turn(countsT_x)
            with act.Else():
                norm_and_turn(countsT)
            def relu_g(j):
                act.wait_ge(g_read, j + 1)
                act.activation(g_hi[0:rows(j), j, :], g_f[0:rows(j), j % 4, :], ACT.Relu)
                act.activation(g_f[0:rows(j), j % 4, :], g_f[0:rows(j), j % 4, :], ACT.Relu).then_inc(g_relu, 1)

            for j in range(NT):
                evac_T(NT + j, j, x1T)
                if j >= 1:
                    relu_g(j - 1)
            relu_g(NT - 1)
            act.wait_ge(deg_step, 2)
            act.activation(degt[:, 1, :], degt[:, 0, :], ACT.Sqrt).then_inc(deg_sq, 1)
            evac_agg(1, DH // P, lambda cc, n: act.copy(z1T[:, cc, n], ps[:, cc, 0:CH]))
            act.wait_ge(deg_step, 5)
            act.activation(degt[:, 3, :], degt[:, 2, :], ACT.Sqrt).then_inc(deg_sq, 1)
            def scale_x(j):
                act.wait_ge(x_ready, NT + j + 1)
                if j >= 2:
                    act.wait_ge(xs_ready, j - 1)
                if j == 0:
                    act.wait_ge(deg_ready, 1)
                act.activation(xs_f[0:rows(j), j % 2, :], xn[0:rows(j), j, :], ACT.Copy, scale=deg[0:rows(j), 1, j:j + 1])
                act.activation(xs_hi[0:rows(j), j, :], xn[0:rows(j), j, :], ACT.Copy, scale=deg[0:rows(j), 1, j:j + 1]).then_inc(xs_done, 1)

            for j in range(NT):
                sqrt_var(NT + j)
                if j >= 2:
                    scale_x(j - 2)
            scale_x(NT - 2)
            scale_x(NT - 1)
            evac_agg(2, KC, lambda cc, n: act.copy(z2T[:, cc, n], ps[:, cc, 0:CH]))
            for j in range(NT):
                sqrt_var(2 * NT + j)
                if j >= TLAG + 1:
                    evac_T(2 * NT + j - TLAG - 1, j - TLAG - 1, x3T)
            for j in range(NT - TLAG - 1, NT):
                evac_T(2 * NT + j, j, x3T)
            act.wait_ge(y_done, 3 * NT)
            act.wait_ge(xT_evac, 3 * NT)
            act.copy(hT[:, :, :], x3T[:, :, :]).then_inc(x3_copied, 1)

            def evac_pre(n):
                cc, (n0, n1) = n // NCH, CUTS[n % NCH]
                act.wait_ge(pre_done, n + 1)
                act.activation(preT[:, cc, n0:n1], ps[:, n % 4, 0:n1 - n0], ACT.Identity,
                               bias=cols[:, 1, cc:cc + 1]).then_inc(pre_evac, 1)

            def rectify(it, s):
                g = RING * it + s
                act.wait_ge(add_done, g + 1)
                act.activation(ea[:, s, :, :], ea[:, s, :, :], ACT.Relu).then_inc(relu_done, 1)

            def evac_z(it, s):
                g, pair = RING * it + s, s // 2
                act.wait_ge(scat_done, g + 1)
                if not (isinstance(it, int) and it == 0):
                    act.wait_ge(pair_done, (RING // 2) * (it - 1) + pair + 1)
                act.copy(zg[:, pair, :, s % 2, :], ps[:, 4 + s % 2, 0:KC * W].rearrange("p (c w) -> p c w", c=KC)).then_inc(zg_ready, 1)

            for n in range(PRE_LEAD):
                evac_pre(n)
            for s in range(RING):
                rectify(0, s)
                if s:
                    for n in pre_after(s - 1):
                        evac_pre(n)
                    evac_z(0, s - 1)
            with act.Fori(1, ITERS) as it:
                for s in range(RING):
                    rectify(it, s)
                    if s:
                        evac_z(it, s - 1)
                    else:
                        evac_z(it - 1, RING - 1)
            evac_z(ITERS - 1, RING - 1)
            for cc in range(KC):
                act.wait_ge(pre_added, NG)
                act.activation(preT[:, cc, :], preT[:, cc, :], ACT.Relu).then_inc(h1_ready, 1)
            for cc in range(KC):
                act.wait_ge(bn_step, 2 * cc + 2)
                act.activation(bn_t[:, 0, cc:cc + 1], bn_mv[:, cc, 1:2], ACT.Sqrt, bias=eps_s[:, 0:1]).then_inc(bn_sq, 1)
                act.wait_ge(bn_ready, cc + 1)
                act.activation(hT[:, cc, :], hT[:, cc, :], ACT.Identity, bias=bn_t[:, 3, cc:cc + 1],
                               scale=bn_t[:, 2, cc:cc + 1]).then_inc(hn_ready, 1)
            for j in range(NT):
                sqrt_var(3 * NT + j)

        @block.vector
        def _(dve):
            steps = [0]

            def step(ins):
                steps[0] += 1
                ins.then_inc(prep, 1)
                dve.wait_ge(prep, steps[0])

            dve.memset(row["dst_i"][:, :], -1).then_inc(row_pad, 1)
            dve.memset(row["src_i"][:, :], 0).then_inc(row_pad, 1)
            dve.wait_ge(rows_loaded, 64)
            r = {n: t[:, :] for n, t in row.items()}
            dve.tensor_copy(r["dst"], r["dst_i"])
            dve.tensor_copy(r["src"], r["src_i"])
            dve.tensor_scalar(r["lo_i"], r["src_i"], P - 1, None, ALU.bitwise_and)
            step(dve.tensor_scalar(r["hi_i"], r["src_i"], P.bit_length() - 1, None, ALU.logical_shift_right))
            dve.tensor_copy(r["lo"], r["lo_i"])
            dve.tensor_copy(r["hi"], r["hi_i"])
            step(dve.tensor_scalar(base_row[:, :], row["dst"][:, 0:1].to_broadcast([NG, P]), float(N - W), 0.0, ALU.min, ALU.max))
            step(dve.tensor_scalar(r["rel"], r["dst"], base_row[:, 0:1], None, ALU.subtract))
            step(dve.tensor_scalar(r["t"], r["rel"], float(W), None, ALU.is_lt))
            step(dve.scalar_tensor_tensor(out=r["valid"], in0=r["rel"], scalar=0.0, in1=r["t"], op0=ALU.is_ge, op1=ALU.mult))
            step(dve.scalar_tensor_tensor(out=r["code"], in0=r["hi"], scalar=float(W), in1=r["rel"], op0=ALU.mult, op1=ALU.add))
            step(dve.scalar_tensor_tensor(out=r["code"], in0=r["code"], scalar=1.0, in1=r["valid"], op0=ALU.add, op1=ALU.mult))
            dve.tensor_scalar(r["code"], r["code"], -1.0, None, ALU.add)
            step(dve.scalar_tensor_tensor(out=r["relw"], in0=r["rel"], scalar=1.0, in1=r["valid"], op0=ALU.add, op1=ALU.mult))
            dve.tensor_scalar(r["relw"], r["relw"], -1.0, None, ALU.add)
            step(dve.tensor_scalar(r["t"], r["valid"], -1.0, 1.0, ALU.mult, ALU.add))
            step(dve.scalar_tensor_tensor(out=r["left"], in0=r["dst"], scalar=1.0, in1=r["t"], op0=ALU.add, op1=ALU.mult))
            step(dve.tensor_scalar(r["left"], r["left"], -1.0, None, ALU.add))
            step(dve.tensor_reduce(left_max[:, :], r["left"], AX.X, ALU.max))
            dve.tensor_copy(left_row[:, :], left_max[:, :].to_broadcast([NG, P])).then_inc(rows_ready, 1)

            dve.wait_ge(idx_done, 1)
            def turned(bank, k):
                return ps[:, bank, k * NG * TPG:(k + 1) * NG * TPG].rearrange("p (r g) -> p g r", r=TPG)
            dve.tensor_copy(codeT[:, :, :], turned(4, 0))
            dve.tensor_copy(src_loT[:, :, :], turned(4, 1))
            dve.tensor_copy(relwT[:, :, :], turned(4, 2))
            dve.tensor_copy(leftT[:, :, :], turned(5, 0))
            dve.tensor_copy(srcT[:, :, :], turned(5, 1))
            dve.tensor_copy(dstT[:, :, :], turned(3, 0))
            dve.tensor_copy(srcT_i[:, :, :], turned(5, 1))
            off = 2 * NG * TPG
            dve.tensor_copy(base_i[:, :], ps[0:1, 5, off:off + NG])
            step(dve.tensor_copy(base_f[:, :], ps[0:1, 5, off:off + NG]))
            dve.tensor_reduce(flag4[:, 0:1], ps[0:1, 5, off + NG:off + 2 * NG], AX.X, ALU.max)
            step(dve.tensor_tensor(gap[:, 0:NG - 1], base_f[:, 1:NG], base_f[:, 0:NG - 1], ALU.subtract))
            step(dve.tensor_reduce(flag4[:, 1:2], gap[:, 0:NG - 1], AX.X, ALU.min))
            step(dve.tensor_tensor(gap[:, 0:NG - BLOCK_SPAN], base_f[:, BLOCK_SPAN:NG], base_f[:, 0:NG - BLOCK_SPAN], ALU.subtract))
            step(dve.tensor_reduce(flag4[:, 2:3], gap[:, 0:NG - BLOCK_SPAN], AX.X, ALU.min))
            step(dve.tensor_scalar(flag4[:, 0:1], flag4[:, 0:1], 0.0, None, ALU.is_ge))
            step(dve.tensor_scalar(flag4[:, 1:2], flag4[:, 1:2], 0.0, None, ALU.is_lt))
            step(dve.tensor_scalar(flag4[:, 2:3], flag4[:, 2:3], float(W), None, ALU.is_lt))
            step(dve.tensor_reduce(flag4[:, 3:4], flag4[:, 0:3], AX.X, ALU.max))
            dve.tensor_copy(flag_i[:, :], flag4[:, 3:4]).then_inc(idx_ready, 1)

            dve.wait_ge(consts, 4)
            dve.wait_ge(counts_zero, 1)
            dve.wait_ge(idx_ready, 1)

            def one_hots(g, half):
                if not (isinstance(g, int) and g < 2):
                    dve.wait_ge(cnt_done, g - 1)
                for rr in range(TPG):
                    dve.tensor_scalar(hot_code[:, half, rr, :], iota_n[:, 0:NCODE],
                                      codeT[:, bass.ds(g, 1), rr:rr + 1].rearrange("p a b -> p (a b)"), None, ALU.is_equal)
                    ins = dve.tensor_scalar(hot_lo[:, half, rr, :], iota_n[:, 0:P],
                                            src_loT[:, bass.ds(g, 1), rr:rr + 1].rearrange("p a b -> p (a b)"), None, ALU.is_equal)
                ins.then_inc(hot_ready, 1)

            def add_counts(g, half):
                base = dve.value_load(base_i[0:1, bass.ds(g, 1)], min_val=0, max_val=N - W)
                dve.wait_ge(cnt_done, g + 1)
                if not (isinstance(g, int) and g == 0):
                    dve.wait_ge(cnt_added, g)
                win = counts[:, :, bass.ds(base, W)]
                dve.tensor_tensor(win, ps[:, 6 + half, 0:NCODE].rearrange("p (h w) -> p h w", h=NT), f32(win), ALU.add).then_inc(cnt_added, 1)

            one_hots(0, 0)
            one_hots(1, 1)
            add_counts(0, 0)
            with dve.Fori(1, NG // 2) as i:
                one_hots(2 * i, 0)
                add_counts(2 * i - 1, 1)
                one_hots(2 * i + 1, 1)
                add_counts(2 * i, 0)
            add_counts(NG - 1, 1)
            dve.wait_ge(cnt_added, NG)

            def diagonal(c, op, done):
                main = c[:, :, :].rearrange("p j n -> p (j n)")[:, 0:(NT - 1) * (N + P)] \
                    .rearrange("p (j r) -> p j r", r=N + P)[:, :, 0:P]
                tail = c[:, NT - 1, (NT - 1) * P:N]
                dve.tensor_tensor(main, f32(main), ident[:, :].unsqueeze(1).to_broadcast([P, NT - 1, P]), op).then_inc(done, 1)
                dve.tensor_tensor(tail, f32(tail), ident[:, 0:TAIL], op).then_inc(done, 1)

            def out_degrees(c):
                diagonal(c, ALU.add, diag_added)
                dve.wait_ge(diag_added, 2)
                dve.tensor_reduce(deg[:, 0, :], f32(c[:, :, :]), AX.X, ALU.add).then_inc(deg_step, 1)

            def in_degrees(c, cT):
                dve.tensor_reduce(deg[:, 2, 0:NT - 1], f32(cT[:, 0:NT - 1, :]), AX.X, ALU.add).then_inc(deg_step, 1)
                dve.tensor_reduce(deg[0:TAIL, 2, NT - 1:NT], f32(cT[0:TAIL, NT - 1, :]), AX.X, ALU.add).then_inc(deg_step, 1)
                diagonal(c, ALU.subtract, diag_taken)

            dve.memset(deg[:, :, :], 1.0)
            dve.memset(degt[:, :, :], 1.0).then_inc(deg_set, 1)
            dve.wait_ge(deg_set, 1)
            irregular = dve.value_load(flag_i[0:1, 0:1], min_val=0, max_val=1)
            with dve.If(irregular > 0):
                dve.memset(counts_x[:, :, :], 0.0).then_inc(counts_zero, 1)
                dve.wait_ge(counts_zero, 2)
                with dve.Fori(0, NG) as g:
                    for rr in range(TPG):
                        dve.tensor_scalar(fixc_dst[:, :], iota_n[:, :],
                                          dstT[:, bass.ds(g, 1), rr:rr + 1].rearrange("p a b -> p (a b)"), None, ALU.is_equal)
                        for h in range(NT):
                            n = (g * TPG + rr) * NT + h
                            dve.tensor_scalar(fixc_src[:, 0:rows(h)], iota_n[:, P * h:P * h + rows(h)],
                                              srcT[:, bass.ds(g, 1), rr:rr + 1].rearrange("p a b -> p (a b)"), None,
                                              ALU.is_equal).then_inc(fixc_hot, 1)
                            dve.wait_ge(fixc_done, n + 1)
                            for q, (n0, n1) in enumerate(CUTS):
                                ins = dve.tensor_tensor(counts_x[0:rows(h), h, n0:n1], ps[0:rows(h), 4 + q, 0:n1 - n0],
                                                        counts_x[0:rows(h), h, n0:n1], ALU.add)
                            ins.then_inc(fixc_added, 1)
                            dve.wait_ge(fixc_added, n + 2)
                out_degrees(counts_x)
            with dve.Else():
                out_degrees(counts)
            dve.wait_ge(deg_step, 1)
            dve.tensor_scalar(degt[:, 0, :], deg[:, 0, :], -1.0, 1.0, ALU.add, ALU.max).then_inc(deg_step, 1)

            def ln_begin(n, j, y_sum):
                dve.wait_ge(y_done, n + 1)
                y_sum(xn[0:rows(j), j, :], ps[0:rows(j), 4 + n % 2, :]).then_inc(y_read, 1)
                dve.wait_ge(y_read, n + 1)
                dve.bn_stats(stats[0:rows(j), n % 2, :], xn[0:rows(j), j, :]).then_inc(ln_step, 1)
                dve.wait_ge(ln_step, 2 * n + 1)
                dve.bn_aggr(mv[0:P if j < NT - 1 else TAIL, n % 2, :], stats[0:rows(j), n % 2, :]).then_inc(ln_step, 1)

            def ln_finish(n, j):
                dve.wait_ge(std_ready, n + 1)
                dve.reciprocal(rstd[0:rows(j), n % 2:n % 2 + 1], std[0:rows(j), n % 2:n % 2 + 1]).then_inc(rstd_ready, 1)
                dve.wait_ge(rstd_ready, n + 1)
                dve.tensor_scalar(xn[0:rows(j), j, :], xn[0:rows(j), j, :], mv[0:rows(j), n % 2, 0:1], rstd[0:rows(j), n % 2:n % 2 + 1],
                                  ALU.subtract, ALU.mult).then_inc(x_ready, 1)

            def layer_norm(layer, before, y_sum):
                for j in range(NT):
                    before(j)
                    ln_begin(NT * layer + j, j, y_sum(j))
                    if j:
                        ln_finish(NT * layer + j - 1, j - 1)
                ln_finish(NT * layer + NT - 1, NT - 1)

            def plus_x(j):
                return lambda xr, y: dve.tensor_tensor(xr, y, xr, ALU.add)

            layer_norm(0, lambda j: dve.wait_ge(xb_ready[0], j + 1), plus_x)

            for j in range(NT):
                dve.wait_ge(g_done, j + 1)
                if j >= 4:
                    dve.wait_ge(g_ready, j - 3)
                dve.tensor_tensor(g_f[0:rows(j), j % 4, :], ps[0:rows(j), 2 + j % 2, 0:DH], b11_b[0:rows(j), :], ALU.add).then_inc(g_read, 1)
                dve.wait_ge(xT_done, NT + j + 1)
                dve.scalar_tensor_tensor(out=xn[0:rows(j), j, :], in0=b12_b[0:rows(j), :], scalar=deg[0:rows(j), 0, j:j + 1],
                                         in1=xn[0:rows(j), j, :], op0=ALU.mult, op1=ALU.add).then_inc(xb_ready[1], 1)
            dve.wait_ge(deg_sq, 1)
            dve.reciprocal(deg[:, 1, :], degt[:, 1, :]).then_inc(deg_ready, 1)
            dve.wait_ge(t_evac, 3 * NT)
            irregular = dve.value_load(flag_i[0:1, 0:1], min_val=0, max_val=1)
            with dve.If(irregular > 0):
                in_degrees(counts_x, countsT_x)
            with dve.Else():
                in_degrees(counts, countsT)
            dve.wait_ge(deg_step, 4)
            dve.tensor_scalar(degt[:, 2, :], deg[:, 2, :], -1.0, 1.0, ALU.add, ALU.max).then_inc(deg_step, 1)
            dve.wait_ge(deg_sq, 2)
            dve.reciprocal(deg[:, 3, :], degt[:, 3, :]).then_inc(deg_ready, 1)
            layer_norm(1, lambda j: dve.wait_ge(xb_ready[1], j + 1), plus_x)

            dve.wait_ge(deg_ready, 2)
            layer_norm(2, lambda j: dve.wait_ge(xb_ready[2], j + 1),
                       lambda j: lambda xr, y: dve.scalar_tensor_tensor(out=xr, in0=y, scalar=deg[0:rows(j), 3, j:j + 1], in1=xr,
                                                                        op0=ALU.mult, op1=ALU.add))

            dve.wait_ge(x3_copied, 1)
            irregular = dve.value_load(flag_i[0:1, 0:1], min_val=0, max_val=1)
            with dve.If(irregular > 0):
                with dve.Fori(0, NG) as g:
                    for rr in range(TPG):
                        n = g * TPG + rr
                        if rr == 0:
                            dve.wait_ge(fix_x, g * (16 * TPG) + 16)
                            dve.wait_ge(fix_e, g * (16 * TPG) + 16)
                        else:
                            dve.wait_ge(fix_x, g * (16 * TPG) + 16 * (rr + 1))
                            dve.wait_ge(fix_e, g * (16 * TPG) + 16 * (rr + 1))
                        dve.tensor_tensor(xg[:, 0, 0, :], xg[:, 0, 0, :], xg[:, 1, 0, :], ALU.add).then_inc(fix_msg, 1)
                        dve.wait_ge(fix_msg, n * 2 + 1)
                        dve.tensor_scalar(xg[:, 0, 0, :], xg[:, 0, 0, :], 0.0, None, ALU.max)
                        dve.tensor_scalar(fix_hot[:, :], iota_n[:, :],
                                          leftT[:, bass.ds(g, 1), rr:rr + 1].rearrange("p a b -> p (a b)"), None,
                                          ALU.is_equal).then_inc(fix_msg, 1)
                        for cc in range(KC):
                            dve.wait_ge(fix_done, n * KC + cc + 1)
                            for q, (n0, n1) in enumerate(CUTS):
                                ins = dve.tensor_tensor(x3T[:, cc, n0:n1], ps[:, q, 0:n1 - n0], x3T[:, cc, n0:n1], ALU.add)
                            ins.then_inc(fix_added, 1)
                            dve.wait_ge(fix_added, n * KC + cc + 2)

            def add_rows(it, s):
                g, slot = RING * it + s, s % XRING
                dve.wait_ge(xg_loaded[slot], it * (16 * TPG * RING // XRING) + 16 * TPG * (s // XRING + 1))
                dve.wait_ge(ea_loaded[s], it * 16 + 16 * (1 + (isinstance(it, int) and g == NG - 1 and LAST_R > 0)))
                dve.tensor_tensor(ea[:, s, :, :], ea[:, s, :, :], xg[:, slot, :, :], ALU.add).then_inc(add_done, 1)
                if not (isinstance(it, int) and it == 0):
                    dve.wait_ge(scat_done, g - RING + 1)
                dve.tensor_tensor(hot_w[:, s, :, :], iota_n[:, 0:W].unsqueeze(1).to_broadcast([P, TPG, W]),
                                  relwT[:, bass.ds(g, 1), :].rearrange("p a r -> p (a r)").unsqueeze(2).to_broadcast([P, TPG, W]),
                                  ALU.is_equal).then_inc(win_ready, 1)

            def add_pair(p, slot):
                bases = [dve.value_load(base_i[0:1, bass.ds(2 * p + half, 1)], min_val=0, max_val=N - W) for half in range(2)]
                if isinstance(p, int) and p == 0:
                    dve.wait_ge(pre_evac, KC * NCH)
                dve.wait_ge(pair_done, p + 1)
                for half in range(2):
                    dve.wait_ge(pre_added, 2 * p + half)
                    win = preT[:, :, bass.ds(bases[half], W)]
                    dve.tensor_tensor(win, win, ps[:, slot, 0:KC * 2 * W].rearrange("p (f h w) -> p f h w", f=KC, h=2)[:, :, half, :],
                                      ALU.add).then_inc(pre_added, 1)

            PAIRS = RING // 2

            def stream(it):
                for s in range(RING):
                    add_rows(it, s)
                    if s % 2 and not (isinstance(it, int) and it == 0 and s < RING - 1):
                        lag = PAIRS - 1 - s // 2
                        add_pair(PAIRS * it - lag, (PAIRS - lag) % PAIRS)

            stream(0)
            with dve.Fori(1, ITERS - 1) as it:
                stream(it)
            stream(ITERS - 1)
            for p in range(NG // 2 - PAIRS + 1, NG // 2):
                add_pair(p, p % PAIRS)

            def bn_finish(cc):
                dve.wait_ge(bn_sq, cc + 1)
                one = slice(cc, cc + 1)
                chain = [dve.reciprocal(bn_t[:, 1, one], bn_t[:, 0, one]).then_inc(bn_calc, 1)]
                dve.wait_ge(bn_calc, 3 * cc + 1)
                dve.tensor_tensor(bn_t[:, 2, one], bn_t[:, 1, one], cols[:, 3, one], ALU.mult).then_inc(bn_calc, 1)
                dve.wait_ge(bn_calc, 3 * cc + 2)
                dve.tensor_tensor(bn_t[:, 1, one], bn_mv[:, cc, 0:1], bn_t[:, 2, one], ALU.mult).then_inc(bn_calc, 1)
                dve.wait_ge(bn_calc, 3 * cc + 3)
                dve.tensor_tensor(bn_t[:, 3, one], cols[:, 4, one], bn_t[:, 1, one], ALU.subtract).then_inc(bn_ready, 1)

            for cc in range(KC):
                for q, (n0, n1) in enumerate(CUTS):
                    n = cc * NCH + q
                    dve.wait_ge(w32_done, n + 1)
                    dve.scalar_tensor_tensor(out=hT[:, cc, n0:n1], in0=ps[:, n % 4, 0:n1 - n0], scalar=cols[:, 2, cc:cc + 1],
                                             in1=hT[:, cc, n0:n1], op0=ALU.add, op1=ALU.add).then_inc(h2_ready, 1)
                    dve.wait_ge(h2_ready, n + 1)
                    ins = dve.bn_stats(bn_st[:, cc, q, :], hT[:, cc, n0:n1])
                ins.then_inc(bn_step, 1)
                dve.wait_ge(bn_step, 2 * cc + 1)
                dve.bn_aggr(bn_mv[:, cc, :], bn_st[:, cc, :, :].rearrange("p q s -> p (q s)")).then_inc(bn_step, 1)
                if cc:
                    bn_finish(cc - 1)
            bn_finish(KC - 1)
            layer_norm(3, lambda j: None, plus_x)

        @block.tensor
        def _(pe):
            def transpose_x(n, j, src_t, ready):
                ready(j)
                if n >= 2:
                    pe.wait_ge(xT_evac, n - 1)
                for cc in range(KC):
                    ins = pe.transpose(ps[:, n % 2, P * cc:P * cc + rows(j)], src_t[0:rows(j), j, P * cc:P * cc + P],
                                       ident[0:rows(j), 0:rows(j)])
                ins.then_inc(xT_done, 1)

            pe.wait_ge(consts, 2)
            for j in range(NT):
                transpose_x(j, j, xn, lambda j: pe.wait_ge(x_loaded[j // 3], 16))

            pe.wait_ge(rows_ready, 1)
            for bank, names in ((4, ("code", "lo", "relw")), (3, ("dst",)), (5, ("left", "src"))):
                for k, name in enumerate(names):
                    for r in range(TPG):
                        pe.transpose(ps[:, bank, (k * TPG + r) * NG:(k * TPG + r + 1) * NG], row[name][:, r:GE:TPG], ident[0:NG, 0:NG])
            off = 2 * NG * TPG
            pe.transpose(ps[:, 5, off:off + NG], base_row[:, :], ident[0:NG, 0:NG])
            pe.transpose(ps[:, 5, off + NG:off + 2 * NG], left_row[:, :], ident[0:NG, 0:NG]).then_inc(idx_done, 1)

            def count_group(g, half):
                pe.wait_ge(hot_ready, g + 1)
                if not (isinstance(g, int) and g < 2):
                    pe.wait_ge(cnt_added, g - 1)
                for r in range(TPG):
                    ins = pe.matmul(ps[:, 6 + half, 0:NCODE], hot_lo[:, half, r, :], hot_code[:, half, r, :],
                                    start=(r == 0), stop=(r == TPG - 1))
                ins.then_inc(cnt_done, 1)

            count_group(0, 0)
            count_group(1, 1)
            pe.wait_ge(w01_loaded, 16)
            for j in range(NT):
                pe.wait_ge(xT_evac, j + 1)
                if j >= 2:
                    pe.wait_ge(u_evac, j - 1)
                for k in range(KC):
                    ins = pe.matmul(ps[0:rows(j), 2 + j % 2, :], xT0[:, k, P * j:P * j + rows(j)], w01_s[:, k, :],
                                    start=(k == 0), stop=(k == KC - 1))
                ins.then_inc(u_done, 1)
                with pe.Fori(1 + 2 * j, 3 + 2 * j) as i:
                    count_group(2 * i, 0)
                    count_group(2 * i + 1, 1)

            irregular = pe.value_load(flag_i[0:1, 0:1], min_val=0, max_val=1)
            with pe.If(irregular > 0):
                pe.sem_inc(fixc_added, 1)
                with pe.Fori(0, NG) as g:
                    for r in range(TPG):
                        for h in range(NT):
                            n = (g * TPG + r) * NT + h
                            pe.wait_ge(fixc_hot, n + 1)
                            pe.wait_ge(fixc_added, n + 1)
                            for q, (n0, n1) in enumerate(CUTS):
                                ins = pe.matmul(ps[0:rows(h), 4 + q, 0:n1 - n0], fixc_src[:, 0:rows(h)], fixc_dst[:, n0:n1],
                                                start=True, stop=True)
                            ins.then_inc(fixc_done, 1)

            def aggregate(layer, blocks, high, low, adj_r, adj):
                def job(parts, rhs, cc, n):
                    pairs = [(part, j) for j in range(NT) for part in parts]
                    for m, (part, j) in enumerate(pairs):
                        ins = pe.matmul(ps[:, cc, 0:CH], part[0:rows(j), j, P * cc:P * cc + P], rhs[0:rows(j), j, n],
                                        start=(m == 0), stop=(m == len(pairs) - 1))
                    ins.then_inc(agg_done[layer], 1)

                def chunks(parts, rhs):
                    with pe.Fori(0, NCH) as i:
                        for cc in range(blocks):
                            pe.wait_ge(agg_evac[layer], i * blocks + cc + 1)
                            job(parts, rhs, cc, bass.ds(i * CS, CH))

                irregular = pe.value_load(flag_i[0:1, 0:1], min_val=0, max_val=1)
                with pe.If(irregular > 0):
                    chunks([high[:, :, :].bitcast(F32), low[:, :, :].bitcast(F32)], adj)
                with pe.Else():
                    chunks([high, low], adj_r)

            def project(act_t, kc, w, j, n):
                if n >= 2:
                    pe.wait_ge(y_read, n - 1)
                for k in range(kc):
                    ins = pe.matmul(ps[0:rows(j), 4 + n % 2, :], act_t[:, k, P * j:P * j + rows(j)], w[:, k, :],
                                    start=(k == 0), stop=(k == kc - 1))
                ins.then_inc(y_done, 1)

            pe.wait_ge(u_ready, NT)
            pe.wait_ge(diag_added, 2)
            aggregate(0, KC, u_hi, u_lo, counts, counts_x)
            pe.wait_ge(w02_loaded, 16)
            pe.wait_ge(agg_evac[0], KC * NCH + KC)

            def project_and_turn(c):
                for j in range(NT):
                    project(h1T0, KC, w02_s, j, j)
                    for q in range(3):
                        t = 3 * j + q
                        if t >= 4:
                            pe.wait_ge(t_evac, t - 3)
                        for i in range(4 * q, min(4 * q + 4, NT)):
                            ins = pe.transpose(ps[0:rows(j), t % 4, P * (i - 4 * q):P * (i - 4 * q) + rows(i)],
                                               f32(c[0:rows(i), i, P * j:P * j + rows(j)]), ident[0:rows(i), 0:rows(i)])
                        ins.then_inc(t_done, 1)

            irregular = pe.value_load(flag_i[0:1, 0:1], min_val=0, max_val=1)
            with pe.If(irregular > 0):
                project_and_turn(counts_x)
            with pe.Else():
                project_and_turn(counts)

            pe.wait_ge(t_evac, 3 * NT)
            pe.wait_ge(w1_loaded, 32)

            def hidden(j):
                pe.wait_ge(xT_evac, NT + j + 1)
                if j >= 2:
                    pe.wait_ge(g_read, j - 1)
                for k in range(KC):
                    ins = pe.matmul(ps[0:rows(j), 2 + j % 2, 0:DH], x1T[:, k, P * j:P * j + rows(j)], w11_s[:, k, :],
                                    start=(k == 0), stop=(k == KC - 1))
                ins.then_inc(g_done, 1)

            for j in range(NT):
                transpose_x(NT + j, j, xn, lambda j: pe.wait_ge(x_ready, j + 1))
                if j:
                    hidden(j - 1)
            hidden(NT - 1)
            pe.wait_ge(g_ready, NT)
            aggregate(1, DH // P, g_hi, g_lo, countsT, countsT_x)
            pe.wait_ge(agg_evac[1], (DH // P) * (NCH + 1))
            for j in range(NT):
                project(z1T, DH // P, w12_s, j, NT + j)

            pe.wait_ge(xs_ready, NT)
            pe.wait_ge(diag_taken, 2)
            aggregate(2, KC, xs_hi, xs_lo, counts, counts_x)
            pe.wait_ge(w2_loaded, 16)
            pe.wait_ge(agg_evac[2], KC * (NCH + 1))
            for j in range(NT):
                project(z2T, KC, w2_s, j, 2 * NT + j)
                if j >= TLAG:
                    transpose_x(2 * NT + j - TLAG, j - TLAG, xn, lambda j: pe.wait_ge(x_ready, 2 * NT + j + 1))

            for j in range(NT - TLAG, NT):
                transpose_x(2 * NT + j, j, xn, lambda j: pe.wait_ge(x_ready, 2 * NT + j + 1))
            irregular = pe.value_load(flag_i[0:1, 0:1], min_val=0, max_val=1)
            with pe.If(irregular > 0):
                pe.wait_ge(xT_evac, 3 * NT)
                pe.sem_inc(fix_added, 1)
                with pe.Fori(0, NG) as g:
                    for r in range(TPG):
                        n = g * TPG + r
                        pe.wait_ge(fix_msg, n * 2 + 2)
                        for cc in range(KC):
                            pe.wait_ge(fix_added, n * KC + cc + 1)
                            for q, (n0, n1) in enumerate(CUTS):
                                ins = pe.matmul(ps[:, q, 0:n1 - n0], xg[:, 0, 0, P * cc:P * cc + P], fix_hot[:, n0:n1],
                                                start=True, stop=True)
                            ins.then_inc(fix_done, 1)
                pe.wait_ge(fix_added, NG * TPG * KC + 1)
            pe.wait_ge(xT_evac, 3 * NT)
            pe.wait_ge(w3_loaded, 32)

            def pre_job(n):
                cc, (n0, n1) = n // NCH, CUTS[n % NCH]
                if n >= 4:
                    pe.wait_ge(pre_evac, n - 3)
                for k in range(KC):
                    ins = pe.matmul(ps[:, n % 4, 0:n1 - n0], w31_s[:, k, P * cc:P * cc + P], x3T[:, k, n0:n1],
                                    start=(k == 0), stop=(k == KC - 1))
                ins.then_inc(pre_done, 1)

            def scatter(it, s):
                g = RING * it + s
                pe.wait_ge(relu_done, g + 1)
                pe.wait_ge(win_ready, g + 1)
                if not (isinstance(g, int) and g < 2):
                    pe.wait_ge(zg_ready, g - 1)
                for r in range(TPG):
                    for cc in range(KC):
                        ins = pe.matmul(ps[:, 4 + s % 2, cc * W:cc * W + W], ea[:, s, r, P * cc:P * cc + P], hot_w[:, s, r, :],
                                        start=(r == 0 and cc == 0), stop=(r == TPG - 1 and cc == KC - 1))
                ins.then_inc(scat_done, 1)

            def pair(p, slot):
                pe.wait_ge(zg_ready, 2 * p + 2)
                if not (isinstance(p, int) and p < PAIRS):
                    pe.wait_ge(pre_added, 2 * (p - PAIRS) + 2)
                for f in range(KC):
                    for k in range(KC):
                        ins = pe.matmul(ps[:, slot, f * 2 * W:(f + 1) * 2 * W], w31_s[:, k, P * f:P * f + P],
                                        zg[:, slot, k, :, :].rearrange("p h w -> p (h w)"),
                                        start=(f == 0 and k == 0), stop=(f == KC - 1 and k == KC - 1))
                ins.then_inc(pair_done, 1)

            PAIRS = RING // 2

            for n in range(PRE_LEAD):
                pre_job(n)
            for s in range(RING):
                scatter(0, s)
                for n in pre_after(s):
                    pre_job(n)
                if s == RING - 2:
                    pe.wait_ge(pre_evac, KC * NCH)
                if s >= RING - 2:
                    pair(s - RING + 2, s - RING + 2)
            with pe.Fori(1, ITERS) as it:
                for s in range(RING):
                    scatter(it, s)
                    if s % 2 == 0:
                        pair(PAIRS * it + s // 2 - 1, (s // 2 - 1) % PAIRS)
            pair(NG // 2 - 1, PAIRS - 1)

            pe.wait_ge(h1_ready, KC)
            for cc in range(KC):
                for q, (n0, n1) in enumerate(CUTS):
                    n = cc * NCH + q
                    if n >= 4:
                        pe.wait_ge(h2_ready, n - 3)
                    for k in range(KC):
                        ins = pe.matmul(ps[:, n % 4, 0:n1 - n0], w32_s[:, k, P * cc:P * cc + P], preT[:, k, n0:n1],
                                        start=(k == 0), stop=(k == KC - 1))
                    ins.then_inc(w32_done, 1)
            pe.wait_ge(hn_ready, KC)
            for j in range(NT):
                n = 3 * NT + j
                pe.wait_ge(y_read, n - 1)
                for cc in range(KC):
                    ins = pe.transpose(ps[0:rows(j), 4 + n % 2, P * cc:P * cc + P], hT[:, cc, P * j:P * j + rows(j)], ident[:, :])
                ins.then_inc(y_done, 1)


_INS = ['x', 'src', 'dst', 'edge_attr_512', 'L0_gnn_W1', 'L0_gnn_b1', 'L0_gnn_W2', 'L0_gnn_b2', 'L1_gnn_W1', 'L1_gnn_b1',
        'L1_gnn_W2', 'L1_gnn_b2', 'L2_gnn_W', 'L2_gnn_b', 'L3_gnn_W1', 'L3_gnn_b1', 'L3_gnn_W2', 'L3_gnn_b2',
        'L3_gnn_gamma', 'L3_gnn_beta']
_OUTS = [((1250, 512), 'float32')]


def kernel(**inputs):
    import numpy as _np
    import concourse.bacc as _bacc
    from concourse import mybir as _mybir
    from concourse.bass_utils import run_bass_kernel_spmd as _run

    nc = _bacc.Bacc("TRN2", target_bir_lowering=False, num_devices=1)
    arrays, args = {}, []
    for name in _INS:
        a = _np.ascontiguousarray(inputs[name])
        arrays[f"in_{name}_dram"] = a
        args.append(nc.dram_tensor(f"in_{name}_dram", a.shape, _mybir.dt.from_np(a.dtype), kind="ExternalInput").ap())
    for i, (shape, dtype) in enumerate(_OUTS):
        dt = _mybir.dt.from_np(_np.dtype(dtype))
        args.append(nc.dram_tensor(f"out_{i}_dram", shape, dt, kind="ExternalOutput").ap())
    args.append(nc.dram_tensor("x3_dram", (1250, 512), _mybir.dt.float32, kind="Internal").ap())
    gnn_kernel(nc, *args)
    r = _run(nc, [arrays], core_ids=[0])
    got = tuple(r.results[0][f"out_{i}_dram"] for i in range(len(_OUTS)))
    return got[0]
```

```python
from contextlib import ExitStack

import concourse.bass as bass
from concourse import mybir

F32 = mybir.dt.float32
F32R = mybir.dt.float32r
BF16 = mybir.dt.bfloat16
F16 = mybir.dt.float16
I32 = mybir.dt.int32
ALU = mybir.AluOpType
ACT = mybir.ActivationFunctionType
AX = mybir.AxisListType

P = 128
N = 1250
D = 512
DH = 256
E = 21250
KC = D // P
NT = (N + P - 1) // P
TAIL = N - (NT - 1) * P
TPG = 4
GE = P * TPG
NG = (E + GE - 1) // GE
LAST = E - (NG - 1) * GE
LAST_P, LAST_R = divmod(LAST, TPG)
W = 48
NCODE = NT * W
CH = 418
CS = CH - 2
NCH = 3
CUTS = [(0, CH), (CH, 2 * CS + 2), (2 * CS + 2, N)]
BLOCK_SPAN = 7
RING = 6
JOIN = 3
JOINS = RING // JOIN
POOL_HOTS = 2
HOTS = 4
XRING = 3
ITERS = NG // RING
PRE_LEAD = 4
TLAG = 3
EPS = 1e-5
assert CS * (NCH - 1) + CH == N and NCODE <= 512 and NG % RING == 0 and RING % XRING == 0 and RING % JOIN == 0 and NG == 2 + NT * HOTS
assert BLOCK_SPAN * GE + 1 <= 4096 and LAST_P < P


def pre_after(s):
    return range(PRE_LEAD + 2 * s, min(PRE_LEAD + 2 * s + 2, KC * NCH))


def rows(j):
    return P if j < NT - 1 else TAIL


def gnn_kernel(nc, x, src, dst, edge_attr, w01, b01, w02, b02, w11, b11, w12, b12, w2, b2,
               w31, b31, w32, b32, gamma, beta, out, x3_dram):
    with ExitStack() as ctx:
        cursor = [(nc.sbuf_base + 31) // 32 * 32]

        def place(nbytes):
            at = cursor[0]
            cursor[0] += (nbytes + 31) // 32 * 32
            return at

        def at(name, shape, dtype, offset):
            return nc.alloc_sbuf_tensor_at(name, shape, dtype, offset=offset)

        def sb(name, shape, dtype):
            size = 2 if dtype in (BF16, F16) else 4
            n = 1
            for s in shape[1:]:
                n *= s
            return at(name, shape, dtype, place(n * size))

        def sem(name):
            return ctx.enter_context(nc.semaphore(name))

        xn = sb("xn", [P, NT, D], F32)
        r_z, r_h = place(NT * D * 4), place(NT * D * 4)
        r_c, r_a = place(NT * N * 4 + 16), place(NT * N * 4 + 16)
        r_w = place(2 * KC * D * 4)
        w11_at = cursor[0]
        w11_s = sb("w11_s", [P, KC, DH], F32)
        w12_s = sb("w12_s", [P, DH // P, D], F32)
        w2_s = sb("w2_s", [P, KC, D], F32)
        w01_s, w02_s = (at(n, [P, KC, D], F32, r_w + i * KC * D * 4) for i, n in enumerate(("w01_s", "w02_s")))
        w31_s, w32_s = (at(n, [P, KC, D], F32, r_w + i * KC * D * 4) for i, n in enumerate(("w31_s", "w32_s")))

        counts = at("counts", [P, NT, N], F32R, r_c)
        countsT = at("countsT", [P, NT, N], F32R, r_a)
        counts_x = at("counts_x", [P, NT, N], F32, r_c)
        countsT_x = at("countsT_x", [P, NT, N], F32, r_a)

        def f32(ap):
            return ap if ap.dtype == F32 else ap.bitcast(F32)

        xT0 = at("xT0", [P, KC, N], F32, r_z)
        u_hi = at("u_hi", [P, NT, D], F32R, r_h)
        a = r_a
        hot_code = at("hot_code", [P, HOTS, TPG, NCODE], BF16, a); a += HOTS * TPG * NCODE * 2
        hot_lo = at("hot_lo", [P, HOTS, TPG, P], BF16, a); a += HOTS * TPG * P * 2
        codeT = at("codeT", [P, NG, TPG], F32, a); a += NG * TPG * 4
        src_loT = at("src_loT", [P, NG, TPG], F32, a); a += NG * TPG * 4
        dstT = at("dstT", [P, NG, TPG], F32, a); a += NG * TPG * 4
        row_at = a
        u_f = at("u_f", [P, 2, D], F32, a); a += 2 * D * 4
        u_lo = at("u_lo", [P, NT, D], F32R, a)
        h1T0 = at("h1T0", [P, KC, N], F32, r_z)
        row = {}
        for n in ("dst_i", "src_i", "lo_i", "hi_i"):
            row[n] = at("row_" + n, [NG, GE], I32, row_at); row_at += GE * 4
        for n in ("dst", "src", "lo", "hi", "rel", "valid", "code", "relw", "left"):
            row[n] = at("row_" + n, [NG, GE], F32, row_at); row_at += GE * 4
        base_row = at("base_row", [NG, P], F32, row_at); row_at += P * 4
        left_row = at("left_row", [NG, P], F32, row_at); row_at += P * 4
        left_max = at("left_max", [NG, 1], F32, row_at); row_at += 32
        assert row_at <= r_a + NT * N * 4
        fixc_dst = at("fixc_dst", [P, N], BF16, r_a)
        fixc_src = at("fixc_src", [P, P], BF16, r_a + 2 * TPG * NCODE * 2)
        x1T = at("x1T", [P, KC, N], F32, r_h)
        g_f = at("g_f", [P, 4, DH], F32, r_w)
        g_hi = at("g_hi", [P, NT, DH], F32R, r_z)
        g_lo = at("g_lo", [P, NT, DH], F32R, r_z + NT * DH * 4)
        z1T = at("z1T", [P, DH // P, N], F32, r_h)
        xs_hi = at("xs_hi", [P, NT, D], F32R, r_z)
        xs_lo = at("xs_lo", [P, NT, D], F32R, r_a)
        xs_f = at("xs_f", [P, 2, D], F32, r_a + NT * D * 4)
        z2T = at("z2T", [P, KC, N], F32, r_h)
        x3T = at("x3T", [P, KC, N], F32, r_z)
        hT = at("hT", [P, KC, N], F32, r_h)
        ea = at("ea", [P, RING, TPG, D], F32, r_a)
        c = r_c
        xg = at("xg", [P, XRING, TPG, D], F32, c); c += XRING * TPG * D * 4
        preT = at("preT", [P, KC, N], F32, c); c += KC * N * 4
        zg = at("zg", [P, JOINS, KC, JOIN, W], F32, c); c += RING * KC * W * 4
        assert c <= r_c + NT * N * 4
        fix_hot = at("fix_hot", [P, N], F32, r_c + 2 * TPG * D * 4)

        ident = sb("ident", [P, P], F32)
        b02_b = sb("b02_b", [P, D], F32)
        b11_b = sb("b11_b", [P, DH], F32)
        b12_b = sb("b12_b", [P, D], F32)
        b2_b = sb("b2_b", [P, D], F32)
        cols = sb("cols", [P, 5, KC], F32)
        relwT = sb("relwT", [P, NG, TPG], F32)
        leftT = sb("leftT", [P, NG, TPG], F32)
        srcT = sb("srcT", [P, NG, TPG], F32)
        srcT_i = sb("srcT_i", [P, NG, TPG], I32)
        idx4 = sb("idx4", [P, XRING, TPG], I32)
        iota_n = sb("iota_n", [P, N], F16)
        lo_col = sb("lo_col", [P, HOTS, TPG], F32)
        hot_w = at("hot_w", [P, RING, TPG, W], F32, w11_at)
        base_f = sb("base_f", [1, NG], F32)
        base_i = sb("base_i", [1, NG], I32)
        gap = sb("gap", [1, NG], F32)
        flag4 = sb("flag4", [1, 4], F32)
        flag_i = sb("flag_i", [1, 1], I32)
        eps_s = sb("eps_s", [P, 1], F32)
        stats = sb("stats", [P, 2, 6], F32)
        mv = sb("mv", [P, 2, 2], F32)
        std = sb("std", [P, 2], F32)
        rstd = sb("rstd", [P, 2], F32)
        deg = sb("deg", [P, 4, NT], F32)
        degt = sb("degt", [P, 4, NT], F32)
        bn_st = sb("bn_st", [P, KC, NCH, 6], F32)
        bn_mv = sb("bn_mv", [P, KC, 2], F32)
        bn_t = sb("bn_t", [P, 4, KC], F32)
        assert cursor[0] <= nc.sbuf_usable_end, cursor[0] - nc.sbuf_usable_end

        ps = ctx.enter_context(nc.psum_tensor("ps", [P, 8, 512], F32))

        rows_loaded = sem("rows_loaded")
        x_loaded = [sem(f"x_loaded{i}") for i in range(4)]
        w01_loaded, w02_loaded = sem("w01_loaded"), sem("w02_loaded")
        w1_loaded, w2_loaded, w3_loaded = sem("w1_loaded"), sem("w2_loaded"), sem("w3_loaded")
        bias_loaded = sem("bias_loaded")
        cols_loaded = sem("cols_loaded")
        consts = sem("consts")
        counts_zero = sem("counts_zero")
        row_pad = sem("row_pad")
        prep = sem("prep")
        rows_ready = sem("rows_ready")
        idx_done = sem("idx_done")
        idx_ready = sem("idx_ready")
        xT_done, xT_evac = sem("xT_done"), sem("xT_evac")
        u_done, u_evac, u_ready = sem("u_done"), sem("u_evac"), sem("u_ready")
        lo_staged, lo_seen = sem("lo_staged"), sem("lo_seen")
        hot_ready, lo_ready, cnt_done, cnt_added = sem("hot_ready"), sem("lo_ready"), sem("cnt_done"), sem("cnt_added")
        fixc_hot, fixc_done, fixc_added = sem("fixc_hot"), sem("fixc_done"), sem("fixc_added")
        diag_added, diag_taken = sem("diag_added"), sem("diag_taken")
        agg_done = [sem(f"agg_done{i}") for i in range(3)]
        agg_evac = [sem(f"agg_evac{i}") for i in range(3)]
        y_done, y_read = sem("y_done"), sem("y_read")
        xb_ready = [sem(f"xb_ready{i}") for i in range(3)]
        ln_step, std_ready, rstd_ready, x_ready = sem("ln_step"), sem("std_ready"), sem("rstd_ready"), sem("x_ready")
        t_done, t_evac = sem("t_done"), sem("t_evac")
        g_done, g_read, g_relu, g_ready = sem("g_done"), sem("g_read"), sem("g_relu"), sem("g_ready")
        deg_set, deg_step, deg_sq, deg_ready = sem("deg_set"), sem("deg_step"), sem("deg_sq"), sem("deg_ready")
        xs_done, xs_ready = sem("xs_done"), sem("xs_ready")
        x3_stored = sem("x3_stored")
        x3_copied = sem("x3_copied")
        pre_done, pre_evac = sem("pre_done"), sem("pre_evac")
        ea_loaded = [sem(f"ea_loaded{i}") for i in range(RING)]
        xg_loaded = [sem(f"xg_loaded{i}") for i in range(XRING)]
        idx_staged, idx_seen = sem("idx_staged"), sem("idx_seen")
        add_done, relu_done, win_ready = sem("add_done"), sem("relu_done"), sem("win_ready")
        scat_done, zg_ready, join_done, pre_added = sem("scat_done"), sem("zg_ready"), sem("join_done"), sem("pre_added")
        fix_x, fix_e, fix_msg, fix_done, fix_added = (sem("fix_x"), sem("fix_e"), sem("fix_msg"), sem("fix_done"), sem("fix_added"))
        fix_idx = sem("fix_idx")
        h1_ready = sem("h1_ready")
        w32_done, h2_ready, bn_step, bn_sq, bn_ready, hn_ready = (
            sem("w32_done"), sem("h2_ready"), sem("bn_step"), sem("bn_sq"), sem("bn_ready"), sem("hn_ready"))
        bn_calc = sem("bn_calc")
        out_stored = sem("out_stored")

        def node_rows(t):
            return t[0:(NT - 1) * P, :].rearrange("(j p) d -> p j d", p=P)

        def w_view(t):
            return t.rearrange("(k p) n -> p k n", p=P)

        def feature_cols(t):
            return t.rearrange("(c p) -> p c", p=P)

        def ea_rows(g):
            return edge_attr[bass.ds(g * GE, GE), :].rearrange("(p r) d -> p (r d)", p=P)

        def join_bank(slot):
            return ps[:, 2 * slot:2 * slot + 2, 0:2 * JOIN * W].rearrange("p b (f h w) -> p b f h w", f=2, h=JOIN)

        block = ctx.enter_context(nc.Block())

        @block.sync
        def _(sp):
            sp.wait_ge(row_pad, 2)
            for n, t in (("dst_i", dst), ("src_i", src)):
                sp.dma_start(row[n][0:NG - 1, :], t[0:(NG - 1) * GE].rearrange("(g e) -> g e", e=GE)).then_inc(rows_loaded, 16)
                sp.dma_start(row[n][NG - 1:NG, 0:LAST],
                             t[(NG - 1) * GE:E].rearrange("(a e) -> a e", a=1)).then_inc(rows_loaded, 16)
            for i in range(3):
                sp.dma_start(xn[:, 3 * i:3 * i + 3, :], node_rows(x)[:, 3 * i:3 * i + 3, :]).then_inc(x_loaded[i], 16)
            sp.dma_start(xn[0:TAIL, NT - 1, :], x[(NT - 1) * P:N, :]).then_inc(x_loaded[3], 16)
            sp.dma_start(w01_s[:, :, :], w_view(w01)).then_inc(w01_loaded, 16)
            sp.dma_start(cols[:, 0, :], feature_cols(b01), allow_slow_non_contiguous=True).then_inc(cols_loaded, 16)
            sp.dma_start(w02_s[:, :, :], w_view(w02)).then_inc(w02_loaded, 16)
            for t, b in ((b02_b, b02), (b11_b, b11), (b12_b, b12), (b2_b, b2)):
                sp.dma_start(t[:, :], b.partition_broadcast(P)).then_inc(bias_loaded, 16)
            sp.dma_start(w11_s[:, :, :], w_view(w11)).then_inc(w1_loaded, 16)
            sp.dma_start(w12_s[:, :, :], w_view(w12)).then_inc(w1_loaded, 16)
            sp.dma_start(w2_s[:, :, :], w_view(w2)).then_inc(w2_loaded, 16)
            for i, b in enumerate((b31, b32, gamma, beta)):
                sp.dma_start(cols[:, 1 + i, :], feature_cols(b), allow_slow_non_contiguous=True).then_inc(cols_loaded, 16)
            sp.wait_ge(g_ready, NT)
            sp.dma_start(w31_s[:, :, :], w_view(w31)).then_inc(w3_loaded, 16)
            sp.dma_start(w32_s[:, :, :], w_view(w32)).then_inc(w3_loaded, 16)

            sp.wait_ge(agg_done[2], NCH * KC)
            for s in range(RING):
                sp.dma_start(ea[:, s, :, :].rearrange("p r d -> p (r d)"), ea_rows(s)).then_inc(ea_loaded[s], 16)
            for j in range(NT):
                sp.wait_ge(x_ready, 2 * NT + j + 1)
                sp.dma_start(x3_dram[j * P:j * P + rows(j), :], xn[0:rows(j), j, :]).then_inc(x3_stored, 16)

            def reload(it, s):
                sp.wait_ge(scat_done, RING * (it - 1) + s + 1)
                g = RING * it + s
                if isinstance(it, int) and g == NG - 1:
                    e0 = g * GE
                    sp.dma_start(ea[0:LAST_P, s, :, :].rearrange("p r d -> p (r d)"),
                                 edge_attr[e0:e0 + LAST_P * TPG, :].rearrange("(p r) d -> p (r d)", r=TPG)).then_inc(ea_loaded[s], 16)
                    if LAST_R:
                        sp.dma_start(ea[LAST_P:LAST_P + 1, s, 0:LAST_R, :].rearrange("p r d -> p (r d)"),
                                     edge_attr[e0 + LAST_P * TPG:E, :].rearrange("(p r) d -> p (r d)", p=1)).then_inc(ea_loaded[s], 16)
                else:
                    sp.dma_start(ea[:, s, :, :].rearrange("p r d -> p (r d)"), ea_rows(g)).then_inc(ea_loaded[s], 16)

            with sp.Fori(1, ITERS - 1) as it:
                for s in range(RING):
                    reload(it, s)
            for s in range(RING):
                reload(ITERS - 1, s)

            for j in range(NT):
                sp.wait_ge(x_ready, 3 * NT + j + 1)
                sp.dma_start(out[j * P:j * P + rows(j), :], xn[0:rows(j), j, :]).then_inc(out_stored, 16)
            sp.wait_ge(x3_stored, 16 * NT)
            sp.wait_ge(out_stored, 16 * NT)

        @block.gpsimd
        def _(pool):
            pool.memset(ident[:, :], 0.0).then_inc(consts, 1)
            pool.wait_ge(consts, 1)
            pool.affine_select(out=ident[:, :], in_=ident[:, :], compare_op=ALU.not_equal, fill=1.0, base=0,
                               pattern=[[-1, P]], channel_multiplier=1).then_inc(consts, 1)
            pool.iota(iota_n[:, :], [[1, N]], base=0, channel_multiplier=0, allow_small_or_imprecise_dtypes=True).then_inc(consts, 1)
            pool.memset(eps_s[:, :], EPS).then_inc(consts, 1)
            pool.memset(f32(counts[:, :, :]), 0.0).then_inc(counts_zero, 1)
            pool.wait_ge(idx_ready, 1)

            def lo_hots(g, slot):
                if not (isinstance(g, int) and g < HOTS):
                    pool.wait_ge(cnt_done, g - HOTS + 1)
                pool.tensor_copy(lo_col[:, slot, :], src_loT[:, bass.ds(g, 1), :].rearrange("p a b -> p (a b)")).then_inc(lo_staged, 1)
                pool.wait_ge(lo_staged, g + 1)
                pool.sem_inc(lo_seen, 1)
                for r in range(POOL_HOTS):
                    ins = pool.tensor_scalar(hot_lo[:, slot, r, :], iota_n[:, 0:P], lo_col[:, slot, r:r + 1], None, ALU.is_equal)
                ins.then_inc(lo_ready, 1)

            def low_u(j, slot, n):
                pool.wait_ge(u_evac, j + 1)
                at_j = slice(j, j + 1) if isinstance(j, int) else bass.ds(j, 1)
                pool.tensor_tensor(u_lo[0:n, at_j, :], u_f[0:n, slot:slot + 1, :], u_hi[0:n, at_j, :].bitcast(F32),
                                   ALU.subtract).then_inc(u_ready, 1)

            for g in range(2 + HOTS):
                lo_hots(g, g % HOTS)
            with pool.Fori(0, NT // 2 - 1) as h:
                for i in range(2):
                    for k in range(HOTS):
                        lo_hots(HOTS * (2 * h + i + 1) + k + 2, (k + 2) % HOTS)
                    low_u(2 * h + i, i, P)
            for k in range(HOTS):
                lo_hots(HOTS * (NT - 1) + k + 2, (k + 2) % HOTS)
            low_u(NT - 2, 0, P)
            low_u(NT - 1, 1, TAIL)
            pool.wait_ge(bias_loaded, 64)
            for j in range(NT):
                pool.tensor_tensor(xn[0:rows(j), j, :], xn[0:rows(j), j, :], b02_b[0:rows(j), :], ALU.add).then_inc(xb_ready[0], 1)
            for j in range(NT):
                pool.wait_ge(g_relu, j + 1)
                pool.tensor_tensor(g_lo[0:rows(j), j, :], g_f[0:rows(j), j % 4, :], g_hi[0:rows(j), j, :].bitcast(F32),
                                   ALU.subtract).then_inc(g_ready, 1)
            for j in range(NT):
                pool.wait_ge(xs_done, j + 1)
                pool.tensor_tensor(xs_lo[0:rows(j), j, :], xs_f[0:rows(j), j % 2, :], xs_hi[0:rows(j), j, :].bitcast(F32),
                                   ALU.subtract).then_inc(xs_ready, 1)
            for j in range(NT):
                pool.tensor_tensor(xn[0:rows(j), j, :], xn[0:rows(j), j, :], b2_b[0:rows(j), :], ALU.add).then_inc(xb_ready[2], 1)

            pool.wait_ge(x3_stored, 16 * NT)
            pool.wait_ge(agg_done[2], NCH * KC)
            irregular = pool.value_load(flag_i[0:1, 0:1], min_val=0, max_val=1)
            with pool.If(irregular > 0):
                def fix_load(g, r, attrs):
                    n = g * TPG + r
                    pool.tensor_copy(idx4[:, 0, 0:1], srcT_i[:, bass.ds(g, 1), r:r + 1].rearrange("p a b -> p (a b)")).then_inc(fix_idx, 1)
                    pool.wait_ge(fix_idx, n + 1)
                    pool.sem_inc(idx_seen, 1)
                    pool.indirect_dma_start(out=xg[:, 0, 0, :], out_offset=None, in_=x3_dram[:, :],
                                            in_offset=bass.IndirectOffsetOnAxis(ap=idx4[:, 0, 0:1], axis=0)).then_inc(fix_x, 16)
                    pool.dma_start(xg[0:attrs.shape[0], 1, 0, :], attrs).then_inc(fix_e, 16)
                    pool.wait_ge(fix_added, n * KC + KC + 1)
                with pool.Fori(0, NG - 1) as g:
                    for r in range(TPG):
                        fix_load(g, r, edge_attr[bass.ds(g * GE, GE), :].rearrange("(p r) d -> r p d", r=TPG)[r, :, :])
                for r in range(TPG):
                    fix_load(NG - 1, r, edge_attr[(NG - 1) * GE + r:E:TPG, :])

            def gather(it, s):
                g, slot = RING * it + s, s % XRING
                if not (isinstance(g, int) and g < XRING):
                    pool.wait_ge(add_done, g - XRING + 1)
                pool.tensor_copy(idx4[:, slot, :], srcT_i[:, bass.ds(g, 1), :].rearrange("p a b -> p (a b)")).then_inc(idx_staged, 1)
                pool.wait_ge(idx_staged, g + 1)
                pool.sem_inc(idx_seen, 1)
                for r in range(TPG):
                    pool.indirect_dma_start(out=xg[:, slot, r, :], out_offset=None, in_=x3_dram[:, :],
                                            in_offset=bass.IndirectOffsetOnAxis(ap=idx4[:, slot, r:r + 1], axis=0)).then_inc(xg_loaded[slot], 16)

            for s in range(RING):
                gather(0, s)
            with pool.Fori(1, ITERS) as it:
                for s in range(RING):
                    gather(it, s)

        @block.scalar
        def _(act):
            def evac_T(n, j, dst_t):
                act.wait_ge(xT_done, n + 1)
                act.copy(dst_t[:, :, P * j:P * j + rows(j)],
                         ps[:, n % 2, :].rearrange("p (c n) -> p c n", c=KC)[:, :, 0:rows(j)]).then_inc(xT_evac, 1)

            for j in range(NT):
                evac_T(j, j, xT0)
            for j in range(NT):
                act.wait_ge(u_done, j + 1)
                if j >= 2:
                    act.wait_ge(u_ready, j - 1)
                act.copy(u_f[0:rows(j), j % 2, :], ps[0:rows(j), 2 + j % 2, :])
                act.copy(u_hi[0:rows(j), j, :], ps[0:rows(j), 2 + j % 2, :]).then_inc(u_evac, 1)

            def evac_agg(layer, nc_, emit):
                act.sem_inc(agg_evac[layer], nc_)
                with act.Fori(0, NCH) as i:
                    for cc in range(nc_):
                        act.wait_ge(agg_done[layer], i * nc_ + cc + 1)
                        emit(cc, bass.ds(i * CS, CH)).then_inc(agg_evac[layer], 1)

            act.wait_ge(cols_loaded, 80)
            evac_agg(0, KC, lambda cc, n: act.activation(h1T0[:, cc, n], ps[:, cc, 0:CH], ACT.Relu, bias=cols[:, 0, cc:cc + 1]))

            def sqrt_var(n):
                act.wait_ge(ln_step, 2 * n + 2)
                act.activation(std[:, n % 2:n % 2 + 1], mv[:, n % 2, 1:2], ACT.Sqrt, bias=eps_s[:, 0:1]).then_inc(std_ready, 1)

            def norm_and_turn(cT):
                for j in range(NT):
                    for q in range(3):
                        t = 3 * j + q
                        act.wait_ge(t_done, t + 1)
                        n0, n1 = 4 * P * q, min(4 * P * (q + 1), N)
                        act.copy(cT[0:rows(j), j, n0:n1], ps[0:rows(j), t % 4, 0:n1 - n0]).then_inc(t_evac, 1)
                    sqrt_var(j)

            irregular = act.value_load(flag_i[0:1, 0:1], min_val=0, max_val=1)
            with act.If(irregular > 0):
                norm_and_turn(countsT_x)
            with act.Else():
                norm_and_turn(countsT)
            def relu_g(j):
                act.wait_ge(g_read, j + 1)
                act.activation(g_hi[0:rows(j), j, :], g_f[0:rows(j), j % 4, :], ACT.Relu)
                act.activation(g_f[0:rows(j), j % 4, :], g_f[0:rows(j), j % 4, :], ACT.Relu).then_inc(g_relu, 1)

            for j in range(NT):
                evac_T(NT + j, j, x1T)
                if j >= 1:
                    relu_g(j - 1)
            relu_g(NT - 1)
            act.wait_ge(deg_step, 2)
            act.activation(degt[:, 1, :], degt[:, 0, :], ACT.Sqrt).then_inc(deg_sq, 1)
            evac_agg(1, DH // P, lambda cc, n: act.copy(z1T[:, cc, n], ps[:, cc, 0:CH]))
            act.wait_ge(deg_step, 5)
            act.activation(degt[:, 3, :], degt[:, 2, :], ACT.Sqrt).then_inc(deg_sq, 1)
            def scale_x(j):
                act.wait_ge(x_ready, NT + j + 1)
                if j >= 2:
                    act.wait_ge(xs_ready, j - 1)
                if j == 0:
                    act.wait_ge(deg_ready, 1)
                act.activation(xs_f[0:rows(j), j % 2, :], xn[0:rows(j), j, :], ACT.Copy, scale=deg[0:rows(j), 1, j:j + 1])
                act.activation(xs_hi[0:rows(j), j, :], xn[0:rows(j), j, :], ACT.Copy, scale=deg[0:rows(j), 1, j:j + 1]).then_inc(xs_done, 1)

            for j in range(NT):
                sqrt_var(NT + j)
                if j >= 2:
                    scale_x(j - 2)
            scale_x(NT - 2)
            scale_x(NT - 1)
            evac_agg(2, KC, lambda cc, n: act.copy(z2T[:, cc, n], ps[:, cc, 0:CH]))
            for j in range(NT):
                sqrt_var(2 * NT + j)
                if j >= TLAG + 1:
                    evac_T(2 * NT + j - TLAG - 1, j - TLAG - 1, x3T)
            for j in range(NT - TLAG - 1, NT):
                evac_T(2 * NT + j, j, x3T)
            act.wait_ge(y_done, 3 * NT)
            act.wait_ge(xT_evac, 3 * NT)
            act.copy(hT[:, :, :], x3T[:, :, :]).then_inc(x3_copied, 1)

            def evac_pre(n):
                cc, (n0, n1) = n // NCH, CUTS[n % NCH]
                act.wait_ge(pre_done, n + 1)
                act.activation(preT[:, cc, n0:n1], ps[:, n % 4, 0:n1 - n0], ACT.Identity,
                               bias=cols[:, 1, cc:cc + 1]).then_inc(pre_evac, 1)

            def rectify(it, s):
                g = RING * it + s
                act.wait_ge(add_done, g + 1)
                act.activation(ea[:, s, :, :], ea[:, s, :, :], ACT.Relu).then_inc(relu_done, 1)

            def evac_z(it, s):
                g, join = RING * it + s, s // JOIN
                act.wait_ge(scat_done, g + 1)
                if not (isinstance(it, int) and it == 0):
                    act.wait_ge(join_done, JOINS * (it - 1) + join + 1)
                act.copy(zg[:, join, :, s % JOIN, :], ps[:, 4 + s % 2, 0:KC * W].rearrange("p (c w) -> p c w", c=KC)).then_inc(zg_ready, 1)

            for n in range(PRE_LEAD):
                evac_pre(n)
            for s in range(RING):
                rectify(0, s)
                if s:
                    for n in pre_after(s - 1):
                        evac_pre(n)
                    evac_z(0, s - 1)
            with act.Fori(1, ITERS) as it:
                for s in range(RING):
                    rectify(it, s)
                    if s:
                        evac_z(it, s - 1)
                    else:
                        evac_z(it - 1, RING - 1)
            evac_z(ITERS - 1, RING - 1)
            for cc in range(KC):
                act.wait_ge(pre_added, NG)
                act.activation(preT[:, cc, :], preT[:, cc, :], ACT.Relu).then_inc(h1_ready, 1)
            for cc in range(KC):
                act.wait_ge(bn_step, 2 * cc + 2)
                act.activation(bn_t[:, 0, cc:cc + 1], bn_mv[:, cc, 1:2], ACT.Sqrt, bias=eps_s[:, 0:1]).then_inc(bn_sq, 1)
                act.wait_ge(bn_ready, cc + 1)
                act.activation(hT[:, cc, :], hT[:, cc, :], ACT.Identity, bias=bn_t[:, 3, cc:cc + 1],
                               scale=bn_t[:, 2, cc:cc + 1]).then_inc(hn_ready, 1)
            for j in range(NT):
                sqrt_var(3 * NT + j)

        @block.vector
        def _(dve):
            steps = [0]

            def step(ins):
                steps[0] += 1
                ins.then_inc(prep, 1)
                dve.wait_ge(prep, steps[0])

            dve.memset(row["dst_i"][:, :], -1).then_inc(row_pad, 1)
            dve.memset(row["src_i"][:, :], 0).then_inc(row_pad, 1)
            dve.wait_ge(rows_loaded, 64)
            r = {n: t[:, :] for n, t in row.items()}
            dve.tensor_copy(r["dst"], r["dst_i"])
            dve.tensor_copy(r["src"], r["src_i"])
            dve.tensor_scalar(r["lo_i"], r["src_i"], P - 1, None, ALU.bitwise_and)
            step(dve.tensor_scalar(r["hi_i"], r["src_i"], P.bit_length() - 1, None, ALU.logical_shift_right))
            dve.tensor_copy(r["lo"], r["lo_i"])
            dve.tensor_copy(r["hi"], r["hi_i"])
            step(dve.tensor_scalar(base_row[:, :], row["dst"][:, 0:1].to_broadcast([NG, P]), float(N - W), 0.0, ALU.min, ALU.max))
            step(dve.tensor_scalar(r["rel"], r["dst"], base_row[:, 0:1], None, ALU.subtract))
            step(dve.tensor_scalar(r["left"], r["rel"], float(W), None, ALU.is_lt))
            step(dve.scalar_tensor_tensor(out=r["valid"], in0=r["rel"], scalar=0.0, in1=r["left"], op0=ALU.is_ge, op1=ALU.mult))
            step(dve.scalar_tensor_tensor(out=r["code"], in0=r["hi"], scalar=float(W), in1=r["rel"], op0=ALU.mult, op1=ALU.add))
            step(dve.scalar_tensor_tensor(out=r["code"], in0=r["code"], scalar=1.0, in1=r["valid"], op0=ALU.add, op1=ALU.mult))
            dve.tensor_scalar(r["code"], r["code"], -1.0, None, ALU.add)
            step(dve.scalar_tensor_tensor(out=r["relw"], in0=r["rel"], scalar=1.0, in1=r["valid"], op0=ALU.add, op1=ALU.mult))
            dve.tensor_scalar(r["relw"], r["relw"], -1.0, None, ALU.add)
            step(dve.tensor_scalar(r["rel"], r["valid"], -1.0, 1.0, ALU.mult, ALU.add))
            step(dve.scalar_tensor_tensor(out=r["left"], in0=r["dst"], scalar=1.0, in1=r["rel"], op0=ALU.add, op1=ALU.mult))
            step(dve.tensor_scalar(r["left"], r["left"], -1.0, None, ALU.add))
            step(dve.tensor_reduce(left_max[:, :], r["left"], AX.X, ALU.max))
            dve.tensor_copy(left_row[:, :], left_max[:, :].to_broadcast([NG, P])).then_inc(rows_ready, 1)

            dve.wait_ge(idx_done, 1)
            def turned(bank, k):
                return ps[:, bank, k * NG * TPG:(k + 1) * NG * TPG].rearrange("p (r g) -> p g r", r=TPG)
            dve.tensor_copy(codeT[:, :, :], turned(4, 0))
            dve.tensor_copy(src_loT[:, :, :], turned(4, 1))
            dve.tensor_copy(relwT[:, :, :], turned(4, 2))
            dve.tensor_copy(leftT[:, :, :], turned(5, 0))
            dve.tensor_copy(srcT[:, :, :], turned(5, 1))
            dve.tensor_copy(dstT[:, :, :], turned(3, 0))
            dve.tensor_copy(srcT_i[:, :, :], turned(5, 1))
            off = 2 * NG * TPG
            dve.tensor_copy(base_i[:, :], ps[0:1, 5, off:off + NG])
            step(dve.tensor_copy(base_f[:, :], ps[0:1, 5, off:off + NG]))
            dve.tensor_reduce(flag4[:, 0:1], ps[0:1, 5, off + NG:off + 2 * NG], AX.X, ALU.max)
            step(dve.tensor_tensor(gap[:, 0:NG - 1], base_f[:, 1:NG], base_f[:, 0:NG - 1], ALU.subtract))
            step(dve.tensor_reduce(flag4[:, 1:2], gap[:, 0:NG - 1], AX.X, ALU.min))
            step(dve.tensor_tensor(gap[:, 0:NG - BLOCK_SPAN], base_f[:, BLOCK_SPAN:NG], base_f[:, 0:NG - BLOCK_SPAN], ALU.subtract))
            step(dve.tensor_reduce(flag4[:, 2:3], gap[:, 0:NG - BLOCK_SPAN], AX.X, ALU.min))
            step(dve.tensor_scalar(flag4[:, 0:1], flag4[:, 0:1], 0.0, None, ALU.is_ge))
            step(dve.tensor_scalar(flag4[:, 1:2], flag4[:, 1:2], 0.0, None, ALU.is_lt))
            step(dve.tensor_scalar(flag4[:, 2:3], flag4[:, 2:3], float(W), None, ALU.is_lt))
            step(dve.tensor_reduce(flag4[:, 3:4], flag4[:, 0:3], AX.X, ALU.max))
            dve.tensor_copy(flag_i[:, :], flag4[:, 3:4]).then_inc(idx_ready, 1)

            dve.wait_ge(consts, 4)
            dve.wait_ge(counts_zero, 1)
            dve.wait_ge(idx_ready, 1)

            def code_hots(g, slot):
                if not (isinstance(g, int) and g < HOTS):
                    dve.wait_ge(cnt_done, g - HOTS + 1)
                for r in range(TPG):
                    ins = dve.tensor_scalar(hot_code[:, slot, r, :], iota_n[:, 0:NCODE],
                                            codeT[:, bass.ds(g, 1), r:r + 1].rearrange("p a b -> p (a b)"), None, ALU.is_equal)
                for r in range(POOL_HOTS, TPG):
                    ins = dve.tensor_scalar(hot_lo[:, slot, r, :], iota_n[:, 0:P],
                                            src_loT[:, bass.ds(g, 1), r:r + 1].rearrange("p a b -> p (a b)"), None, ALU.is_equal)
                ins.then_inc(hot_ready, 1)

            def add_counts(g, slot):
                base = dve.value_load(base_i[0:1, bass.ds(g, 1)], min_val=0, max_val=N - W)
                dve.wait_ge(cnt_done, g + 1)
                if not (isinstance(g, int) and g == 0):
                    dve.wait_ge(cnt_added, g)
                win = counts[:, :, bass.ds(base, W)]
                dve.tensor_tensor(win, ps[:, 4 + slot, 0:NCODE].rearrange("p (h w) -> p h w", h=NT), f32(win), ALU.add).then_inc(cnt_added, 1)

            def count_round(i):
                for k in range(HOTS):
                    code_hots(HOTS * i + k + 2, (k + 2) % HOTS)
                    add_counts(HOTS * i + k, k)

            code_hots(0, 0)
            code_hots(1, 1)
            count_round(0)
            with dve.Fori(1, NT) as i:
                count_round(i)
            add_counts(NG - 2, (NG - 2) % HOTS)
            add_counts(NG - 1, (NG - 1) % HOTS)
            dve.wait_ge(cnt_added, NG)

            def diagonal(c, op, done):
                main = c[:, :, :].rearrange("p j n -> p (j n)")[:, 0:(NT - 1) * (N + P)] \
                    .rearrange("p (j r) -> p j r", r=N + P)[:, :, 0:P]
                tail = c[:, NT - 1, (NT - 1) * P:N]
                dve.tensor_tensor(main, f32(main), ident[:, :].unsqueeze(1).to_broadcast([P, NT - 1, P]), op).then_inc(done, 1)
                dve.tensor_tensor(tail, f32(tail), ident[:, 0:TAIL], op).then_inc(done, 1)

            def out_degrees(c):
                diagonal(c, ALU.add, diag_added)
                dve.wait_ge(diag_added, 2)
                dve.tensor_reduce(deg[:, 0, :], f32(c[:, :, :]), AX.X, ALU.add).then_inc(deg_step, 1)

            def in_degrees(c, cT):
                dve.tensor_reduce(deg[:, 2, 0:NT - 1], f32(cT[:, 0:NT - 1, :]), AX.X, ALU.add).then_inc(deg_step, 1)
                dve.tensor_reduce(deg[0:TAIL, 2, NT - 1:NT], f32(cT[0:TAIL, NT - 1, :]), AX.X, ALU.add).then_inc(deg_step, 1)
                diagonal(c, ALU.subtract, diag_taken)

            dve.memset(deg[:, :, :], 1.0)
            dve.memset(degt[:, :, :], 1.0).then_inc(deg_set, 1)
            dve.wait_ge(deg_set, 1)
            irregular = dve.value_load(flag_i[0:1, 0:1], min_val=0, max_val=1)
            with dve.If(irregular > 0):
                dve.memset(counts_x[:, :, :], 0.0).then_inc(counts_zero, 1)
                dve.wait_ge(counts_zero, 2)
                with dve.Fori(0, NG) as g:
                    for rr in range(TPG):
                        dve.tensor_scalar(fixc_dst[:, :], iota_n[:, :],
                                          dstT[:, bass.ds(g, 1), rr:rr + 1].rearrange("p a b -> p (a b)"), None, ALU.is_equal)
                        for h in range(NT):
                            n = (g * TPG + rr) * NT + h
                            dve.tensor_scalar(fixc_src[:, 0:rows(h)], iota_n[:, P * h:P * h + rows(h)],
                                              srcT[:, bass.ds(g, 1), rr:rr + 1].rearrange("p a b -> p (a b)"), None,
                                              ALU.is_equal).then_inc(fixc_hot, 1)
                            dve.wait_ge(fixc_done, n + 1)
                            for q, (n0, n1) in enumerate(CUTS):
                                ins = dve.tensor_tensor(counts_x[0:rows(h), h, n0:n1], ps[0:rows(h), 4 + q, 0:n1 - n0],
                                                        counts_x[0:rows(h), h, n0:n1], ALU.add)
                            ins.then_inc(fixc_added, 1)
                            dve.wait_ge(fixc_added, n + 2)
                out_degrees(counts_x)
            with dve.Else():
                out_degrees(counts)
            dve.wait_ge(deg_step, 1)
            dve.tensor_scalar(degt[:, 0, :], deg[:, 0, :], -1.0, 1.0, ALU.add, ALU.max).then_inc(deg_step, 1)

            def ln_begin(n, j, y_sum):
                dve.wait_ge(y_done, n + 1)
                y_sum(xn[0:rows(j), j, :], ps[0:rows(j), 4 + n % 2, :]).then_inc(y_read, 1)
                dve.wait_ge(y_read, n + 1)
                dve.bn_stats(stats[0:rows(j), n % 2, :], xn[0:rows(j), j, :]).then_inc(ln_step, 1)
                dve.wait_ge(ln_step, 2 * n + 1)
                dve.bn_aggr(mv[0:P if j < NT - 1 else TAIL, n % 2, :], stats[0:rows(j), n % 2, :]).then_inc(ln_step, 1)

            def ln_finish(n, j):
                dve.wait_ge(std_ready, n + 1)
                dve.reciprocal(rstd[0:rows(j), n % 2:n % 2 + 1], std[0:rows(j), n % 2:n % 2 + 1]).then_inc(rstd_ready, 1)
                dve.wait_ge(rstd_ready, n + 1)
                dve.tensor_scalar(xn[0:rows(j), j, :], xn[0:rows(j), j, :], mv[0:rows(j), n % 2, 0:1], rstd[0:rows(j), n % 2:n % 2 + 1],
                                  ALU.subtract, ALU.mult).then_inc(x_ready, 1)

            def layer_norm(layer, before, y_sum):
                for j in range(NT):
                    before(j)
                    ln_begin(NT * layer + j, j, y_sum(j))
                    if j:
                        ln_finish(NT * layer + j - 1, j - 1)
                ln_finish(NT * layer + NT - 1, NT - 1)

            def plus_x(j):
                return lambda xr, y: dve.tensor_tensor(xr, y, xr, ALU.add)

            layer_norm(0, lambda j: dve.wait_ge(xb_ready[0], j + 1), plus_x)

            for j in range(NT):
                dve.wait_ge(g_done, j + 1)
                if j >= 4:
                    dve.wait_ge(g_ready, j - 3)
                dve.tensor_tensor(g_f[0:rows(j), j % 4, :], ps[0:rows(j), 2 + j % 2, 0:DH], b11_b[0:rows(j), :], ALU.add).then_inc(g_read, 1)
                dve.wait_ge(xT_done, NT + j + 1)
                dve.scalar_tensor_tensor(out=xn[0:rows(j), j, :], in0=b12_b[0:rows(j), :], scalar=deg[0:rows(j), 0, j:j + 1],
                                         in1=xn[0:rows(j), j, :], op0=ALU.mult, op1=ALU.add).then_inc(xb_ready[1], 1)
            dve.wait_ge(deg_sq, 1)
            dve.reciprocal(deg[:, 1, :], degt[:, 1, :]).then_inc(deg_ready, 1)
            dve.wait_ge(t_evac, 3 * NT)
            irregular = dve.value_load(flag_i[0:1, 0:1], min_val=0, max_val=1)
            with dve.If(irregular > 0):
                in_degrees(counts_x, countsT_x)
            with dve.Else():
                in_degrees(counts, countsT)
            dve.wait_ge(deg_step, 4)
            dve.tensor_scalar(degt[:, 2, :], deg[:, 2, :], -1.0, 1.0, ALU.add, ALU.max).then_inc(deg_step, 1)
            dve.wait_ge(deg_sq, 2)
            dve.reciprocal(deg[:, 3, :], degt[:, 3, :]).then_inc(deg_ready, 1)
            layer_norm(1, lambda j: dve.wait_ge(xb_ready[1], j + 1), plus_x)

            dve.wait_ge(deg_ready, 2)
            layer_norm(2, lambda j: dve.wait_ge(xb_ready[2], j + 1),
                       lambda j: lambda xr, y: dve.scalar_tensor_tensor(out=xr, in0=y, scalar=deg[0:rows(j), 3, j:j + 1], in1=xr,
                                                                        op0=ALU.mult, op1=ALU.add))

            dve.wait_ge(x3_copied, 1)
            irregular = dve.value_load(flag_i[0:1, 0:1], min_val=0, max_val=1)
            with dve.If(irregular > 0):
                with dve.Fori(0, NG) as g:
                    for rr in range(TPG):
                        n = g * TPG + rr
                        if rr == 0:
                            dve.wait_ge(fix_x, g * (16 * TPG) + 16)
                            dve.wait_ge(fix_e, g * (16 * TPG) + 16)
                        else:
                            dve.wait_ge(fix_x, g * (16 * TPG) + 16 * (rr + 1))
                            dve.wait_ge(fix_e, g * (16 * TPG) + 16 * (rr + 1))
                        dve.tensor_tensor(xg[:, 0, 0, :], xg[:, 0, 0, :], xg[:, 1, 0, :], ALU.add).then_inc(fix_msg, 1)
                        dve.wait_ge(fix_msg, n * 2 + 1)
                        dve.tensor_scalar(xg[:, 0, 0, :], xg[:, 0, 0, :], 0.0, None, ALU.max)
                        dve.tensor_scalar(fix_hot[:, :], iota_n[:, :],
                                          leftT[:, bass.ds(g, 1), rr:rr + 1].rearrange("p a b -> p (a b)"), None,
                                          ALU.is_equal).then_inc(fix_msg, 1)
                        for cc in range(KC):
                            dve.wait_ge(fix_done, n * KC + cc + 1)
                            for q, (n0, n1) in enumerate(CUTS):
                                ins = dve.tensor_tensor(x3T[:, cc, n0:n1], ps[:, q, 0:n1 - n0], x3T[:, cc, n0:n1], ALU.add)
                            ins.then_inc(fix_added, 1)
                            dve.wait_ge(fix_added, n * KC + cc + 2)

            def add_rows(it, s):
                g, slot = RING * it + s, s % XRING
                dve.wait_ge(xg_loaded[slot], it * (16 * TPG * RING // XRING) + 16 * TPG * (s // XRING + 1))
                dve.wait_ge(ea_loaded[s], it * 16 + 16 * (1 + (isinstance(it, int) and g == NG - 1 and LAST_R > 0)))
                dve.tensor_tensor(ea[:, s, :, :], ea[:, s, :, :], xg[:, slot, :, :], ALU.add).then_inc(add_done, 1)
                if not (isinstance(it, int) and it == 0):
                    dve.wait_ge(scat_done, g - RING + 1)
                dve.tensor_tensor(hot_w[:, s, :, :], iota_n[:, 0:W].unsqueeze(1).to_broadcast([P, TPG, W]),
                                  relwT[:, bass.ds(g, 1), :].rearrange("p a r -> p (a r)").unsqueeze(2).to_broadcast([P, TPG, W]),
                                  ALU.is_equal).then_inc(win_ready, 1)

            def add_join(m, slot):
                bases = [dve.value_load(base_i[0:1, bass.ds(JOIN * m + h, 1)], min_val=0, max_val=N - W) for h in range(JOIN)]
                if isinstance(m, int) and m == 0:
                    dve.wait_ge(pre_evac, KC * NCH)
                dve.wait_ge(join_done, m + 1)
                for h in range(JOIN):
                    if not (isinstance(m, int) and m == 0 and h == 0):
                        dve.wait_ge(pre_added, JOIN * m + h)
                    win = preT[:, :, bass.ds(bases[h], W)].rearrange("p (b f) w -> p b f w", b=2)
                    dve.tensor_tensor(win, win, join_bank(slot)[:, :, :, h, :], ALU.add).then_inc(pre_added, 1)

            def stream(it):
                for s in range(RING):
                    add_rows(it, s)
                    if s % JOIN == 0 and not (isinstance(it, int) and it == 0):
                        add_join(JOINS * it + s // JOIN - 2, s // JOIN)

            stream(0)
            with dve.Fori(1, ITERS - 1) as it:
                stream(it)
            stream(ITERS - 1)
            for m in range(NG // JOIN - 2, NG // JOIN):
                add_join(m, m % JOINS)

            def bn_finish(cc):
                dve.wait_ge(bn_sq, cc + 1)
                one = slice(cc, cc + 1)
                chain = [dve.reciprocal(bn_t[:, 1, one], bn_t[:, 0, one]).then_inc(bn_calc, 1)]
                dve.wait_ge(bn_calc, 3 * cc + 1)
                dve.tensor_tensor(bn_t[:, 2, one], bn_t[:, 1, one], cols[:, 3, one], ALU.mult).then_inc(bn_calc, 1)
                dve.wait_ge(bn_calc, 3 * cc + 2)
                dve.tensor_tensor(bn_t[:, 1, one], bn_mv[:, cc, 0:1], bn_t[:, 2, one], ALU.mult).then_inc(bn_calc, 1)
                dve.wait_ge(bn_calc, 3 * cc + 3)
                dve.tensor_tensor(bn_t[:, 3, one], cols[:, 4, one], bn_t[:, 1, one], ALU.subtract).then_inc(bn_ready, 1)

            for cc in range(KC):
                for q, (n0, n1) in enumerate(CUTS):
                    n = cc * NCH + q
                    dve.wait_ge(w32_done, n + 1)
                    dve.scalar_tensor_tensor(out=hT[:, cc, n0:n1], in0=ps[:, n % 4, 0:n1 - n0], scalar=cols[:, 2, cc:cc + 1],
                                             in1=hT[:, cc, n0:n1], op0=ALU.add, op1=ALU.add).then_inc(h2_ready, 1)
                    dve.wait_ge(h2_ready, n + 1)
                    ins = dve.bn_stats(bn_st[:, cc, q, :], hT[:, cc, n0:n1])
                ins.then_inc(bn_step, 1)
                dve.wait_ge(bn_step, 2 * cc + 1)
                dve.bn_aggr(bn_mv[:, cc, :], bn_st[:, cc, :, :].rearrange("p q s -> p (q s)")).then_inc(bn_step, 1)
                if cc:
                    bn_finish(cc - 1)
            bn_finish(KC - 1)
            layer_norm(3, lambda j: None, plus_x)

        @block.tensor
        def _(pe):
            def transpose_x(n, j, src_t, ready):
                ready(j)
                if n >= 2:
                    pe.wait_ge(xT_evac, n - 1)
                for cc in range(KC):
                    ins = pe.transpose(ps[:, n % 2, P * cc:P * cc + rows(j)], src_t[0:rows(j), j, P * cc:P * cc + P],
                                       ident[0:rows(j), 0:rows(j)])
                ins.then_inc(xT_done, 1)

            pe.wait_ge(consts, 2)
            for j in range(NT):
                transpose_x(j, j, xn, lambda j: pe.wait_ge(x_loaded[j // 3], 16))

            pe.wait_ge(rows_ready, 1)
            for bank, names in ((4, ("code", "lo", "relw")), (3, ("dst",)), (5, ("left", "src"))):
                for k, name in enumerate(names):
                    for r in range(TPG):
                        pe.transpose(ps[:, bank, (k * TPG + r) * NG:(k * TPG + r + 1) * NG], row[name][:, r:GE:TPG], ident[0:NG, 0:NG])
            off = 2 * NG * TPG
            pe.transpose(ps[:, 5, off:off + NG], base_row[:, :], ident[0:NG, 0:NG])
            pe.transpose(ps[:, 5, off + NG:off + 2 * NG], left_row[:, :], ident[0:NG, 0:NG]).then_inc(idx_done, 1)

            def count_group(g):
                slot = g % HOTS
                pe.wait_ge(hot_ready, g + 1)
                pe.wait_ge(lo_ready, g + 1)
                if g >= HOTS:
                    pe.wait_ge(cnt_added, g - HOTS + 1)
                for r in range(TPG):
                    ins = pe.matmul(ps[:, 4 + slot, 0:NCODE], hot_lo[:, slot, r, :], hot_code[:, slot, r, :],
                                    start=(r == 0), stop=(r == TPG - 1))
                ins.then_inc(cnt_done, 1)

            count_group(0)
            count_group(1)
            pe.wait_ge(w01_loaded, 16)
            for j in range(NT):
                pe.wait_ge(xT_evac, j + 1)
                if j >= 2:
                    pe.wait_ge(u_evac, j - 1)
                for k in range(KC):
                    count_group(HOTS * j + k + 2)
                    ins = pe.matmul(ps[0:rows(j), 2 + j % 2, :], xT0[:, k, P * j:P * j + rows(j)], w01_s[:, k, :],
                                    start=(k == 0), stop=(k == KC - 1))
                ins.then_inc(u_done, 1)

            irregular = pe.value_load(flag_i[0:1, 0:1], min_val=0, max_val=1)
            with pe.If(irregular > 0):
                pe.sem_inc(fixc_added, 1)
                with pe.Fori(0, NG) as g:
                    for r in range(TPG):
                        for h in range(NT):
                            n = (g * TPG + r) * NT + h
                            pe.wait_ge(fixc_hot, n + 1)
                            pe.wait_ge(fixc_added, n + 1)
                            for q, (n0, n1) in enumerate(CUTS):
                                ins = pe.matmul(ps[0:rows(h), 4 + q, 0:n1 - n0], fixc_src[:, 0:rows(h)], fixc_dst[:, n0:n1],
                                                start=True, stop=True)
                            ins.then_inc(fixc_done, 1)

            def aggregate(layer, blocks, high, low, adj_r, adj, ready):
                def job(parts, rhs, cc, n):
                    pairs = [(part, j) for j in range(NT) for part in parts]
                    for m, (part, j) in enumerate(pairs):
                        if cc == 0 and part is parts[0]:
                            pe.wait_ge(ready, j + 1)
                        ins = pe.matmul(ps[:, cc, 0:CH], part[0:rows(j), j, P * cc:P * cc + P], rhs[0:rows(j), j, n],
                                        start=(m == 0), stop=(m == len(pairs) - 1))
                    ins.then_inc(agg_done[layer], 1)

                def chunks(parts, rhs):
                    with pe.Fori(0, NCH) as i:
                        for cc in range(blocks):
                            pe.wait_ge(agg_evac[layer], i * blocks + cc + 1)
                            job(parts, rhs, cc, bass.ds(i * CS, CH))

                irregular = pe.value_load(flag_i[0:1, 0:1], min_val=0, max_val=1)
                with pe.If(irregular > 0):
                    chunks([high[:, :, :].bitcast(F32), low[:, :, :].bitcast(F32)], adj)
                with pe.Else():
                    chunks([high, low], adj_r)

            def project(act_t, kc, w, j, n):
                if n >= 2:
                    pe.wait_ge(y_read, n - 1)
                for k in range(kc):
                    ins = pe.matmul(ps[0:rows(j), 4 + n % 2, :], act_t[:, k, P * j:P * j + rows(j)], w[:, k, :],
                                    start=(k == 0), stop=(k == kc - 1))
                ins.then_inc(y_done, 1)

            pe.wait_ge(diag_added, 2)
            aggregate(0, KC, u_hi, u_lo, counts, counts_x, u_ready)
            pe.wait_ge(w02_loaded, 16)
            pe.wait_ge(agg_evac[0], KC * NCH + KC)

            def project_and_turn(c):
                for j in range(NT):
                    project(h1T0, KC, w02_s, j, j)
                    for q in range(3):
                        t = 3 * j + q
                        if t >= 4:
                            pe.wait_ge(t_evac, t - 3)
                        for i in range(4 * q, min(4 * q + 4, NT)):
                            ins = pe.transpose(ps[0:rows(j), t % 4, P * (i - 4 * q):P * (i - 4 * q) + rows(i)],
                                               f32(c[0:rows(i), i, P * j:P * j + rows(j)]), ident[0:rows(i), 0:rows(i)])
                        ins.then_inc(t_done, 1)

            irregular = pe.value_load(flag_i[0:1, 0:1], min_val=0, max_val=1)
            with pe.If(irregular > 0):
                project_and_turn(counts_x)
            with pe.Else():
                project_and_turn(counts)

            pe.wait_ge(t_evac, 3 * NT)
            pe.wait_ge(w1_loaded, 32)

            def hidden(j):
                pe.wait_ge(xT_evac, NT + j + 1)
                if j >= 2:
                    pe.wait_ge(g_read, j - 1)
                for k in range(KC):
                    ins = pe.matmul(ps[0:rows(j), 2 + j % 2, 0:DH], x1T[:, k, P * j:P * j + rows(j)], w11_s[:, k, :],
                                    start=(k == 0), stop=(k == KC - 1))
                ins.then_inc(g_done, 1)

            for j in range(NT):
                transpose_x(NT + j, j, xn, lambda j: pe.wait_ge(x_ready, j + 1))
                if j:
                    hidden(j - 1)
            hidden(NT - 1)
            aggregate(1, DH // P, g_hi, g_lo, countsT, countsT_x, g_ready)
            pe.wait_ge(agg_evac[1], (DH // P) * (NCH + 1))
            for j in range(NT):
                project(z1T, DH // P, w12_s, j, NT + j)

            pe.wait_ge(diag_taken, 2)
            aggregate(2, KC, xs_hi, xs_lo, counts, counts_x, xs_ready)
            pe.wait_ge(w2_loaded, 16)
            pe.wait_ge(agg_evac[2], KC * (NCH + 1))
            for j in range(NT):
                project(z2T, KC, w2_s, j, 2 * NT + j)
                if j >= TLAG:
                    transpose_x(2 * NT + j - TLAG, j - TLAG, xn, lambda j: pe.wait_ge(x_ready, 2 * NT + j + 1))

            for j in range(NT - TLAG, NT):
                transpose_x(2 * NT + j, j, xn, lambda j: pe.wait_ge(x_ready, 2 * NT + j + 1))
            irregular = pe.value_load(flag_i[0:1, 0:1], min_val=0, max_val=1)
            with pe.If(irregular > 0):
                pe.wait_ge(xT_evac, 3 * NT)
                pe.sem_inc(fix_added, 1)
                with pe.Fori(0, NG) as g:
                    for r in range(TPG):
                        n = g * TPG + r
                        pe.wait_ge(fix_msg, n * 2 + 2)
                        for cc in range(KC):
                            pe.wait_ge(fix_added, n * KC + cc + 1)
                            for q, (n0, n1) in enumerate(CUTS):
                                ins = pe.matmul(ps[:, q, 0:n1 - n0], xg[:, 0, 0, P * cc:P * cc + P], fix_hot[:, n0:n1],
                                                start=True, stop=True)
                            ins.then_inc(fix_done, 1)
                pe.wait_ge(fix_added, NG * TPG * KC + 1)
            pe.wait_ge(xT_evac, 3 * NT)
            pe.wait_ge(w3_loaded, 32)

            def pre_job(n):
                cc, (n0, n1) = n // NCH, CUTS[n % NCH]
                if n >= 4:
                    pe.wait_ge(pre_evac, n - 3)
                for k in range(KC):
                    ins = pe.matmul(ps[:, n % 4, 0:n1 - n0], w31_s[:, k, P * cc:P * cc + P], x3T[:, k, n0:n1],
                                    start=(k == 0), stop=(k == KC - 1))
                ins.then_inc(pre_done, 1)

            def scatter(it, s):
                g = RING * it + s
                pe.wait_ge(relu_done, g + 1)
                pe.wait_ge(win_ready, g + 1)
                if not (isinstance(g, int) and g < 2):
                    pe.wait_ge(zg_ready, g - 1)
                for r in range(TPG):
                    for cc in range(KC):
                        ins = pe.matmul(ps[:, 4 + s % 2, cc * W:cc * W + W], ea[:, s, r, P * cc:P * cc + P], hot_w[:, s, r, :],
                                        start=(r == 0 and cc == 0), stop=(r == TPG - 1 and cc == KC - 1))
                ins.then_inc(scat_done, 1)

            def join(m, slot):
                pe.wait_ge(zg_ready, JOIN * m + JOIN)
                if not (isinstance(m, int) and m < JOINS):
                    pe.wait_ge(pre_added, JOIN * (m - JOINS) + JOIN)
                for f in range(KC):
                    for k in range(KC):
                        ins = pe.matmul(join_bank(slot)[:, f // 2, f % 2, :, :].rearrange("p h w -> p (h w)"),
                                        w31_s[:, k, P * f:P * f + P], zg[:, slot, k, :, :].rearrange("p h w -> p (h w)"),
                                        start=(f % 2 == 0 and k == 0), stop=(f % 2 == 1 and k == KC - 1))
                ins.then_inc(join_done, 1)

            for n in range(PRE_LEAD):
                pre_job(n)
            for s in range(RING):
                scatter(0, s)
                for n in pre_after(s):
                    pre_job(n)
                if s == JOIN + 1:
                    pe.wait_ge(pre_evac, KC * NCH)
                    join(0, 0)
            with pe.Fori(1, ITERS) as it:
                for s in range(RING):
                    scatter(it, s)
                    if s % JOIN == 0:
                        join(JOINS * it + s // JOIN - 1, (s // JOIN - 1) % JOINS)
            join(NG // JOIN - 1, JOINS - 1)

            pe.wait_ge(h1_ready, KC)
            for cc in range(KC):
                for q, (n0, n1) in enumerate(CUTS):
                    n = cc * NCH + q
                    if n >= 4:
                        pe.wait_ge(h2_ready, n - 3)
                    for k in range(KC):
                        ins = pe.matmul(ps[:, n % 4, 0:n1 - n0], w32_s[:, k, P * cc:P * cc + P], preT[:, k, n0:n1],
                                        start=(k == 0), stop=(k == KC - 1))
                    ins.then_inc(w32_done, 1)
            pe.wait_ge(hn_ready, KC)
            for j in range(NT):
                n = 3 * NT + j
                pe.wait_ge(y_read, n - 1)
                for cc in range(KC):
                    ins = pe.transpose(ps[0:rows(j), 4 + n % 2, P * cc:P * cc + P], hT[:, cc, P * j:P * j + rows(j)], ident[:, :])
                ins.then_inc(y_done, 1)


_INS = ['x', 'src', 'dst', 'edge_attr_512', 'L0_gnn_W1', 'L0_gnn_b1', 'L0_gnn_W2', 'L0_gnn_b2', 'L1_gnn_W1', 'L1_gnn_b1',
        'L1_gnn_W2', 'L1_gnn_b2', 'L2_gnn_W', 'L2_gnn_b', 'L3_gnn_W1', 'L3_gnn_b1', 'L3_gnn_W2', 'L3_gnn_b2',
        'L3_gnn_gamma', 'L3_gnn_beta']
_OUTS = [((1250, 512), 'float32')]


def kernel(**inputs):
    import numpy as _np
    import concourse.bacc as _bacc
    from concourse import mybir as _mybir
    from concourse.bass_utils import run_bass_kernel_spmd as _run

    nc = _bacc.Bacc("TRN2", target_bir_lowering=False, num_devices=1)
    arrays, args = {}, []
    for name in _INS:
        a = _np.ascontiguousarray(inputs[name])
        arrays[f"in_{name}_dram"] = a
        args.append(nc.dram_tensor(f"in_{name}_dram", a.shape, _mybir.dt.from_np(a.dtype), kind="ExternalInput").ap())
    for i, (shape, dtype) in enumerate(_OUTS):
        dt = _mybir.dt.from_np(_np.dtype(dtype))
        args.append(nc.dram_tensor(f"out_{i}_dram", shape, dt, kind="ExternalOutput").ap())
    args.append(nc.dram_tensor("x3_dram", (1250, 512), _mybir.dt.float32, kind="Internal").ap())
    gnn_kernel(nc, *args)
    r = _run(nc, [arrays], core_ids=[0])
    got = tuple(r.results[0][f"out_{i}_dram"] for i in range(len(_OUTS)))
    return got[0]
```

```python
from contextlib import ExitStack

import concourse.bass as bass
from concourse import mybir

F32 = mybir.dt.float32
F32R = mybir.dt.float32r
BF16 = mybir.dt.bfloat16
F16 = mybir.dt.float16
I32 = mybir.dt.int32
ALU = mybir.AluOpType
ACT = mybir.ActivationFunctionType
AX = mybir.AxisListType

P = 128
N = 1250
D = 512
DH = 256
E = 21250
KC = D // P
NT = (N + P - 1) // P
TAIL = N - (NT - 1) * P
TPG = 4
GE = P * TPG
NG = (E + GE - 1) // GE
LAST = E - (NG - 1) * GE
LAST_P, LAST_R = divmod(LAST, TPG)
W = 38
NCODE = NT * W
CH = 418
CS = CH - 2
NCH = 3
CUTS = [(0, CH), (CH, 2 * CS + 2), (2 * CS + 2, N)]
BLOCK_SPAN = 7
RING = 6
JOIN = 3
JOINS = RING // JOIN
POOL_HOTS = 2
HOTS = 4
XRING = 3
ITERS = NG // RING
BL = (N - 512) // (ITERS - 1)
LEAD = N - (ITERS - 1) * BL
HALF = N // 2
XTILES = 4
TLAG = 3
EPS = 1e-5
assert CS * (NCH - 1) + CH == N and NCODE <= 512 and NG % RING == 0 and RING % XRING == 0 and RING % JOIN == 0 and NG == 2 + NT * HOTS and LEAD <= 512 and KC * BL <= 512 and KC * JOIN * W <= 512
assert BLOCK_SPAN * GE + 1 <= 4096 and LAST_P < P


def rows(j):
    return P if j < NT - 1 else TAIL


def gnn_kernel(nc, x, src, dst, edge_attr, w01, b01, w02, b02, w11, b11, w12, b12, w2, b2,
               w31, b31, w32, b32, gamma, beta, out, x3_dram):
    with ExitStack() as ctx:
        cursor = [(nc.sbuf_base + 31) // 32 * 32]

        def place(nbytes):
            at = cursor[0]
            cursor[0] += (nbytes + 31) // 32 * 32
            return at

        def at(name, shape, dtype, offset):
            return nc.alloc_sbuf_tensor_at(name, shape, dtype, offset=offset)

        def sb(name, shape, dtype):
            size = 2 if dtype in (BF16, F16) else 4
            n = 1
            for s in shape[1:]:
                n *= s
            return at(name, shape, dtype, place(n * size))

        def sem(name):
            return ctx.enter_context(nc.semaphore(name))

        xn = sb("xn", [P, NT, D], F32)
        r_z, r_h = place(NT * D * 4), place(NT * D * 4)
        r_c, r_a = place(NT * N * 4 + 16), place(NT * N * 4 + 16)
        r_w = place(2 * KC * D * 4)
        w11_at = cursor[0]
        w11_s = sb("w11_s", [P, KC, DH], F32)
        w12_s = sb("w12_s", [P, DH // P, D], F32)
        w2_at = cursor[0]
        w2_s = sb("w2_s", [P, KC, D], F32)
        w01_s, w02_s = (at(n, [P, KC, D], F32, r_w + i * KC * D * 4) for i, n in enumerate(("w01_s", "w02_s")))
        w31_s, w32_s = (at(n, [P, KC, D], F32, r_w + i * KC * D * 4) for i, n in enumerate(("w31_s", "w32_s")))

        counts = at("counts", [P, NT, N], F32R, r_c)
        countsT = at("countsT", [P, NT, N], F32R, r_a)
        counts_x = at("counts_x", [P, NT, N], F32, r_c)
        countsT_x = at("countsT_x", [P, NT, N], F32, r_a)

        def f32(ap):
            return ap if ap.dtype == F32 else ap.bitcast(F32)

        def diagonal_of(c):
            main = c[:, :, :].rearrange("p j n -> p (j n)")[:, 0:(NT - 1) * (N + P)].rearrange("p (j r) -> p j r", r=N + P)[:, :, 0:P]
            return main, c[:, NT - 1, (NT - 1) * P:N]

        xT0 = at("xT0", [P, KC, N], F32, r_z)
        u_hi = at("u_hi", [P, NT, D], F32R, r_h)
        a = r_a
        hot_code = at("hot_code", [P, HOTS, TPG, NCODE], BF16, a); a += HOTS * TPG * NCODE * 2
        hot_lo = at("hot_lo", [P, HOTS, TPG, P], BF16, a); a += HOTS * TPG * P * 2
        codeT = at("codeT", [P, NG, TPG], F32, a); a += NG * TPG * 4
        src_loT = at("src_loT", [P, NG, TPG], F32, a); a += NG * TPG * 4
        dstT = at("dstT", [P, NG, TPG], F32, a); a += NG * TPG * 4
        row_at = a
        u_f = at("u_f", [P, 2, D], F32, a); a += 2 * D * 4
        a = max(a, r_a + (KC * N * 4 + 2 * CH * 4 + 31) // 32 * 32)
        u_lo = at("u_lo", [P, NT, D], F32R, a)
        h1_hi0 = at("h1_hi0", [P, KC, N], F32R, r_z)
        h1_lo0 = at("h1_lo0", [P, KC, N], F32R, r_a)
        h1_f0 = at("h1_f0", [P, 2, CH], F32, r_a + KC * N * 4)
        w02_hi = at("w02_hi", [P, KC, D], F32R, r_w)
        w02_lo = at("w02_lo", [P, KC, D], F32R, r_w + KC * D * 4)
        row = {}
        for n in ("dst_i", "src_i", "lo_i", "hi_i"):
            row[n] = at("row_" + n, [NG, GE], I32, row_at); row_at += GE * 4
        for n in ("dst", "src", "lo", "hi", "rel", "valid", "code", "relw", "left"):
            row[n] = at("row_" + n, [NG, GE], F32, row_at); row_at += GE * 4
        base_row = at("base_row", [NG, P], F32, row_at); row_at += P * 4
        left_row = at("left_row", [NG, P], F32, row_at); row_at += P * 4
        left_max = at("left_max", [NG, 1], F32, row_at); row_at += 32
        assert row_at <= r_a + NT * N * 4
        fixc_dst = at("fixc_dst", [P, N], BF16, r_a)
        fixc_src = at("fixc_src", [P, P], BF16, r_a + 2 * TPG * NCODE * 2)
        x1_hi = at("x1_hi", [P, XTILES, KC, P], F32R, r_h)
        x1_lo = at("x1_lo", [P, XTILES, KC, P], F32R, r_h + XTILES * KC * P * 4)
        w11_hi = at("w11_hi", [P, KC, DH], F32R, r_h + 2 * XTILES * KC * P * 4)
        w11_lo = at("w11_lo", [P, KC, DH], F32R, w11_at)
        g_f = at("g_f", [P, 4, DH], F32, r_w)
        g_hi = at("g_hi", [P, NT, DH], F32R, r_z)
        g_lo = at("g_lo", [P, NT, DH], F32R, r_z + NT * DH * 4)
        z1T = at("z1T", [P, DH // P, N], F32, r_h)
        xs_hi = at("xs_hi", [P, NT, D], F32R, r_z)
        xs_lo = at("xs_lo", [P, NT, D], F32R, r_a)
        xs_f = at("xs_f", [P, 2, D], F32, r_a + NT * D * 4)
        z2_hi = at("z2_hi", [P, KC, N], F32R, r_h)
        z2_lo_at = NT * D * 4 + 2 * D * 4
        z2_lo = at("z2_lo", [P, KC, N], F32R, r_a + z2_lo_at)
        assert z2_lo_at + KC * N * 4 <= NT * N * 4 and w2_at - w11_at == KC * D * 4
        w2_hi = at("w2_hi", [P, KC, D], F32R, w11_at)
        w2_lo = at("w2_lo", [P, KC, D], F32R, w2_at)
        x3T = at("x3T", [P, KC, N], F32, r_z)
        hT = at("hT", [P, KC, N], F32, r_h)
        ea = at("ea", [P, RING, TPG, D], F32, r_a)
        c = r_c
        xg = at("xg", [P, XRING, TPG, D], F32, c); c += XRING * TPG * D * 4
        pre_at = c
        preT = at("preT", [P, KC, N], F32, c); c += KC * N * 4
        zg = at("zg", [P, JOINS, KC, JOIN, W], F32, c); c += RING * KC * W * 4
        assert c <= r_c + NT * N * 4
        fix_hot = at("fix_hot", [P, N], F32, r_c + 2 * TPG * D * 4)

        ident = sb("ident", [P, P], F32)
        b02_b = sb("b02_b", [P, D], F32)
        b11_b = sb("b11_b", [P, DH], F32)
        b12_b = sb("b12_b", [P, D], F32)
        b2_b = sb("b2_b", [P, D], F32)
        cols = sb("cols", [P, 5, KC], F32)
        relwT = sb("relwT", [P, NG, TPG], F32)
        leftT = sb("leftT", [P, NG, TPG], F32)
        srcT = sb("srcT", [P, NG, TPG], F32)
        srcT_i = sb("srcT_i", [P, NG, TPG], I32)
        idx4 = sb("idx4", [P, XRING, TPG], I32)
        iota_n = sb("iota_n", [P, N], F16)
        lo_col = sb("lo_col", [P, HOTS, TPG], F32)
        hot_w = at("hot_w", [P, RING, TPG, W], F32, w11_at)
        zn = at("zn", [W, 2, D], F32, w11_at + RING * TPG * W * 4)
        assert w11_at + RING * TPG * W * 4 + 2 * D * 4 <= w2_at
        w32_hi = at("w32_hi", [P, KC, D], F32R, w2_at)
        w32_lo = at("w32_lo", [P, KC, D], F32R, r_w + KC * D * 4)
        h1_hi = at("h1_hi", [P, KC, N], F32R, r_z)
        h1_lo = at("h1_lo", [P, KC, N], F32R, pre_at)
        base_f = sb("base_f", [1, NG], F32)
        base_i = sb("base_i", [1, NG], I32)
        gap = sb("gap", [1, NG], F32)
        flag4 = sb("flag4", [1, 4], F32)
        flag_i = sb("flag_i", [1, 1], I32)
        eps_s = sb("eps_s", [P, 1], F32)
        one_s = sb("one_s", [P, 1], F32)
        hot_abs = sb("hot_abs", [P, 2, P], BF16)
        stats = sb("stats", [P, 2, 6], F32)
        mv = sb("mv", [P, 2, 2], F32)
        std = sb("std", [P, 2], F32)
        rstd = sb("rstd", [P, 2], F32)
        nmr = sb("nmr", [P, 2], F32)
        deg = sb("deg", [P, 4, NT], F32)
        degt = sb("degt", [P, 4, NT], F32)
        bn_st = sb("bn_st", [P, KC, NCH, 6], F32)
        bn_mv = sb("bn_mv", [P, KC, 2], F32)
        bn_t = sb("bn_t", [P, 4, KC], F32)
        assert cursor[0] <= nc.sbuf_usable_end, cursor[0] - nc.sbuf_usable_end

        ps = ctx.enter_context(nc.psum_tensor("ps", [P, 8, 512], F32))

        rows_loaded = sem("rows_loaded")
        x_loaded = [sem(f"x_loaded{i}") for i in range(4)]
        w01_loaded, w02_loaded = sem("w01_loaded"), sem("w02_loaded")
        w1_loaded, w2_loaded, w3_loaded = sem("w1_loaded"), sem("w2_loaded"), sem("w3_loaded")
        bias_loaded = sem("bias_loaded")
        cols_loaded = sem("cols_loaded")
        consts = sem("consts")
        counts_set = sem("counts_set")
        row_pad = sem("row_pad")
        prep = sem("prep")
        rows_ready = sem("rows_ready")
        idx_done = sem("idx_done")
        idx_ready = sem("idx_ready")
        xT_done, xT_evac = sem("xT_done"), sem("xT_evac")
        u_done, u_evac, u_ready = sem("u_done"), sem("u_evac"), sem("u_ready")
        abs_ready, act_lo_ready = sem("abs_ready"), sem("act_lo_ready")
        lo_staged, lo_seen = sem("lo_staged"), sem("lo_seen")
        hot_ready, lo_ready, cnt_done, cnt_added = sem("hot_ready"), sem("lo_ready"), sem("cnt_done"), sem("cnt_added")
        fixc_hot, fixc_done, fixc_added = sem("fixc_hot"), sem("fixc_done"), sem("fixc_added")
        diag_added, diag_taken = sem("diag_added"), sem("diag_taken")
        agg_done = [sem(f"agg_done{i}") for i in range(3)]
        agg_evac = [sem(f"agg_evac{i}") for i in range(3)]
        y_done, y_read = sem("y_done"), sem("y_read")
        xb_ready = [sem(f"xb_ready{i}") for i in range(3)]
        ln_step, std_ready, rstd_ready, x_ready = sem("ln_step"), sem("std_ready"), sem("rstd_ready"), sem("x_ready")
        t_done, t_evac = sem("t_done"), sem("t_evac")
        g_done, g_read, g_relu, g_ready = sem("g_done"), sem("g_read"), sem("g_relu"), sem("g_ready")
        deg_set, deg_step, deg_sq, deg_ready = sem("deg_set"), sem("deg_step"), sem("deg_sq"), sem("deg_ready")
        xs_done, xs_ready = sem("xs_done"), sem("xs_ready")
        x3_stored = sem("x3_stored")
        x3_copied = sem("x3_copied")
        pre_done, pre_evac, pre_set = sem("pre_done"), sem("pre_evac"), sem("pre_set")
        blk_done, blk_added = sem("blk_done"), sem("blk_added")
        ea_loaded = [sem(f"ea_loaded{i}") for i in range(RING)]
        xg_loaded = [sem(f"xg_loaded{i}") for i in range(XRING)]
        idx_staged, idx_seen = sem("idx_staged"), sem("idx_seen")
        add_done, relu_done, win_ready = sem("add_done"), sem("relu_done"), sem("win_ready")
        scat_done, zn_ready, turn_done, zg_ready = sem("scat_done"), sem("zn_ready"), sem("turn_done"), sem("zg_ready")
        turn_seen = sem("turn_seen")
        join_done, pre_added = sem("join_done"), sem("pre_added")
        fix_x, fix_e, fix_msg, fix_done, fix_added = (sem("fix_x"), sem("fix_e"), sem("fix_msg"), sem("fix_done"), sem("fix_added"))
        fix_idx = sem("fix_idx")
        w11_split, x1_hi_ready = sem("w11_split"), sem("x1_hi_ready")
        w02_split, w2_split, w32_split = sem("w02_split"), sem("w2_split"), sem("w32_split")
        h1_hi0_ready, h1_f0_ready, z2_hi_ready = sem("h1_hi0_ready"), sem("h1_f0_ready"), sem("z2_hi_ready")
        h1_hi_ready, h1_ready = sem("h1_hi_ready"), sem("h1_ready")
        nmr_ready = sem("nmr_ready")
        w32_done, h2_ready, bn_step, bn_sq, bn_ready, hn_ready = (
            sem("w32_done"), sem("h2_ready"), sem("bn_step"), sem("bn_sq"), sem("bn_ready"), sem("hn_ready"))
        bn_calc = sem("bn_calc")
        out_stored = sem("out_stored")

        def node_rows(t):
            return t[0:(NT - 1) * P, :].rearrange("(j p) d -> p j d", p=P)

        def w_view(t):
            return t.rearrange("(k p) n -> p k n", p=P)

        def feature_cols(t):
            return t.rearrange("(c p) -> p c", p=P)

        def ea_rows(g):
            return edge_attr[bass.ds(g * GE, GE), :].rearrange("(p r) d -> p (r d)", p=P)

        def join_bank(slot):
            return ps[:, slot, 0:KC * JOIN * W].rearrange("p (f h w) -> p f h w", f=KC, h=JOIN)

        block = ctx.enter_context(nc.Block())

        @block.sync
        def _(sp):
            sp.wait_ge(row_pad, 2)
            for n, t in (("dst_i", dst), ("src_i", src)):
                sp.dma_start(row[n][0:NG - 1, :], t[0:(NG - 1) * GE].rearrange("(g e) -> g e", e=GE)).then_inc(rows_loaded, 16)
                sp.dma_start(row[n][NG - 1:NG, 0:LAST],
                             t[(NG - 1) * GE:E].rearrange("(a e) -> a e", a=1)).then_inc(rows_loaded, 16)
            for i in range(3):
                sp.dma_start(xn[:, 3 * i:3 * i + 3, :], node_rows(x)[:, 3 * i:3 * i + 3, :]).then_inc(x_loaded[i], 16)
            sp.dma_start(xn[0:TAIL, NT - 1, :], x[(NT - 1) * P:N, :]).then_inc(x_loaded[3], 16)
            sp.dma_start(w01_s[:, :, :], w_view(w01)).then_inc(w01_loaded, 16)
            sp.dma_start(cols[:, 0, :], feature_cols(b01), allow_slow_non_contiguous=True).then_inc(cols_loaded, 16)
            sp.dma_start(w02_s[:, :, :], w_view(w02)).then_inc(w02_loaded, 16)
            for t, b in ((b02_b, b02), (b11_b, b11), (b12_b, b12), (b2_b, b2)):
                sp.dma_start(t[:, :], b.partition_broadcast(P)).then_inc(bias_loaded, 16)
            sp.dma_start(w11_s[:, :, :], w_view(w11)).then_inc(w1_loaded, 16)
            sp.dma_start(w12_s[:, :, :], w_view(w12)).then_inc(w1_loaded, 16)
            sp.dma_start(w2_s[:, :, :], w_view(w2)).then_inc(w2_loaded, 16)
            for i, b in enumerate((b31, b32, gamma, beta)):
                sp.dma_start(cols[:, 1 + i, :], feature_cols(b), allow_slow_non_contiguous=True).then_inc(cols_loaded, 16)
            sp.wait_ge(g_ready, NT)
            sp.dma_start(w31_s[:, :, :], w_view(w31)).then_inc(w3_loaded, 16)
            sp.dma_start(w32_s[:, :, :], w_view(w32)).then_inc(w3_loaded, 16)

            sp.wait_ge(agg_done[2], NCH * KC)
            def preload(s):
                sp.dma_start(ea[:, s, :, :].rearrange("p r d -> p (r d)"), ea_rows(s)).then_inc(ea_loaded[s], 16)

            early = z2_lo_at // (TPG * D * 4)
            for s in range(early):
                preload(s)
            for j in range(NT):
                sp.wait_ge(x_ready, 2 * NT + j + 1)
                sp.dma_start(x3_dram[j * P:j * P + rows(j), :], xn[0:rows(j), j, :]).then_inc(x3_stored, 16)
            sp.wait_ge(y_done, 3 * NT)
            for s in range(early, RING):
                preload(s)

            def reload(it, s):
                sp.wait_ge(scat_done, RING * (it - 1) + s + 1)
                g = RING * it + s
                if isinstance(it, int) and g == NG - 1:
                    e0 = g * GE
                    sp.dma_start(ea[0:LAST_P, s, :, :].rearrange("p r d -> p (r d)"),
                                 edge_attr[e0:e0 + LAST_P * TPG, :].rearrange("(p r) d -> p (r d)", r=TPG)).then_inc(ea_loaded[s], 16)
                    if LAST_R:
                        sp.dma_start(ea[LAST_P:LAST_P + 1, s, 0:LAST_R, :].rearrange("p r d -> p (r d)"),
                                     edge_attr[e0 + LAST_P * TPG:E, :].rearrange("(p r) d -> p (r d)", p=1)).then_inc(ea_loaded[s], 16)
                else:
                    sp.dma_start(ea[:, s, :, :].rearrange("p r d -> p (r d)"), ea_rows(g)).then_inc(ea_loaded[s], 16)

            with sp.Fori(1, ITERS - 1) as it:
                for s in range(RING):
                    reload(it, s)
            for s in range(RING):
                reload(ITERS - 1, s)

            for j in range(NT):
                sp.wait_ge(x_ready, 3 * NT + j + 1)
                sp.dma_start(out[j * P:j * P + rows(j), :], xn[0:rows(j), j, :]).then_inc(out_stored, 16)
            sp.wait_ge(x3_stored, 16 * NT)
            sp.wait_ge(out_stored, 16 * NT)

        @block.gpsimd
        def _(pool):
            pool.memset(ident[:, :], 0.0).then_inc(consts, 1)
            pool.wait_ge(consts, 1)
            pool.affine_select(out=ident[:, :], in_=ident[:, :], compare_op=ALU.not_equal, fill=1.0, base=0,
                               pattern=[[-1, P]], channel_multiplier=1).then_inc(consts, 1)
            pool.iota(iota_n[:, :], [[1, N]], base=0, channel_multiplier=0, allow_small_or_imprecise_dtypes=True).then_inc(consts, 1)
            pool.memset(eps_s[:, :], EPS).then_inc(consts, 1)
            pool.memset(one_s[:, :], 1.0).then_inc(consts, 1)
            pool.memset(f32(counts[:, :, :]), 0.0).then_inc(counts_set, 1)
            pool.wait_ge(counts_set, 1)
            diag_main, diag_tail = diagonal_of(counts)
            pool.tensor_copy(f32(diag_main), ident[:, :].unsqueeze(1).to_broadcast([P, NT - 1, P])).then_inc(counts_set, 1)
            pool.tensor_copy(f32(diag_tail), ident[:, 0:TAIL]).then_inc(counts_set, 1)
            pool.wait_ge(idx_ready, 1)

            def lo_hots(g, slot):
                if not (isinstance(g, int) and g < HOTS):
                    pool.wait_ge(cnt_done, g - HOTS + 1)
                pool.tensor_copy(lo_col[:, slot, :], src_loT[:, bass.ds(g, 1), :].rearrange("p a b -> p (a b)")).then_inc(lo_staged, 1)
                pool.wait_ge(lo_staged, g + 1)
                pool.sem_inc(lo_seen, 1)
                for r in range(POOL_HOTS):
                    ins = pool.tensor_scalar(hot_lo[:, slot, r, :], iota_n[:, 0:P], lo_col[:, slot, r:r + 1], None, ALU.is_equal)
                ins.then_inc(lo_ready, 1)

            def low_u(j, slot, n):
                pool.wait_ge(u_evac, j + 1)
                at_j = slice(j, j + 1) if isinstance(j, int) else bass.ds(j, 1)
                pool.tensor_tensor(u_lo[0:n, at_j, :], u_f[0:n, slot:slot + 1, :], u_hi[0:n, at_j, :].bitcast(F32),
                                   ALU.subtract).then_inc(u_ready, 1)

            for g in range(2 + HOTS):
                lo_hots(g, g % HOTS)
            with pool.Fori(0, NT // 2 - 1) as h:
                for i in range(2):
                    for k in range(HOTS):
                        lo_hots(HOTS * (2 * h + i + 1) + k + 2, (k + 2) % HOTS)
                    low_u(2 * h + i, i, P)
            for k in range(HOTS):
                lo_hots(HOTS * (NT - 1) + k + 2, (k + 2) % HOTS)
            low_u(NT - 2, 0, P)
            low_u(NT - 1, 1, TAIL)
            pool.wait_ge(w02_split, 1)
            pool.tensor_tensor(w02_lo[:, :, :], w02_s[:, :, :], w02_hi[:, :, :].bitcast(F32), ALU.subtract).then_inc(w02_split, 1)
            pool.wait_ge(bias_loaded, 64)
            for j in range(NT):
                pool.tensor_tensor(xn[0:rows(j), j, :], xn[0:rows(j), j, :], b02_b[0:rows(j), :], ALU.add).then_inc(xb_ready[0], 1)
            pool.wait_ge(w11_split, 1)
            pool.tensor_tensor(w11_lo[:, :, :], w11_s[:, :, :], w11_hi[:, :, :].bitcast(F32), ALU.subtract).then_inc(w11_split, 1)
            for j in range(NT):
                pool.wait_ge(g_relu, j + 1)
                pool.tensor_tensor(g_lo[0:rows(j), j, :], g_f[0:rows(j), j % 4, :], g_hi[0:rows(j), j, :].bitcast(F32),
                                   ALU.subtract).then_inc(g_ready, 1)
            for j in range(NT):
                pool.wait_ge(xs_done, j + 1)
                pool.tensor_tensor(xs_lo[0:rows(j), j, :], xs_f[0:rows(j), j % 2, :], xs_hi[0:rows(j), j, :].bitcast(F32),
                                   ALU.subtract).then_inc(xs_ready, 1)
            pool.wait_ge(w2_split, 1)
            pool.tensor_tensor(w2_lo[:, :, :], w2_s[:, :, :], w2_hi[:, :, :].bitcast(F32), ALU.subtract).then_inc(w2_split, 1)
            for j in range(NT):
                pool.tensor_tensor(xn[0:rows(j), j, :], xn[0:rows(j), j, :], b2_b[0:rows(j), :], ALU.add).then_inc(xb_ready[2], 1)

            pool.wait_ge(x3_stored, 16 * NT)
            pool.wait_ge(agg_done[2], NCH * KC)
            irregular = pool.value_load(flag_i[0:1, 0:1], min_val=0, max_val=1)
            with pool.If(irregular > 0):
                def fix_load(g, r, attrs):
                    n = g * TPG + r
                    pool.tensor_copy(idx4[:, 0, 0:1], srcT_i[:, bass.ds(g, 1), r:r + 1].rearrange("p a b -> p (a b)")).then_inc(fix_idx, 1)
                    pool.wait_ge(fix_idx, n + 1)
                    pool.sem_inc(idx_seen, 1)
                    pool.indirect_dma_start(out=xg[:, 0, 0, :], out_offset=None, in_=x3_dram[:, :],
                                            in_offset=bass.IndirectOffsetOnAxis(ap=idx4[:, 0, 0:1], axis=0)).then_inc(fix_x, 16)
                    pool.dma_start(xg[0:attrs.shape[0], 1, 0, :], attrs).then_inc(fix_e, 16)
                    pool.wait_ge(fix_added, n * KC + KC + 1)
                with pool.Fori(0, NG - 1) as g:
                    for r in range(TPG):
                        fix_load(g, r, edge_attr[bass.ds(g * GE, GE), :].rearrange("(p r) d -> r p d", r=TPG)[r, :, :])
                for r in range(TPG):
                    fix_load(NG - 1, r, edge_attr[(NG - 1) * GE + r:E:TPG, :])

            def gather(it, s):
                g, slot = RING * it + s, s % XRING
                if not (isinstance(g, int) and g < XRING):
                    pool.wait_ge(add_done, g - XRING + 1)
                pool.tensor_copy(idx4[:, slot, :], srcT_i[:, bass.ds(g, 1), :].rearrange("p a b -> p (a b)")).then_inc(idx_staged, 1)
                pool.wait_ge(idx_staged, g + 1)
                pool.sem_inc(idx_seen, 1)
                for r in range(TPG):
                    pool.indirect_dma_start(out=xg[:, slot, r, :], out_offset=None, in_=x3_dram[:, :],
                                            in_offset=bass.IndirectOffsetOnAxis(ap=idx4[:, slot, r:r + 1], axis=0)).then_inc(xg_loaded[slot], 16)

            for s in range(RING):
                gather(0, s)
            with pool.Fori(1, ITERS) as it:
                for s in range(RING):
                    gather(it, s)

        @block.scalar
        def _(act):
            def evac_T(n, j, dst_t):
                act.wait_ge(xT_done, n + 1)
                act.copy(dst_t[:, :, P * j:P * j + rows(j)],
                         ps[:, n % 2, :].rearrange("p (c n) -> p c n", c=KC)[:, :, 0:rows(j)]).then_inc(xT_evac, 1)

            for layer, blocks in enumerate((KC, DH // P, KC)):
                act.sem_inc(agg_evac[layer], blocks)
            for j in range(NT):
                evac_T(j, j, xT0)
            act.wait_ge(consts, 5)

            def act_hot(g, slot):
                act.wait_ge(lo_staged, g + 1)
                if not (isinstance(g, int) and g < HOTS):
                    act.wait_ge(cnt_done, g - HOTS + 1)
                act.activation(hot_abs[:, slot % 2, :], iota_n[:, 0:P], ACT.Abs, bias=lo_col[:, slot, POOL_HOTS:POOL_HOTS + 1],
                               scale=-1.0).then_inc(abs_ready, 1)
                act.wait_ge(abs_ready, g + 1)
                act.activation(hot_lo[:, slot, POOL_HOTS, :], hot_abs[:, slot % 2, :], ACT.Relu, bias=one_s[:, 0:1],
                               scale=-1.0).then_inc(act_lo_ready, 1)

            def evac_u(j, slot, n):
                act.wait_ge(u_done, j + 1)
                if not (isinstance(j, int) and j < 2):
                    act.wait_ge(u_ready, j - 1)
                at_j = slice(j, j + 1) if isinstance(j, int) else bass.ds(j, 1)
                act.copy(u_f[0:n, slot, :], ps[0:n, 2 + slot, :])
                act.copy(u_hi[0:n, at_j, :].rearrange("p a d -> p (a d)"), ps[0:n, 2 + slot, :]).then_inc(u_evac, 1)

            def hot_round(i):
                for k in range(HOTS):
                    act_hot(HOTS * i + k + 2, (k + 2) % HOTS)

            for g in range(2):
                act_hot(g, g)
            hot_round(0)
            hot_round(1)
            evac_u(0, 0, P)
            with act.Fori(1, NT // 2) as h:
                hot_round(2 * h)
                evac_u(2 * h - 1, 1, P)
                hot_round(2 * h + 1)
                evac_u(2 * h, 0, P)
            evac_u(NT - 1, 1, TAIL)

            def evac_agg(layer, nc_, emit):
                with act.Fori(0, NCH) as i:
                    for cc in range(nc_):
                        act.wait_ge(agg_done[layer], i * nc_ + cc + 1)
                        emit(cc, bass.ds(i * CS, CH))

            act.wait_ge(u_done, NT)
            act.wait_ge(w02_loaded, 16)
            act.copy(w02_hi[:, :, :], w02_s[:, :, :]).then_inc(w02_split, 1)
            act.wait_ge(cols_loaded, 80)
            evac_agg(0, KC, lambda cc, n: act.activation(h1_hi0[:, cc, n], ps[:, cc, 0:CH], ACT.Relu, bias=cols[:, 0, cc:cc + 1])
                     .then_inc(h1_hi0_ready, 1))

            act.wait_ge(w1_loaded, 32)
            act.copy(w11_hi[:, :, :], w11_s[:, :, :]).then_inc(w11_split, 1)

            def sqrt_var(n):
                act.wait_ge(ln_step, 2 * n + 2)
                act.activation(std[:, n % 2:n % 2 + 1], mv[:, n % 2, 1:2], ACT.Sqrt, bias=eps_s[:, 0:1]).then_inc(std_ready, 1)

            def norm_and_turn(cT):
                for j in range(NT - 1):
                    sqrt_var(j)
                for t in range(3 * NT):
                    j, q = divmod(t, 3)
                    act.wait_ge(t_done, t + 1)
                    n0, n1 = 4 * P * q, min(4 * P * (q + 1), N)
                    act.copy(cT[0:rows(j), j, n0:n1], ps[0:rows(j), t % 4, 0:n1 - n0]).then_inc(t_evac, 1)
                    if t == 2:
                        sqrt_var(NT - 1)

            irregular = act.value_load(flag_i[0:1, 0:1], min_val=0, max_val=1)
            with act.If(irregular > 0):
                norm_and_turn(countsT_x)
            with act.Else():
                norm_and_turn(countsT)
            def relu_g(j):
                act.wait_ge(g_read, j + 1)
                act.activation(g_hi[0:rows(j), j, :], g_f[0:rows(j), j % 4, :], ACT.Relu)
                act.activation(g_f[0:rows(j), j % 4, :], g_f[0:rows(j), j % 4, :], ACT.Relu).then_inc(g_relu, 1)

            for j in range(NT):
                act.wait_ge(xT_done, NT + j + 1)
                if j >= XTILES:
                    act.wait_ge(g_done, j - XTILES + 1)
                act.copy(x1_hi[:, j % XTILES, :, 0:rows(j)],
                         ps[:, j % 2, :].rearrange("p (c n) -> p c n", c=KC)[:, :, 0:rows(j)]).then_inc(x1_hi_ready, 1)
                if j >= 2:
                    relu_g(j - 2)
            relu_g(NT - 2)
            relu_g(NT - 1)
            act.wait_ge(deg_step, 2)
            act.activation(degt[:, 1, :], degt[:, 0, :], ACT.Sqrt).then_inc(deg_sq, 1)
            evac_agg(1, DH // P, lambda cc, n: act.copy(z1T[:, cc, n], ps[:, cc, 0:CH]).then_inc(agg_evac[1], 1))
            act.wait_ge(deg_step, 5)
            act.activation(degt[:, 3, :], degt[:, 2, :], ACT.Sqrt).then_inc(deg_sq, 1)
            def scale_x(j):
                act.wait_ge(x_ready, NT + j + 1)
                if j >= 2:
                    act.wait_ge(xs_ready, j - 1)
                if j == 0:
                    act.wait_ge(deg_ready, 1)
                act.activation(xs_f[0:rows(j), j % 2, :], xn[0:rows(j), j, :], ACT.Copy, scale=deg[0:rows(j), 1, j:j + 1])
                act.activation(xs_hi[0:rows(j), j, :], xn[0:rows(j), j, :], ACT.Copy, scale=deg[0:rows(j), 1, j:j + 1]).then_inc(xs_done, 1)

            for j in range(NT):
                sqrt_var(NT + j)
                if j >= 2:
                    scale_x(j - 2)
            scale_x(NT - 2)
            scale_x(NT - 1)
            act.wait_ge(w2_loaded, 16)
            act.copy(w2_hi[:, :, :], w2_s[:, :, :]).then_inc(w2_split, 1)
            evac_agg(2, KC, lambda cc, n: act.copy(z2_hi[:, cc, n], ps[:, cc, 0:CH]).then_inc(z2_hi_ready, 1))
            for j in range(NT):
                sqrt_var(2 * NT + j)
                if j >= TLAG + 1:
                    evac_T(2 * NT + j - TLAG - 1, j - TLAG - 1, x3T)
            for j in range(NT - TLAG - 1, NT):
                evac_T(2 * NT + j, j, x3T)
            act.wait_ge(y_done, 3 * NT)
            act.wait_ge(w3_loaded, 32)
            act.copy(w32_hi[:, :, :], w32_s[:, :, :]).then_inc(w32_split, 1)
            act.wait_ge(y_done, 3 * NT)
            act.wait_ge(xT_evac, 3 * NT)
            act.copy(hT[:, :, :], x3T[:, :, :]).then_inc(x3_copied, 1)

            def evac_lead(cc):
                act.wait_ge(pre_done, cc + 1)
                act.activation(preT[:, cc, 0:LEAD], ps[:, 2 + cc % 2, 0:LEAD], ACT.Identity, bias=cols[:, 1, cc:cc + 1]).then_inc(pre_evac, 1)

            def rectify(it, s):
                g = RING * it + s
                act.wait_ge(add_done, g + 1)
                act.activation(ea[:, s, :, :], ea[:, s, :, :], ACT.Relu).then_inc(relu_done, 1)

            def evac_n(it, s):
                g = RING * it + s
                act.wait_ge(scat_done, g + 1)
                if not (isinstance(g, int) and g < 2):
                    act.wait_ge(turn_done, g - 1)
                act.copy(zn[:, s % 2, :], ps[0:W, 4 + s % 2, :]).then_inc(zn_ready, 1)

            def evac_z(it, s):
                g, join = RING * it + s, s // JOIN
                act.wait_ge(turn_done, g + 1)
                if not (isinstance(it, int) and it == 0):
                    act.wait_ge(join_done, JOINS * (it - 1) + join + 1)
                act.copy(zg[:, join, :, s % JOIN, :], ps[:, 6 + s % 2, 0:KC * W].rearrange("p (c w) -> p c w", c=KC)).then_inc(zg_ready, 1)

            for cc in range(KC - 1):
                evac_lead(cc)
            for s in range(RING):
                rectify(0, s)
                if s == 0:
                    evac_lead(KC - 1)
                if s >= 2:
                    evac_z(0, s - 2)
                if s:
                    evac_n(0, s - 1)
            with act.Fori(1, ITERS) as it:
                for s in range(RING):
                    rectify(it, s)
                    if s >= 2:
                        evac_z(it, s - 2)
                    else:
                        evac_z(it - 1, RING - 2 + s)
                    if s:
                        evac_n(it, s - 1)
                    else:
                        evac_n(it - 1, RING - 1)
            evac_n(ITERS - 1, RING - 1)
            evac_z(ITERS - 1, RING - 2)
            evac_z(ITERS - 1, RING - 1)
            act.wait_ge(pre_added, NG + 1)
            for n0, n1 in CUTS:
                act.activation(h1_hi[:, :, n0:n1], preT[:, :, n0:n1], ACT.Relu).then_inc(h1_hi_ready, 1)
            for cc in range(KC):
                nodes = slice(0, N if cc < KC - 1 else HALF)
                act.wait_ge(bn_step, 2 * cc + 2)
                act.activation(bn_t[:, 0, cc:cc + 1], bn_mv[:, cc, 1:2], ACT.Sqrt, bias=eps_s[:, 0:1]).then_inc(bn_sq, 1)
                act.wait_ge(bn_ready, cc + 1)
                act.activation(hT[:, cc, nodes], hT[:, cc, nodes], ACT.Identity, bias=bn_t[:, 3, cc:cc + 1],
                               scale=bn_t[:, 2, cc:cc + 1]).then_inc(hn_ready, 1)

            def normalise(j):
                act.wait_ge(nmr_ready, j + 1)
                act.activation(xn[0:rows(j), j, :], xn[0:rows(j), j, :], ACT.Identity, bias=nmr[0:rows(j), j % 2:j % 2 + 1],
                               scale=rstd[0:rows(j), j % 2:j % 2 + 1]).then_inc(x_ready, 1)

            for j in range(NT):
                sqrt_var(3 * NT + j)
                if j:
                    normalise(j - 1)
            normalise(NT - 1)

        @block.vector
        def _(dve):
            steps = [0]

            def step(ins):
                steps[0] += 1
                ins.then_inc(prep, 1)
                dve.wait_ge(prep, steps[0])

            dve.memset(row["dst_i"][:, :], -1).then_inc(row_pad, 1)
            dve.memset(row["src_i"][:, :], 0).then_inc(row_pad, 1)
            dve.wait_ge(rows_loaded, 64)
            r = {n: t[:, :] for n, t in row.items()}
            dve.tensor_copy(r["dst"], r["dst_i"])
            dve.tensor_copy(r["src"], r["src_i"])
            dve.tensor_scalar(r["lo_i"], r["src_i"], P - 1, None, ALU.bitwise_and)
            step(dve.tensor_scalar(r["hi_i"], r["src_i"], P.bit_length() - 1, None, ALU.logical_shift_right))
            dve.tensor_copy(r["lo"], r["lo_i"])
            dve.tensor_copy(r["hi"], r["hi_i"])
            step(dve.tensor_scalar(base_row[:, :], row["dst"][:, 0:1].to_broadcast([NG, P]), float(N - W), 0.0, ALU.min, ALU.max))
            step(dve.tensor_scalar(r["rel"], r["dst"], base_row[:, 0:1], None, ALU.subtract))
            step(dve.tensor_scalar(r["left"], r["rel"], float(W), None, ALU.is_lt))
            step(dve.scalar_tensor_tensor(out=r["valid"], in0=r["rel"], scalar=0.0, in1=r["left"], op0=ALU.is_ge, op1=ALU.mult))
            step(dve.scalar_tensor_tensor(out=r["code"], in0=r["hi"], scalar=float(W), in1=r["rel"], op0=ALU.mult, op1=ALU.add))
            step(dve.scalar_tensor_tensor(out=r["code"], in0=r["code"], scalar=1.0, in1=r["valid"], op0=ALU.add, op1=ALU.mult))
            dve.tensor_scalar(r["code"], r["code"], -1.0, None, ALU.add)
            step(dve.scalar_tensor_tensor(out=r["relw"], in0=r["rel"], scalar=1.0, in1=r["valid"], op0=ALU.add, op1=ALU.mult))
            dve.tensor_scalar(r["relw"], r["relw"], -1.0, None, ALU.add)
            step(dve.tensor_scalar(r["rel"], r["valid"], -1.0, 1.0, ALU.mult, ALU.add))
            step(dve.scalar_tensor_tensor(out=r["left"], in0=r["dst"], scalar=1.0, in1=r["rel"], op0=ALU.add, op1=ALU.mult))
            step(dve.tensor_scalar(r["left"], r["left"], -1.0, None, ALU.add))
            step(dve.tensor_reduce(left_max[:, :], r["left"], AX.X, ALU.max))
            dve.tensor_copy(left_row[:, :], left_max[:, :].to_broadcast([NG, P])).then_inc(rows_ready, 1)

            dve.wait_ge(idx_done, 1)
            def turned(bank, k):
                return ps[:, bank, k * NG * TPG:(k + 1) * NG * TPG].rearrange("p (r g) -> p g r", r=TPG)
            dve.tensor_copy(codeT[:, :, :], turned(4, 0))
            dve.tensor_copy(src_loT[:, :, :], turned(4, 1))
            dve.tensor_copy(relwT[:, :, :], turned(4, 2))
            dve.tensor_copy(leftT[:, :, :], turned(5, 0))
            dve.tensor_copy(srcT[:, :, :], turned(5, 1))
            dve.tensor_copy(dstT[:, :, :], turned(3, 0))
            dve.tensor_copy(srcT_i[:, :, :], turned(5, 1))
            off = 2 * NG * TPG
            dve.tensor_copy(base_i[:, :], ps[0:1, 5, off:off + NG])
            step(dve.tensor_copy(base_f[:, :], ps[0:1, 5, off:off + NG]))
            dve.tensor_reduce(flag4[:, 0:1], ps[0:1, 5, off + NG:off + 2 * NG], AX.X, ALU.max)
            step(dve.tensor_tensor(gap[:, 0:NG - 1], base_f[:, 1:NG], base_f[:, 0:NG - 1], ALU.subtract))
            step(dve.tensor_reduce(flag4[:, 1:2], gap[:, 0:NG - 1], AX.X, ALU.min))
            step(dve.tensor_tensor(gap[:, 0:NG - BLOCK_SPAN], base_f[:, BLOCK_SPAN:NG], base_f[:, 0:NG - BLOCK_SPAN], ALU.subtract))
            step(dve.tensor_reduce(flag4[:, 2:3], gap[:, 0:NG - BLOCK_SPAN], AX.X, ALU.min))
            step(dve.tensor_scalar(flag4[:, 0:1], flag4[:, 0:1], 0.0, None, ALU.is_ge))
            step(dve.tensor_scalar(flag4[:, 1:2], flag4[:, 1:2], 0.0, None, ALU.is_lt))
            step(dve.tensor_scalar(flag4[:, 2:3], flag4[:, 2:3], float(W), None, ALU.is_lt))
            step(dve.tensor_reduce(flag4[:, 3:4], flag4[:, 0:3], AX.X, ALU.max))
            dve.tensor_copy(flag_i[:, :], flag4[:, 3:4]).then_inc(idx_ready, 1)

            dve.wait_ge(consts, 5)
            dve.wait_ge(counts_set, 3)
            dve.wait_ge(idx_ready, 1)

            def code_hots(g, slot):
                if not (isinstance(g, int) and g < HOTS):
                    dve.wait_ge(cnt_done, g - HOTS + 1)
                for r in range(TPG):
                    ins = dve.tensor_scalar(hot_code[:, slot, r, :], iota_n[:, 0:NCODE],
                                            codeT[:, bass.ds(g, 1), r:r + 1].rearrange("p a b -> p (a b)"), None, ALU.is_equal)
                for r in range(POOL_HOTS + 1, TPG):
                    ins = dve.tensor_scalar(hot_lo[:, slot, r, :], iota_n[:, 0:P],
                                            src_loT[:, bass.ds(g, 1), r:r + 1].rearrange("p a b -> p (a b)"), None, ALU.is_equal)
                ins.then_inc(hot_ready, 1)

            def window_base(g):
                return dve.value_load(base_i[0:1, bass.ds(g, 1)], min_val=0, max_val=N - W)

            def add_counts(g, slot, base):
                dve.wait_ge(cnt_done, g + 1)
                if not (isinstance(g, int) and g == 0):
                    dve.wait_ge(cnt_added, g)
                win = counts[:, :, bass.ds(base, W)]
                dve.tensor_tensor(win, ps[:, 4 + slot, 0:NCODE].rearrange("p (h w) -> p h w", h=NT), f32(win), ALU.add).then_inc(cnt_added, 1)

            def count_round(i):
                for k in range(HOTS):
                    base = window_base(HOTS * i + k)
                    code_hots(HOTS * i + k + 2, (k + 2) % HOTS)
                    add_counts(HOTS * i + k, k, base)

            code_hots(0, 0)
            code_hots(1, 1)
            count_round(0)
            with dve.Fori(1, NT) as i:
                count_round(i)
            for g in (NG - 2, NG - 1):
                add_counts(g, g % HOTS, window_base(g))
            dve.wait_ge(cnt_added, NG)

            def diagonal(c, op, done):
                for d, i in zip(diagonal_of(c), (ident[:, :].unsqueeze(1).to_broadcast([P, NT - 1, P]), ident[:, 0:TAIL])):
                    dve.tensor_tensor(d, f32(d), i, op).then_inc(done, 1)

            def low_h0(c):
                for n in range(NCH * KC):
                    i, cc = divmod(n, KC)
                    nodes = slice(i * CS, i * CS + CH)
                    dve.wait_ge(h1_hi0_ready, n + 1)
                    dve.tensor_scalar(h1_f0[:, n % 2, :], ps[:, cc, 0:CH], cols[:, 0, cc:cc + 1], 0.0, ALU.add, ALU.max).then_inc(h1_f0_ready, 1)
                    dve.wait_ge(h1_f0_ready, n + 1)
                    dve.tensor_tensor(h1_lo0[:, cc, nodes], h1_f0[:, n % 2, :], h1_hi0[:, cc, nodes].bitcast(F32),
                                      ALU.subtract).then_inc(agg_evac[0], 1)
                    if n < NT:
                        ins = dve.tensor_reduce(deg[:, 0, n:n + 1], f32(c[:, n, :]), AX.X, ALU.add)
                    if n == NT - 1:
                        ins.then_inc(deg_step, 1)

            def in_degrees(c, cT):
                dve.tensor_reduce(deg[:, 2, 0:NT - 1], f32(cT[:, 0:NT - 1, :]), AX.X, ALU.add).then_inc(deg_step, 1)
                dve.tensor_reduce(deg[0:TAIL, 2, NT - 1:NT], f32(cT[0:TAIL, NT - 1, :]), AX.X, ALU.add).then_inc(deg_step, 1)
                diagonal(c, ALU.subtract, diag_taken)

            dve.memset(deg[:, :, :], 1.0)
            dve.memset(degt[:, :, :], 1.0).then_inc(deg_set, 1)
            dve.wait_ge(deg_set, 1)
            irregular = dve.value_load(flag_i[0:1, 0:1], min_val=0, max_val=1)
            with dve.If(irregular > 0):
                dve.memset(counts_x[:, :, :], 0.0).then_inc(counts_set, 1)
                dve.wait_ge(counts_set, 4)
                with dve.Fori(0, NG) as g:
                    for rr in range(TPG):
                        dve.tensor_scalar(fixc_dst[:, :], iota_n[:, :],
                                          dstT[:, bass.ds(g, 1), rr:rr + 1].rearrange("p a b -> p (a b)"), None, ALU.is_equal)
                        for h in range(NT):
                            n = (g * TPG + rr) * NT + h
                            dve.tensor_scalar(fixc_src[:, 0:rows(h)], iota_n[:, P * h:P * h + rows(h)],
                                              srcT[:, bass.ds(g, 1), rr:rr + 1].rearrange("p a b -> p (a b)"), None,
                                              ALU.is_equal).then_inc(fixc_hot, 1)
                            dve.wait_ge(fixc_done, n + 1)
                            for q, (n0, n1) in enumerate(CUTS):
                                ins = dve.tensor_tensor(counts_x[0:rows(h), h, n0:n1], ps[0:rows(h), 4 + q, 0:n1 - n0],
                                                        counts_x[0:rows(h), h, n0:n1], ALU.add)
                            ins.then_inc(fixc_added, 1)
                            dve.wait_ge(fixc_added, n + 2)
                diagonal(counts_x, ALU.add, diag_added)
                dve.wait_ge(diag_added, 2)
                low_h0(counts_x)
            with dve.Else():
                low_h0(counts)
            dve.wait_ge(deg_step, 1)
            dve.tensor_scalar(degt[:, 0, :], deg[:, 0, :], -1.0, 1.0, ALU.add, ALU.max).then_inc(deg_step, 1)

            def ln_begin(n, j, y_sum):
                dve.wait_ge(y_done, n + 1)
                y_sum(xn[0:rows(j), j, :], ps[0:rows(j), 4 + n % 2, :]).then_inc(y_read, 1)
                dve.wait_ge(y_read, n + 1)
                dve.bn_stats(stats[0:rows(j), n % 2, :], xn[0:rows(j), j, :]).then_inc(ln_step, 1)
                dve.wait_ge(ln_step, 2 * n + 1)
                dve.bn_aggr(mv[0:P if j < NT - 1 else TAIL, n % 2, :], stats[0:rows(j), n % 2, :]).then_inc(ln_step, 1)

            def ln_finish(n, j):
                dve.wait_ge(std_ready, n + 1)
                dve.reciprocal(rstd[0:rows(j), n % 2:n % 2 + 1], std[0:rows(j), n % 2:n % 2 + 1]).then_inc(rstd_ready, 1)
                dve.wait_ge(rstd_ready, n + 1)
                dve.tensor_scalar(xn[0:rows(j), j, :], xn[0:rows(j), j, :], mv[0:rows(j), n % 2, 0:1], rstd[0:rows(j), n % 2:n % 2 + 1],
                                  ALU.subtract, ALU.mult).then_inc(x_ready, 1)

            def layer_norm(layer, before, y_sum):
                for j in range(NT):
                    before(j)
                    ln_begin(NT * layer + j, j, y_sum(j))
                    if j:
                        ln_finish(NT * layer + j - 1, j - 1)
                ln_finish(NT * layer + NT - 1, NT - 1)

            def plus_x(j):
                return lambda xr, y: dve.tensor_tensor(xr, y, xr, ALU.add)

            layer_norm(0, lambda j: dve.wait_ge(xb_ready[0], j + 1), plus_x)

            def hidden_in(j):
                dve.wait_ge(x1_hi_ready, j + 1)
                dve.tensor_tensor(x1_lo[:, j % XTILES, :, 0:rows(j)], ps[:, j % 2, :].rearrange("p (c n) -> p c n", c=KC)[:, :, 0:rows(j)],
                                  x1_hi[:, j % XTILES, :, 0:rows(j)].bitcast(F32), ALU.subtract).then_inc(xT_evac, 1)

            def hidden_out(j):
                dve.wait_ge(g_done, j + 1)
                if j >= 4:
                    dve.wait_ge(g_ready, j - 3)
                dve.tensor_tensor(g_f[0:rows(j), j % 4, :], ps[0:rows(j), 2 + j % 2, 0:DH], b11_b[0:rows(j), :], ALU.add).then_inc(g_read, 1)
                dve.wait_ge(xT_done, NT + j + 1)
                dve.scalar_tensor_tensor(out=xn[0:rows(j), j, :], in0=b12_b[0:rows(j), :], scalar=deg[0:rows(j), 0, j:j + 1],
                                         in1=xn[0:rows(j), j, :], op0=ALU.mult, op1=ALU.add).then_inc(xb_ready[1], 1)

            for j in range(NT):
                hidden_in(j)
                if j >= 2:
                    hidden_out(j - 2)
            hidden_out(NT - 2)
            hidden_out(NT - 1)
            dve.wait_ge(deg_sq, 1)
            dve.reciprocal(deg[:, 1, :], degt[:, 1, :]).then_inc(deg_ready, 1)
            dve.wait_ge(t_evac, 3 * NT)
            irregular = dve.value_load(flag_i[0:1, 0:1], min_val=0, max_val=1)
            with dve.If(irregular > 0):
                in_degrees(counts_x, countsT_x)
            with dve.Else():
                in_degrees(counts, countsT)
            dve.wait_ge(deg_step, 4)
            dve.tensor_scalar(degt[:, 2, :], deg[:, 2, :], -1.0, 1.0, ALU.add, ALU.max).then_inc(deg_step, 1)
            dve.wait_ge(deg_sq, 2)
            dve.reciprocal(deg[:, 3, :], degt[:, 3, :]).then_inc(deg_ready, 1)
            layer_norm(1, lambda j: dve.wait_ge(xb_ready[1], j + 1), plus_x)

            with dve.Fori(0, NCH) as i:
                for cc in range(KC):
                    nodes = bass.ds(i * CS, CH)
                    dve.wait_ge(z2_hi_ready, i * KC + cc + 1)
                    dve.tensor_tensor(z2_lo[:, cc, nodes], ps[:, cc, 0:CH], z2_hi[:, cc, nodes].bitcast(F32),
                                      ALU.subtract).then_inc(agg_evac[2], 1)

            dve.wait_ge(deg_ready, 2)
            layer_norm(2, lambda j: dve.wait_ge(xb_ready[2], j + 1),
                       lambda j: lambda xr, y: dve.scalar_tensor_tensor(out=xr, in0=y, scalar=deg[0:rows(j), 3, j:j + 1], in1=xr,
                                                                        op0=ALU.mult, op1=ALU.add))

            dve.wait_ge(x3_copied, 1)
            irregular = dve.value_load(flag_i[0:1, 0:1], min_val=0, max_val=1)
            with dve.If(irregular > 0):
                with dve.Fori(0, NG) as g:
                    for rr in range(TPG):
                        n = g * TPG + rr
                        if rr == 0:
                            dve.wait_ge(fix_x, g * (16 * TPG) + 16)
                            dve.wait_ge(fix_e, g * (16 * TPG) + 16)
                        else:
                            dve.wait_ge(fix_x, g * (16 * TPG) + 16 * (rr + 1))
                            dve.wait_ge(fix_e, g * (16 * TPG) + 16 * (rr + 1))
                        dve.tensor_tensor(xg[:, 0, 0, :], xg[:, 0, 0, :], xg[:, 1, 0, :], ALU.add).then_inc(fix_msg, 1)
                        dve.wait_ge(fix_msg, n * 2 + 1)
                        dve.tensor_scalar(xg[:, 0, 0, :], xg[:, 0, 0, :], 0.0, None, ALU.max)
                        dve.tensor_scalar(fix_hot[:, :], iota_n[:, :],
                                          leftT[:, bass.ds(g, 1), rr:rr + 1].rearrange("p a b -> p (a b)"), None,
                                          ALU.is_equal).then_inc(fix_msg, 1)
                        for cc in range(KC):
                            dve.wait_ge(fix_done, n * KC + cc + 1)
                            for q, (n0, n1) in enumerate(CUTS):
                                ins = dve.tensor_tensor(x3T[:, cc, n0:n1], ps[:, q, 0:n1 - n0], x3T[:, cc, n0:n1], ALU.add)
                            ins.then_inc(fix_added, 1)
                            dve.wait_ge(fix_added, n * KC + cc + 2)

            def add_rows(it, s):
                g, slot = RING * it + s, s % XRING
                dve.wait_ge(xg_loaded[slot], it * (16 * TPG * RING // XRING) + 16 * TPG * (s // XRING + 1))
                dve.wait_ge(ea_loaded[s], it * 16 + 16 * (1 + (isinstance(it, int) and g == NG - 1 and LAST_R > 0)))
                dve.tensor_tensor(ea[:, s, :, :], ea[:, s, :, :], xg[:, slot, :, :], ALU.add).then_inc(add_done, 1)
                if not (isinstance(it, int) and it == 0):
                    dve.wait_ge(scat_done, g - RING + 1)
                dve.tensor_tensor(hot_w[:, s, :, :], iota_n[:, 0:W].unsqueeze(1).to_broadcast([P, TPG, W]),
                                  relwT[:, bass.ds(g, 1), :].rearrange("p a r -> p (a r)").unsqueeze(2).to_broadcast([P, TPG, W]),
                                  ALU.is_equal).then_inc(win_ready, 1)

            def add_join(m, slot, after=None):
                bases = [dve.value_load(base_i[0:1, bass.ds(JOIN * m + h, 1)], min_val=0, max_val=N - W) for h in range(JOIN)]
                if isinstance(m, int) and m == 0:
                    dve.wait_ge(pre_evac, KC)
                    dve.wait_ge(pre_set, KC)
                if slot == 1:
                    dve.wait_ge(blk_added, m // 2 + 1 if isinstance(m, int) else after)
                dve.wait_ge(join_done, m + 1)
                for h in range(JOIN):
                    dve.wait_ge(pre_added, JOIN * m + h + 1)
                    win = preT[:, :, bass.ds(bases[h], W)]
                    dve.tensor_tensor(win, win, join_bank(slot)[:, :, h, :], ALU.add).then_inc(pre_added, 1)

            def add_block(it):
                dve.wait_ge(blk_done, it)
                dve.wait_ge(pre_added, JOIN * (JOINS * it + 1) + 1)
                blk = preT[:, :, bass.ds((it - 1) * BL + LEAD, BL)]
                dve.tensor_tensor(blk, blk, ps[:, 2, 0:KC * BL].rearrange("p (f n) -> p f n", f=KC), ALU.add).then_inc(blk_added, 1)

            def stream(it):
                first = isinstance(it, int) and it <= 1
                for s in range(RING):
                    add_rows(it, s)
                    if s % JOIN == 0 and not (isinstance(it, int) and it == 0):
                        add_join(JOINS * it + s // JOIN - 2, s // JOIN, it)
                    if s == 1 and not first:
                        add_block(it - 1)

            dve.wait_ge(w32_split, 1)
            dve.tensor_tensor(w32_lo[:, :, :], w32_s[:, :, :], w32_hi[:, :, :].bitcast(F32), ALU.subtract).then_inc(w32_split, 1)
            for cc in range(KC):
                dve.tensor_copy(preT[:, cc, LEAD:N], cols[:, 1, cc:cc + 1].to_broadcast([P, N - LEAD])).then_inc(pre_set, 1)
            dve.sem_inc(pre_added, 1)
            dve.sem_inc(blk_added, 1)
            stream(0)
            stream(1)
            with dve.Fori(2, ITERS - 1) as it:
                stream(it)
            stream(ITERS - 1)
            add_join(NG // JOIN - 2, 0)
            add_block(ITERS - 1)
            add_join(NG // JOIN - 1, 1)

            def low_h(q):
                n0, n1 = CUTS[q]
                dve.wait_ge(h1_hi_ready, q + 1)
                dve.scalar_tensor_tensor(out=h1_lo[:, :, n0:n1], in0=preT[:, :, n0:n1], scalar=0.0, in1=h1_hi[:, :, n0:n1].bitcast(F32),
                                         op0=ALU.max, op1=ALU.subtract).then_inc(h1_ready, 1)

            dve.wait_ge(pre_added, NG + 1)
            low_h(0)
            low_h(1)

            def bn_finish(cc):
                dve.wait_ge(bn_sq, cc + 1)
                one = slice(cc, cc + 1)
                chain = [dve.reciprocal(bn_t[:, 1, one], bn_t[:, 0, one]).then_inc(bn_calc, 1)]
                dve.wait_ge(bn_calc, 3 * cc + 1)
                dve.tensor_tensor(bn_t[:, 2, one], bn_t[:, 1, one], cols[:, 3, one], ALU.mult).then_inc(bn_calc, 1)
                dve.wait_ge(bn_calc, 3 * cc + 2)
                dve.tensor_tensor(bn_t[:, 1, one], bn_mv[:, cc, 0:1], bn_t[:, 2, one], ALU.mult).then_inc(bn_calc, 1)
                dve.wait_ge(bn_calc, 3 * cc + 3)
                dve.tensor_tensor(bn_t[:, 3, one], cols[:, 4, one], bn_t[:, 1, one], ALU.subtract).then_inc(bn_ready, 1)
                if cc < KC - 1:
                    return
                dve.wait_ge(bn_ready, cc + 1)
                dve.tensor_scalar(hT[:, cc, HALF:N], hT[:, cc, HALF:N], bn_t[:, 2, one], bn_t[:, 3, one], ALU.mult, ALU.add).then_inc(hn_ready, 1)

            for n in range(KC * NCH):
                q, cc = divmod(n, KC)
                n0, n1 = CUTS[q]
                if n == KC:
                    low_h(2)
                dve.wait_ge(w32_done, n + 1)
                dve.scalar_tensor_tensor(out=hT[:, cc, n0:n1], in0=ps[:, n % 8, 0:n1 - n0], scalar=cols[:, 2, cc:cc + 1],
                                         in1=hT[:, cc, n0:n1], op0=ALU.add, op1=ALU.add).then_inc(h2_ready, 1)
                dve.wait_ge(h2_ready, n + 1)
                ins = dve.bn_stats(bn_st[:, cc, q, :], hT[:, cc, n0:n1])
                if q == NCH - 1:
                    ins.then_inc(bn_step, 1)
                    dve.wait_ge(bn_step, 2 * cc + 1)
                    dve.bn_aggr(bn_mv[:, cc, :], bn_st[:, cc, :, :].rearrange("p q s -> p (q s)")).then_inc(bn_step, 1)
                    if cc:
                        bn_finish(cc - 1)
            bn_finish(KC - 1)

            def ln_scale(j):
                n = 3 * NT + j
                dve.wait_ge(std_ready, n + 1)
                if j >= 2:
                    dve.wait_ge(x_ready, n - 1)
                dve.reciprocal(rstd[0:rows(j), j % 2:j % 2 + 1], std[0:rows(j), j % 2:j % 2 + 1]).then_inc(rstd_ready, 1)
                dve.wait_ge(rstd_ready, n + 1)
                dve.scalar_tensor_tensor(out=nmr[0:rows(j), j % 2:j % 2 + 1], in0=mv[0:rows(j), j % 2, 0:1], scalar=-1.0,
                                         in1=rstd[0:rows(j), j % 2:j % 2 + 1], op0=ALU.mult, op1=ALU.mult).then_inc(nmr_ready, 1)

            for j in range(NT):
                ln_begin(3 * NT + j, j, plus_x(j))
                if j:
                    ln_scale(j - 1)
            ln_scale(NT - 1)


        @block.tensor
        def _(pe):
            def transpose_x(n, j, src_t, ready):
                ready(j)
                if n >= 2:
                    pe.wait_ge(xT_evac, n - 1)
                for cc in range(KC):
                    ins = pe.transpose(ps[:, n % 2, P * cc:P * cc + rows(j)], src_t[0:rows(j), j, P * cc:P * cc + P],
                                       ident[0:rows(j), 0:rows(j)])
                ins.then_inc(xT_done, 1)

            pe.wait_ge(consts, 2)
            for j in range(NT):
                transpose_x(j, j, xn, lambda j: pe.wait_ge(x_loaded[j // 3], 16))

            pe.wait_ge(rows_ready, 1)
            for bank, names in ((4, ("code", "lo", "relw")), (3, ("dst",)), (5, ("left", "src"))):
                for k, name in enumerate(names):
                    for r in range(TPG):
                        pe.transpose(ps[:, bank, (k * TPG + r) * NG:(k * TPG + r + 1) * NG], row[name][:, r:GE:TPG], ident[0:NG, 0:NG])
            off = 2 * NG * TPG
            pe.transpose(ps[:, 5, off:off + NG], base_row[:, :], ident[0:NG, 0:NG])
            pe.transpose(ps[:, 5, off + NG:off + 2 * NG], left_row[:, :], ident[0:NG, 0:NG]).then_inc(idx_done, 1)

            def count_group(g):
                slot = g % HOTS
                pe.wait_ge(hot_ready, g + 1)
                pe.wait_ge(lo_ready, g + 1)
                pe.wait_ge(act_lo_ready, g + 1)
                if g >= HOTS:
                    pe.wait_ge(cnt_added, g - HOTS + 1)
                for r in range(TPG):
                    ins = pe.matmul(ps[:, 4 + slot, 0:NCODE], hot_lo[:, slot, r, :], hot_code[:, slot, r, :],
                                    start=(r == 0), stop=(r == TPG - 1))
                ins.then_inc(cnt_done, 1)

            count_group(0)
            count_group(1)
            pe.wait_ge(w01_loaded, 16)
            for j in range(NT):
                pe.wait_ge(xT_evac, j + 1)
                if j >= 2:
                    pe.wait_ge(u_evac, j - 1)
                for k in range(KC):
                    count_group(HOTS * j + k + 2)
                    ins = pe.matmul(ps[0:rows(j), 2 + j % 2, :], xT0[:, k, P * j:P * j + rows(j)], w01_s[:, k, :],
                                    start=(k == 0), stop=(k == KC - 1))
                ins.then_inc(u_done, 1)

            irregular = pe.value_load(flag_i[0:1, 0:1], min_val=0, max_val=1)
            with pe.If(irregular > 0):
                pe.sem_inc(fixc_added, 1)
                with pe.Fori(0, NG) as g:
                    for r in range(TPG):
                        for h in range(NT):
                            n = (g * TPG + r) * NT + h
                            pe.wait_ge(fixc_hot, n + 1)
                            pe.wait_ge(fixc_added, n + 1)
                            for q, (n0, n1) in enumerate(CUTS):
                                ins = pe.matmul(ps[0:rows(h), 4 + q, 0:n1 - n0], fixc_src[:, 0:rows(h)], fixc_dst[:, n0:n1],
                                                start=True, stop=True)
                            ins.then_inc(fixc_done, 1)

            def aggregate(layer, blocks, high, low, adj_r, adj, ready, adj_ready, adj_x_ready):
                def job(parts, rhs, cc, n):
                    pairs = [(part, j) for j in range(NT) for part in parts]
                    for m, (part, j) in enumerate(pairs):
                        if cc == 0 and part is parts[0]:
                            pe.wait_ge(ready, j + 1)
                        ins = pe.matmul(ps[:, cc, 0:CH], part[0:rows(j), j, P * cc:P * cc + P], rhs[0:rows(j), j, n],
                                        start=(m == 0), stop=(m == len(pairs) - 1))
                    ins.then_inc(agg_done[layer], 1)

                def chunks(parts, rhs):
                    with pe.Fori(0, NCH) as i:
                        for cc in range(blocks):
                            pe.wait_ge(agg_evac[layer], i * blocks + cc + 1)
                            job(parts, rhs, cc, bass.ds(i * CS, CH))

                irregular = pe.value_load(flag_i[0:1, 0:1], min_val=0, max_val=1)
                with pe.If(irregular > 0):
                    pe.wait_ge(*adj_x_ready)
                    chunks([high[:, :, :].bitcast(F32), low[:, :, :].bitcast(F32)], adj)
                with pe.Else():
                    pe.wait_ge(*adj_ready)
                    chunks([high, low], adj_r)

            def project(parts, kc, j, n):
                if n >= 2:
                    pe.wait_ge(y_read, n - 1)
                pairs = [(act_t, w, k) for act_t, w in parts for k in range(kc)]
                for m, (act_t, w, k) in enumerate(pairs):
                    ins = pe.matmul(ps[0:rows(j), 4 + n % 2, :], act_t[:, k, P * j:P * j + rows(j)], w[:, k, :],
                                    start=(m == 0), stop=(m == len(pairs) - 1))
                ins.then_inc(y_done, 1)

            aggregate(0, KC, u_hi, u_lo, counts, counts_x, u_ready, (cnt_added, NG), (diag_added, 2))
            pe.wait_ge(w02_split, 2)
            pe.wait_ge(agg_evac[0], KC * NCH + KC)

            for j in range(NT):
                project([(h1_hi0, w02_hi), (h1_hi0, w02_lo), (h1_lo0, w02_hi)], KC, j, j)

            def turn_counts(c):
                for t in range(3 * NT):
                    j, q = divmod(t, 3)
                    if t >= 4:
                        pe.wait_ge(t_evac, t - 3)
                    for i in range(4 * q, min(4 * q + 4, NT)):
                        ins = pe.transpose(ps[0:rows(j), t % 4, P * (i - 4 * q):P * (i - 4 * q) + rows(i)],
                                           f32(c[0:rows(i), i, P * j:P * j + rows(j)]), ident[0:rows(i), 0:rows(i)])
                    ins.then_inc(t_done, 1)

            irregular = pe.value_load(flag_i[0:1, 0:1], min_val=0, max_val=1)
            with pe.If(irregular > 0):
                turn_counts(counts_x)
            with pe.Else():
                turn_counts(counts)

            pe.wait_ge(t_evac, 3 * NT)
            pe.wait_ge(w11_split, 2)

            def hidden(j):
                pe.wait_ge(xT_evac, NT + j + 1)
                if j >= 2:
                    pe.wait_ge(g_read, j - 1)
                pairs = [(t, w, k) for t, w in ((x1_hi, w11_hi), (x1_hi, w11_lo), (x1_lo, w11_hi)) for k in range(KC)]
                for m, (t, w, k) in enumerate(pairs):
                    ins = pe.matmul(ps[0:rows(j), 2 + j % 2, 0:DH], t[:, j % XTILES, k, 0:rows(j)], w[:, k, :],
                                    start=(m == 0), stop=(m == len(pairs) - 1))
                ins.then_inc(g_done, 1)

            for j in range(NT):
                transpose_x(NT + j, j, xn, lambda j: pe.wait_ge(x_ready, j + 1))
                if j >= 2:
                    hidden(j - 2)
            hidden(NT - 2)
            hidden(NT - 1)
            aggregate(1, DH // P, g_hi, g_lo, countsT, countsT_x, g_ready, (t_evac, 3 * NT), (t_evac, 3 * NT))
            pe.wait_ge(agg_evac[1], (DH // P) * (NCH + 1))
            for j in range(NT):
                project([(z1T, w12_s)], DH // P, j, NT + j)

            aggregate(2, KC, xs_hi, xs_lo, counts, counts_x, xs_ready, (diag_taken, 2), (diag_taken, 2))
            pe.wait_ge(w2_split, 2)
            pe.wait_ge(agg_evac[2], KC * (NCH + 1))
            for j in range(NT):
                project([(z2_hi, w2_hi), (z2_hi, w2_lo), (z2_lo, w2_hi)], KC, j, 2 * NT + j)
                if j >= TLAG:
                    transpose_x(2 * NT + j - TLAG, j - TLAG, xn, lambda j: pe.wait_ge(x_ready, 2 * NT + j + 1))

            for j in range(NT - TLAG, NT):
                transpose_x(2 * NT + j, j, xn, lambda j: pe.wait_ge(x_ready, 2 * NT + j + 1))
            irregular = pe.value_load(flag_i[0:1, 0:1], min_val=0, max_val=1)
            with pe.If(irregular > 0):
                pe.wait_ge(xT_evac, 3 * NT)
                pe.sem_inc(fix_added, 1)
                with pe.Fori(0, NG) as g:
                    for r in range(TPG):
                        n = g * TPG + r
                        pe.wait_ge(fix_msg, n * 2 + 2)
                        for cc in range(KC):
                            pe.wait_ge(fix_added, n * KC + cc + 1)
                            for q, (n0, n1) in enumerate(CUTS):
                                ins = pe.matmul(ps[:, q, 0:n1 - n0], xg[:, 0, 0, P * cc:P * cc + P], fix_hot[:, n0:n1],
                                                start=True, stop=True)
                            ins.then_inc(fix_done, 1)
                pe.wait_ge(fix_added, NG * TPG * KC + 1)
            pe.wait_ge(xT_evac, 3 * NT)
            pe.wait_ge(w3_loaded, 32)

            for cc in range(KC):
                if cc >= 2:
                    pe.wait_ge(pre_evac, cc - 1)
                for k in range(KC):
                    ins = pe.matmul(ps[:, 2 + cc % 2, 0:LEAD], w31_s[:, k, P * cc:P * cc + P], x3T[:, k, 0:LEAD],
                                    start=(k == 0), stop=(k == KC - 1))
                ins.then_inc(pre_done, 1)

            def pre_block(it, blocks):
                if 0 in blocks:
                    pe.wait_ge(blk_added, it)
                for cc in blocks:
                    for k in range(KC):
                        ins = pe.matmul(ps[:, 2, cc * BL:cc * BL + BL], w31_s[:, k, P * cc:P * cc + P],
                                        x3T[:, k, bass.ds((it - 1) * BL + LEAD, BL)],
                                        start=(cc == 0 and k == 0), stop=(cc == KC - 1 and k == KC - 1))
                if KC - 1 in blocks:
                    ins.then_inc(blk_done, 1)

            def scatter(it, s):
                g = RING * it + s
                pe.wait_ge(relu_done, g + 1)
                pe.wait_ge(win_ready, g + 1)
                if not (isinstance(g, int) and g < 2):
                    pe.wait_ge(zn_ready, g - 1)
                for r in range(TPG):
                    ins = pe.matmul(ps[0:W, 4 + s % 2, :], hot_w[:, s, r, :], ea[:, s, r, :], start=(r == 0), stop=(r == TPG - 1))
                ins.then_inc(scat_done, 1)

            def turn(it, s):
                g = RING * it + s
                pe.wait_ge(zn_ready, g + 1)
                if not (isinstance(g, int) and g < 2):
                    pe.wait_ge(zg_ready, g - 1)
                pe.sem_inc(turn_seen, 1)
                for cc in range(KC):
                    ins = pe.transpose(ps[:, 6 + s % 2, cc * W:cc * W + W], zn[:, s % 2, P * cc:P * cc + P], ident[0:W, 0:W])
                ins.then_inc(turn_done, 1)

            def join(m, slot):
                pe.wait_ge(zg_ready, JOIN * m + JOIN)
                if not (isinstance(m, int) and m < JOINS):
                    pe.wait_ge(pre_added, JOIN * (m - JOINS) + JOIN + 1)
                for f in range(KC):
                    for k in range(KC):
                        ins = pe.matmul(join_bank(slot)[:, f, :, :].rearrange("p h w -> p (h w)"),
                                        w31_s[:, k, P * f:P * f + P], zg[:, slot, k, :, :].rearrange("p h w -> p (h w)"),
                                        start=(f == 0 and k == 0), stop=(f == KC - 1 and k == KC - 1))
                ins.then_inc(join_done, 1)

            for s in range(RING):
                scatter(0, s)
                if s:
                    turn(0, s - 1)
                if s == JOIN + 1:
                    join(0, 0)
            pe.wait_ge(pre_evac, KC)
            with pe.Fori(1, ITERS) as it:
                for s in range(RING):
                    scatter(it, s)
                    if s:
                        turn(it, s - 1)
                    else:
                        turn(it - 1, RING - 1)
                    if s % JOIN == 1:
                        join(JOINS * it + s // JOIN - 1, (s // JOIN - 1) % JOINS)
                    else:
                        pre_block(it, {2: (0,), 3: (1,), 5: (2, 3)}.get(s, ()))
            turn(ITERS - 1, RING - 1)
            join(NG // JOIN - 1, JOINS - 1)

            pe.wait_ge(w32_split, 2)
            for n in range(KC * NCH):
                q, cc = divmod(n, KC)
                n0, n1 = CUTS[q]
                if n >= 8:
                    pe.wait_ge(h2_ready, n - 7)
                pairs = [(w, h, k) for w, h in ((w32_hi, h1_hi), (w32_lo, h1_hi), (w32_hi, h1_lo)) for k in range(KC)]
                for m, (w, h, k) in enumerate(pairs):
                    if cc == 0 and k == 0 and w is w32_hi:
                        pe.wait_ge(h1_ready if h is h1_lo else h1_hi_ready, q + 1)
                    ins = pe.matmul(ps[:, n % 8, 0:n1 - n0], w[:, k, P * cc:P * cc + P], h[:, k, n0:n1],
                                    start=(m == 0), stop=(m == len(pairs) - 1))
                ins.then_inc(w32_done, 1)
            pe.wait_ge(hn_ready, KC + 1)
            for j in range(NT):
                n = 3 * NT + j
                pe.wait_ge(y_read, n - 1)
                for cc in range(KC):
                    ins = pe.transpose(ps[0:rows(j), 4 + n % 2, P * cc:P * cc + P], hT[:, cc, P * j:P * j + rows(j)], ident[:, :])
                ins.then_inc(y_done, 1)


_INS = ['x', 'src', 'dst', 'edge_attr_512', 'L0_gnn_W1', 'L0_gnn_b1', 'L0_gnn_W2', 'L0_gnn_b2', 'L1_gnn_W1', 'L1_gnn_b1',
        'L1_gnn_W2', 'L1_gnn_b2', 'L2_gnn_W', 'L2_gnn_b', 'L3_gnn_W1', 'L3_gnn_b1', 'L3_gnn_W2', 'L3_gnn_b2',
        'L3_gnn_gamma', 'L3_gnn_beta']
_OUTS = [((1250, 512), 'float32')]


def kernel(**inputs):
    import numpy as _np
    import concourse.bacc as _bacc
    from concourse import mybir as _mybir
    from concourse.bass_utils import run_bass_kernel_spmd as _run

    nc = _bacc.Bacc("TRN2", target_bir_lowering=False, num_devices=1)
    arrays, args = {}, []
    for name in _INS:
        a = _np.ascontiguousarray(inputs[name])
        arrays[f"in_{name}_dram"] = a
        args.append(nc.dram_tensor(f"in_{name}_dram", a.shape, _mybir.dt.from_np(a.dtype), kind="ExternalInput").ap())
    for i, (shape, dtype) in enumerate(_OUTS):
        dt = _mybir.dt.from_np(_np.dtype(dtype))
        args.append(nc.dram_tensor(f"out_{i}_dram", shape, dt, kind="ExternalOutput").ap())
    args.append(nc.dram_tensor("x3_dram", (1250, 512), _mybir.dt.float32, kind="Internal").ap())
    gnn_kernel(nc, *args)
    r = _run(nc, [arrays], core_ids=[0])
    got = tuple(r.results[0][f"out_{i}_dram"] for i in range(len(_OUTS)))
    return got[0]
```
